# Optimizing a Trainium2 kernel written in Bass

```python
import numpy as np
import jax
import jax.numpy as jnp

def _softmax(x, axis=-1):
    return jax.nn.softmax(x, axis=axis)

def _gelu(x):
    return jax.nn.gelu(x, approximate=True)

def _silu(x):
    return jax.nn.silu(x)

def _sigmoid(x):
    return jax.nn.sigmoid(x)

def _layernorm(x, axis=-1, eps=1e-05):
    m = jnp.mean(x, axis=axis, keepdims=True)
    v = jnp.var(x, axis=axis, keepdims=True)
    return (x - m) / jnp.sqrt(v + eps)

def _scatter_add(tgt, idx, src, axis=0):
    return tgt.at[idx].add(src)

def _segment_sum(src, seg, n):
    return jax.ops.segment_sum(src, seg, n)
kernel_name = 'mk_decoder_preln_d1_seqx_r8_1b7959'

def setup_inputs(seed: int=0):
    np.random.seed(seed)
    _w = jnp.asarray

    def _rec_inputs():
        import jax
        import jax.numpy as jnp
        _rk = jax.random.key(seed)
        x = -0.0003929 + 0.9999 * jax.random.normal(jax.random.fold_in(_rk, 1), (128, 64, 128), jnp.float32)
        _lenS = 64 - jax.random.randint(jax.random.fold_in(_rk, 7), (128,), 0, max(1, 64 // 4) + 1, jnp.int32)
        _lenS2 = 64 - jax.random.randint(jax.random.fold_in(_rk, 8), (128,), 0, max(1, 64 // 4) + 1, jnp.int32)
        _ctx_1024P = jax.random.normal(jax.random.fold_in(_rk, 11), (128, 16, 128), jnp.float32)
        _ctx_1024c = jax.random.dirichlet(jax.random.fold_in(_rk, 511), 0.3 * jnp.ones((16,), jnp.float32), (128, 64))
        _ctx_1024t = jnp.einsum('bsk,bkd->bsd', _ctx_1024c, _ctx_1024P)
        _ctx_1024t = _ctx_1024t * jax.lax.rsqrt(jnp.mean(jnp.square(_ctx_1024t)) + 1e-12) * 0.953939
        ctx_1024 = 2.81802e-05 + 1.00001 * (_ctx_1024t + 0.3 * jax.random.normal(jax.random.fold_in(_rk, 611), (128, 64, 128), jnp.float32))
        return (x, ctx_1024)
    x, ctx_1024 = _rec_inputs()

    def _L0_attn_setup():
        import jax, jax.numpy as jnp
        import numpy as np
        B, T, E, H = (2, 512, 128, 16)
        D = E // H
        EPS = 1e-06

        def _feature_map(x):
            return jnp.where(x > 0, x + 1.0, jnp.exp(x))
        key = jax.random.key(seed)
        ks = jax.random.split(key, 9)
        s = 1.0 / np.sqrt(E)
        return {'x': jax.random.normal(ks[0], (B, T, E), dtype=jnp.float32), 'wq': jax.random.uniform(ks[1], (E, E), jnp.float32, -s, s), 'bq': jax.random.uniform(ks[2], (E,), jnp.float32, -s, s), 'wk': jax.random.uniform(ks[3], (E, E), jnp.float32, -s, s), 'bk': jax.random.uniform(ks[4], (E,), jnp.float32, -s, s), 'wv': jax.random.uniform(ks[5], (E, E), jnp.float32, -s, s), 'bv': jax.random.uniform(ks[6], (E,), jnp.float32, -s, s), 'wo': jax.random.uniform(ks[7], (E, E), jnp.float32, -s, s), 'bo': jax.random.uniform(ks[8], (E,), jnp.float32, -s, s)}
    _L0_attn_all = _L0_attn_setup()
    _L0_attn_in = {k: v for k, v in _L0_attn_all.items() if k in ('wq', 'bq', 'wk', 'bk', 'wv', 'bv', 'wo', 'bo')}
    del _L0_attn_all

    def _L0_xattn_setup():
        import jax, jax.numpy as jnp
        import numpy as np
        import math
        B, L, D, H = (8, 256, 128, 16)
        E = D // H
        FACTOR = 1
        TOP_K = int(FACTOR * math.log(L))
        key = jax.random.key(seed)
        ks = jax.random.split(key, 11)
        s = 1.0 / math.sqrt(D)
        f32 = jnp.float32
        return {'queries': jax.random.normal(ks[0], (B, L, D), f32), 'keys': jax.random.normal(ks[1], (B, L, D), f32), 'values': jax.random.normal(ks[2], (B, L, D), f32), 'Wq': jax.random.normal(ks[3], (D, D), f32) * s, 'bq': jax.random.normal(ks[4], (D,), f32) * 0.01, 'Wk': jax.random.normal(ks[5], (D, D), f32) * s, 'bk': jax.random.normal(ks[6], (D,), f32) * 0.01, 'Wv': jax.random.normal(ks[7], (D, D), f32) * s, 'bv': jax.random.normal(ks[8], (D,), f32) * 0.01, 'Wo': jax.random.normal(ks[9], (D, D), f32) * s, 'bo': jax.random.normal(ks[10], (D,), f32) * 0.01}
    _L0_xattn_all = _L0_xattn_setup()
    _L0_xattn_in = {k: v for k, v in _L0_xattn_all.items() if k in ('Wq', 'bq', 'Wk', 'bk', 'Wv', 'bv', 'Wo', 'bo')}
    del _L0_xattn_all

    def _L0_ffn_setup():
        import jax, jax.numpy as jnp
        import numpy as np
        DIM = 128
        HIDDEN = 256
        N_EXPERTS = 8
        TOP_K = 2
        EPS = 1e-06

        def rms_norm(x, scale, eps=EPS):
            ms = jnp.mean(jnp.square(x.astype(jnp.float32)), axis=-1, keepdims=True)
            s = scale.astype(jnp.float32) * jax.lax.rsqrt(ms + eps)
            return x * s.astype(x.dtype)

        def moe_linear(xf, ids, W):
            E = W.shape[0]
            out = jnp.zeros((xf.shape[0], W.shape[1]), dtype=xf.dtype)
            for e in range(E):
                out = out + jnp.where((ids == e)[:, None], xf @ W[e].T, 0.0)
            return out
        key = jax.random.key(seed)
        k1, k2, k3, k4 = jax.random.split(key, 4)
        x = jax.random.normal(k1, (4, 512, DIM), dtype=jnp.float32)
        norm_scale = jnp.ones((DIM,), dtype=jnp.float32)
        w_router = jax.random.normal(k2, (N_EXPERTS, DIM), dtype=jnp.float32) / np.sqrt(DIM)
        lim_up = np.sqrt(6.0 / (DIM + 2 * HIDDEN))
        w_up = jax.random.uniform(k3, (N_EXPERTS, 2 * HIDDEN, DIM), dtype=jnp.float32, minval=-lim_up, maxval=lim_up)
        lim_dn = np.sqrt(6.0 / (HIDDEN + DIM))
        w_down = jax.random.uniform(k4, (N_EXPERTS, DIM, HIDDEN), dtype=jnp.float32, minval=-lim_dn, maxval=lim_dn)
        return {'x': x, 'norm_scale': norm_scale, 'w_router': w_router, 'w_up': w_up, 'w_down': w_down}
    _L0_ffn_all = _L0_ffn_setup()
    _L0_ffn_in = {k: v for k, v in _L0_ffn_all.items() if k in ('norm_scale', 'w_router', 'w_up', 'w_down')}
    del _L0_ffn_all
    return {'x': x, 'ctx_1024': ctx_1024, 'L0_attn_wq': _L0_attn_in['wq'], 'L0_attn_bq': _L0_attn_in['bq'], 'L0_attn_wk': _L0_attn_in['wk'], 'L0_attn_bk': _L0_attn_in['bk'], 'L0_attn_wv': _L0_attn_in['wv'], 'L0_attn_bv': _L0_attn_in['bv'], 'L0_attn_wo': _L0_attn_in['wo'], 'L0_attn_bo': _L0_attn_in['bo'], 'L0_xattn_Wq': _L0_xattn_in['Wq'], 'L0_xattn_bq': _L0_xattn_in['bq'], 'L0_xattn_Wk': _L0_xattn_in['Wk'], 'L0_xattn_bk': _L0_xattn_in['bk'], 'L0_xattn_Wv': _L0_xattn_in['Wv'], 'L0_xattn_bv': _L0_xattn_in['bv'], 'L0_xattn_Wo': _L0_xattn_in['Wo'], 'L0_xattn_bo': _L0_xattn_in['bo'], 'L0_ffn_norm_scale': _L0_ffn_in['norm_scale'], 'L0_ffn_w_router': _L0_ffn_in['w_router'], 'L0_ffn_w_up': _L0_ffn_in['w_up'], 'L0_ffn_w_down': _L0_ffn_in['w_down']}

def reference(x, ctx_1024, L0_attn_wq, L0_attn_bq, L0_attn_wk, L0_attn_bk, L0_attn_wv, L0_attn_bv, L0_attn_wo, L0_attn_bo, L0_xattn_Wq, L0_xattn_bq, L0_xattn_Wk, L0_xattn_bk, L0_xattn_Wv, L0_xattn_bv, L0_xattn_Wo, L0_xattn_bo, L0_ffn_norm_scale, L0_ffn_w_router, L0_ffn_w_up, L0_ffn_w_down):
    import jax
    import jax.numpy as jnp

    def _L0_attn_ref(x, wq, bq, wk, bk, wv, bv, wo, bo):
        import jax, jax.numpy as jnp
        import numpy as np
        B, T, E, H = (2, 512, 128, 16)
        D = E // H
        EPS = 1e-06

        def _feature_map(x):
            return jnp.where(x > 0, x + 1.0, jnp.exp(x))
        b, t, e = x.shape
        q = _feature_map(x @ wq + bq).reshape(b, t, H, D)
        k = _feature_map(x @ wk + bk).reshape(b, t, H, D)
        v = (x @ wv + bv).reshape(b, t, H, D)
        qT = jnp.moveaxis(q, 1, 0)
        kT = jnp.moveaxis(k, 1, 0)
        vT = jnp.moveaxis(v, 1, 0)
        S0 = jnp.zeros((b, H, D, D), dtype=x.dtype)
        z0 = jnp.zeros((b, H, D), dtype=x.dtype)

        def step(carry, qkv):
            S, z = carry
            qt, kt, vt = qkv
            S = S + jnp.einsum('bhd,bhe->bhde', kt, vt)
            z = z + kt
            num = jnp.einsum('bhd,bhde->bhe', qt, S)
            den = jnp.einsum('bhd,bhd->bh', qt, z)[..., None] + EPS
            return ((S, z), num / den)
        _, outT = jax.lax.scan(step, (S0, z0), (qT, kT, vT))
        out = jnp.moveaxis(outT, 0, 1).reshape(b, t, e)
        return out @ wo + bo

    def _L0_xattn_ref(queries, keys, values, Wq, bq, Wk, bk, Wv, bv, Wo, bo):
        import jax, jax.numpy as jnp
        import numpy as np
        import math
        B, L, D, H = (8, 256, 128, 16)
        E = D // H
        FACTOR = 1
        TOP_K = int(FACTOR * math.log(L))
        Bq, Lq, Dq = queries.shape
        q = (queries @ Wq + bq).reshape(Bq, Lq, H, E).transpose(0, 2, 3, 1)
        k = (keys @ Wk + bk).reshape(Bq, Lq, H, E).transpose(0, 2, 3, 1)
        v = (values @ Wv + bv).reshape(Bq, Lq, H, E).transpose(0, 2, 3, 1)
        q_fft = jnp.fft.rfft(q, axis=-1)
        k_fft = jnp.fft.rfft(k, axis=-1)
        corr = jnp.fft.irfft(q_fft * jnp.conj(k_fft), n=Lq, axis=-1)
        mean_value = corr.mean(axis=(1, 2))
        _, index = jax.lax.top_k(mean_value.mean(axis=0), TOP_K)
        weights = mean_value[:, index]
        tmp_corr = jax.nn.softmax(weights, axis=-1)
        idx = (jnp.arange(Lq)[None, :] + index[:, None]) % Lq
        gathered = v[..., idx]
        agg = jnp.einsum('bhekl,bk->bhel', gathered, tmp_corr)
        out = agg.transpose(0, 3, 1, 2).reshape(Bq, Lq, Dq)
        return out @ Wo + bo

    def _L0_ffn_ref(x, norm_scale, w_router, w_up, w_down):
        import jax, jax.numpy as jnp
        import numpy as np
        DIM = 128
        HIDDEN = 256
        N_EXPERTS = 8
        TOP_K = 2
        EPS = 1e-06

        def rms_norm(x, scale, eps=EPS):
            ms = jnp.mean(jnp.square(x.astype(jnp.float32)), axis=-1, keepdims=True)
            s = scale.astype(jnp.float32) * jax.lax.rsqrt(ms + eps)
            return x * s.astype(x.dtype)

        def moe_linear(xf, ids, W):
            E = W.shape[0]
            out = jnp.zeros((xf.shape[0], W.shape[1]), dtype=xf.dtype)
            for e in range(E):
                out = out + jnp.where((ids == e)[:, None], xf @ W[e].T, 0.0)
            return out
        B, S, D = x.shape
        skip = x
        xn = rms_norm(x, norm_scale)
        scores = (xn @ w_router.T).astype(jnp.float32)
        scores_topk, idx = jax.lax.top_k(scores, TOP_K)
        weights = jax.nn.softmax(scores_topk, axis=-1)
        xf = jnp.broadcast_to(xn[..., None, :], (B, S, TOP_K, D)).reshape(-1, D)
        ids = idx.reshape(-1)
        up = moe_linear(xf, ids, w_up)
        u, gate = jnp.split(up, 2, axis=-1)
        h = u * jax.nn.silu(gate)
        down = moe_linear(h, ids, w_down)
        down = down.reshape(B, S, TOP_K, D)
        out = jnp.sum(down * weights[..., None].astype(down.dtype), axis=-2)
        return out + skip
    x = x + _L0_attn_ref(_layernorm(x, axis=-1), L0_attn_wq, L0_attn_bq, L0_attn_wk, L0_attn_bk, L0_attn_wv, L0_attn_bv, L0_attn_wo, L0_attn_bo)
    x = x + _L0_xattn_ref(_layernorm(x, axis=-1), ctx_1024, ctx_1024, L0_xattn_Wq, L0_xattn_bq, L0_xattn_Wk, L0_xattn_bk, L0_xattn_Wv, L0_xattn_bv, L0_xattn_Wo, L0_xattn_bo)
    x = x + _L0_ffn_ref(_layernorm(x, axis=-1), L0_ffn_norm_scale, L0_ffn_w_router, L0_ffn_w_up, L0_ffn_w_down)
    return x

_drawn_inputs = setup_inputs


def setup_inputs(seed=0):
    import zlib

    import numpy as np

    out = dict(_drawn_inputs(seed))
    spreads = {'L0_ffn_norm_scale': (1.0, 0.2)}
    factors = {'L0_attn_wq': 8.0,
     'L0_attn_bq': 64.0,
     'L0_attn_wk': 4.26,
     'L0_attn_bk': 64.0,
     'L0_xattn_bq': 64.0,
     'L0_xattn_bk': 64.0,
     'L0_xattn_bv': 5.283,
     'L0_xattn_bo': 5.008}
    for name, (base, spread) in spreads.items():
        noise = np.random.default_rng([zlib.crc32(name.encode()), seed]).standard_normal(out[name].shape)
        drawn = base * np.exp(spread * noise) if base else spread * noise
        out[name] = jnp.asarray(drawn.astype(out[name].dtype))
    for name, factor in factors.items():
        out[name] = (out[name] * factor).astype(out[name].dtype)
    return out
```

```python
from contextlib import ExitStack

import concourse.bass as bass
from concourse import mybir

F32, BF16 = mybir.dt.float32, mybir.dt.bfloat16
I32, U32 = mybir.dt.int32, mybir.dt.uint32
ALU = mybir.AluOpType
ACT = mybir.ActivationFunctionType
AX = mybir.AxisListType

P = 128
B, L, E, H = 128, 64, 128, 16
D = E // H
D1 = D + 1
T = B * L
NT = T // P
GT = 4
NG = NT // GT
GW = GT * P
NE, HID, TOPK = 8, 256, 2
LAGS = 5
XT = T * TOPK // P + NE
SPARE = T * TOPK
LN_EPS, ATT_EPS, RMS_EPS = 1e-5, 1e-6, 1e-6
HEADS = [(0, 6), (6, 11), (11, 16)]


def need(eng, sem, count):
    if not (isinstance(count, int) and count <= 0):
        eng.wait_ge(sem, count)


def bcast_rows(ap, rows, width):
    return bass.AP(ap.tensor, 0, [[0, rows], [1, width]])


def build(nc, x, ctx_t, ctx_r, wqkv_p, b_all, wo, wq2, wk2, wv2, wo2, bq2, bk2, scale, w_router, w_up, w_down,
          tri, stri, ident, iota, out):
    with ExitStack() as ctx:
        def sb(name, shape, dt=F32):
            return ctx.enter_context(nc.sbuf_tensor(name, shape, dt))

        def sem(name):
            return ctx.enter_context(nc.semaphore(name))

        def sems(name, n):
            return [sem(f"{name}{i}") for i in range(n)]

        gram_d = nc.dram_tensor("gram_d", (B * L * 2 * L,), F32).ap()
        prob_d = nc.dram_tensor("prob_d", (B * 2 * L,), F32).ap()
        xr_d = nc.dram_tensor("xr_d", (T, E), F32).ap()
        y_d = nc.dram_tensor("y_d", (SPARE + XT * P, E), F32).ap()

        wqkv = sb("wqkv", [P, 3 * E])
        wo_s, wq2_s, wk2_s, wv2_s, wo2_s = (sb(n, [P, E]) for n in ("wo_s", "wq2_s", "wk2_s", "wv2_s", "wo2_s"))
        bq2_s, bk2_s, scale_s = sb("bq2_s", [P, 1]), sb("bk2_s", [P, 1]), sb("scale_s", [P, 1])
        wr_s = sb("wr_s", [P, NE])
        wu_s = sb("wu_s", [P, NE * 2 * HID])
        wd_s = sb("wd_s", [P, NE * 2 * E])
        tri_s, stri_s, id_s = sb("tri_s", [P, P]), sb("stri_s", [P, P]), sb("id_s", [P, P])
        iota_s = sb("iota_s", [P, 160])
        ones_f = sb("ones_f", [P, P])
        ones3 = sb("ones3", [3, P], BF16)
        NBIAS = 6 * E
        bias_p = [sb(f"bias_p{i}", [3, NBIAS], BF16) for i in range(3)]
        bias3 = sb("bias3", [3, NBIAS], BF16)
        power = sb("power", [P, GT])

        X = sb("X", [P, NT, E])

        st_a, mv_a = sb("st_a", [P, GT, 6]), [sb(f"mv_a{i}", [P, GT, 2]) for i in range(2)]
        ve_a, rs_a = sb("ve_a", [P, GT]), [sb(f"rs_a{i}", [P, GT]) for i in range(2)]
        xh = sb("xh", [P, GT, E])
        xT = sb("xT", [P, GW])
        ex, rl = [sb(f"ex{i}", [P, 2 * E]) for i in range(2)], [sb(f"rl{i}", [P, 2 * E]) for i in range(2)]
        v9 = [sb(f"v9_{i}", [P, H, D1]) for i in range(2)]
        qk = [sb(f"qk{i}", [P, GT, 2 * E]) for i in range(2)]
        shared = sb("shared", [P, GT * H * D1 * D])
        bias_f, bias_r, bias_a, bias_b = (shared[0:3, i * NBIAS:(i + 1) * NBIAS] for i in range(4))
        outer = [shared[:, i * H * D1 * D:(i + 1) * H * D1 * D].rearrange("p (h e d) -> p h e d", h=H, e=D1)
                 for i in range(GT)]
        diag = shared[:, 0:L * L].rearrange("p (t l) -> p t l", t=L)
        y_in = [shared[:, i * TOPK * GW:(i + 1) * TOPK * GW].rearrange("p (c t e) -> p c t e", c=TOPK, t=GT)
                for i in range(2)]
        R = sb("R", [P, H, D1, D])
        nd = [sb(f"nd{i}", [P, GT, H, D1]) for i in range(2)]
        den, rden = sb("den", [P, GT * H]), sb("rden", [P, GT * H])
        on = sb("on", [P, GT, E])
        oT = sb("oT", [P, GW])
        st_c, mv_c = sb("st_c", [P, GT, 6]), [sb(f"mv_c{i}", [P, GT, 2]) for i in range(2)]
        ve_c, rs_c = sb("ve_c", [P, GT]), [sb(f"rs_c{i}", [P, GT]) for i in range(2)]
        xh2 = sb("xh2", [P, GT, E])
        x2T, q2T, k2T = sb("x2T", [P, GW]), sb("q2T", [P, GW]), sb("k2T", [P, GW])
        ct = [sb(f"ct{i}", [P, GW]) for i in range(2)]
        gd = [sb(f"gd{i}", [P, GT, 2, L]) for i in range(2)]

        mean, mean_all = sb("mean", [P, L]), sb("mean_all", [P, L])
        top8, top_at, top_f = sb("top8", [P, 8]), sb("top_at", [P, 8], U32), sb("top_f", [P, 8])
        kept = [sb(f"kept{i}", [P, L]) for i in range(2)]
        away, masked, scores = sb("away", [P, L]), sb("masked", [P, L]), sb("scores", [P, L])
        neg_max, prob, prob_sum, prob_r = sb("neg_max", [P, 1]), sb("prob", [P, L]), sb("prob_sum", [P, 1]), sb("prob_r", [P, 1])
        prob2 = sb("prob2", [P, 2, L])
        circ = [sb(f"circ{i}", [P, GT, P]) for i in range(2)]
        v2, aT = sb("v2", [P, GT, E]), sb("aT", [P, GW])
        st_e, mv_e = sb("st_e", [P, GT, 6]), [sb(f"mv_e{i}", [P, GT, 2]) for i in range(2)]
        ve_e, rs_e = sb("ve_e", [P, GT]), [sb(f"rs_e{i}", [P, GT]) for i in range(2)]
        vl_e, rl_e, vr_e = sb("vl_e", [P, GT]), sb("rl_e", [P, GT]), sb("vr_e", [P, GT])
        ms_e = [sb(f"ms_e{i}", [P, GT]) for i in range(2)]
        xr = [sb(f"xr{i}", [P, GT, E]) for i in range(2)]
        xrT = sb("xrT", [P, GW])
        best, best_at = sb("best", [P, GT, 8]), sb("best_at", [P, GT, 8], U32)

        top_s, top_e = sb("top_s", [P, NT, TOPK]), sb("top_e", [P, NT, TOPK])
        gate = sb("gate", [P, TOPK, NT])
        gap, gap_e, gap_s = sb("gap", [P, NT]), sb("gap_e", [P, NT]), sb("gap_s", [P, NT])
        hot = [sb(f"hot{i}", [P, NT, NE]) for i in range(TOPK)]
        picked = sb("picked", [P, NT, NE])
        tot, upto, pos, pos_b, pos_c = (sb(n, [P, NT, NE]) for n in ("tot", "upto", "pos", "pos_b", "pos_c"))
        cnt_f, cnt_c, end_t, base_t, base = (sb(n, [P, NE]) for n in ("cnt_f", "cnt_c", "end_t", "base_t", "base"))
        cnt_i, cnt_s = sb("cnt_i", [P, NE], I32), sb("cnt_s", [P, NE], I32)
        mine = [sb(f"mine{i}", [P, NT, NE]) for i in range(TOPK)]
        slot_f = sb("slot_f", [P, TOPK, NT])
        slot_i, hi_i, lo_i = (sb(n, [P, TOPK, NT], I32) for n in ("slot_i", "hi_i", "lo_i"))
        hi_f, lo_f = sb("hi_f", [P, TOPK, NT]), sb("lo_f", [P, TOPK, NT])
        iota_b, zero_b = sb("iota_b", [P, 160], BF16), sb("zero_b", [P, 2 * XT], BF16)
        row1 = sb("row1", [P, 1])
        hot_lo = [sb(f"hot_lo{i}", [P, P], BF16) for i in range(4)]
        hot_hi = [sb(f"hot_hi{i}", [P, 2, XT], BF16) for i in range(4)]
        of_tile = [sb(f"of_tile{i}", [P, XT]) for i in range(2)]
        off_f = sb("off_f", [P, 2, XT])
        off_i = sb("off_i", [P, 2, XT], I32)
        inv_row, inv_pad, inv, spare_a, spare_b, dest_f = (
            sb(n, [P, XT]) for n in ("inv_row", "inv_pad", "inv", "spare_a", "spare_b", "dest_f"))
        dest_i, src_i = sb("dest_i", [P, XT], I32), sb("src_i", [P, XT], I32)

        src_x, dest_x = [sb(f"src_x{i}", [P, 1], U32) for i in range(2)], [sb(f"dest_x{i}", [P, 1], U32) for i in range(2)]
        xg, xgT = [sb(f"xg{i}", [P, E]) for i in range(2)], [sb(f"xgT{i}", [P, P]) for i in range(2)]
        silu, hid = [sb(f"silu{i}", [P, HID]) for i in range(2)], [sb(f"hid{i}", [P, HID]) for i in range(2)]
        hidT, yg = [sb(f"hidT{i}", [P, HID]) for i in range(2)], [sb(f"yg{i}", [P, E]) for i in range(2)]
        part, fin = sb("part", [P, GT, E]), [sb(f"fin{i}", [P, GT, E]) for i in range(2)]

        bank = [ctx.enter_context(nc.psum_tensor(f"bank{i}", [P, 512], F32)) for i in range(8)]

        settled = sem("settled")
        const_in = sem("const_in")
        w_in = sem("w_in")
        bias_ch = sem("bias_ch")
        setup = sem("setup")
        x_in = sems("x_in", 2)
        ct_in = sems("ct_in", 2)
        a_st, a_mv, a_ve, a_rs, a_xh = sem("a_st"), sem("a_mv"), sem("a_ve"), sem("a_rs"), sem("a_xh")
        a_tr, a_xT, a_proj, a_pev, a_f, a_outer = (sem(n) for n in ("a_tr", "a_xT", "a_proj", "a_pev", "a_f", "a_outer"))
        b_run, b_mul, b_red = sem("b_run"), sem("b_mul"), sem("b_red")
        c_den, c_on, c_tr, c_oT, c_y, c_x1, c_st, c_mv, c_ve, c_rs = (
            sem(n) for n in ("c_den", "c_on", "c_tr", "c_oT", "c_y", "c_x1", "c_st", "c_mv", "c_ve", "c_rs"))
        d_xh, d_tr, d_xT, d_k, d_kT, d_q, d_qT, d_gram, d_gd = (
            sem(n) for n in ("d_xh", "d_tr", "d_xT", "d_k", "d_kT", "d_q", "d_qT", "d_gram", "d_gd"))
        gram_out = sems("gram_out", 2)
        diag_in, mean_ch, mean_mm, prob_e = sem("diag_in"), sem("mean_ch"), sem("mean_mm"), sem("prob_e")
        prob_out, circ_0, circ_in = sem("prob_out"), sem("circ_0"), sems("circ_in", 2)
        e_v, e_v2, e_agg, e_aT, e_y, e_x2, e_st, e_mv, e_ve, e_rs = (
            sem(n) for n in ("e_v", "e_v2", "e_agg", "e_aT", "e_y", "e_x2", "e_st", "e_mv", "e_ve", "e_rs"))
        e_rl, e_ms = sem("e_rl"), sem("e_ms")
        f_x3 = sem("f_x3")
        f_xr, f_tr, f_xT, f_sc, f_max, f_at, f_top = (
            sem(n) for n in ("f_xr", "f_tr", "f_xT", "f_sc", "f_max", "f_at", "f_top"))
        xr_out = sems("xr_out", 2)
        r_ch, r_gap, r_exp, r_pick, r_cnt, r_hot, r_inv, r_done = (
            sem(n) for n in ("r_ch", "r_gap", "r_exp", "r_pick", "r_cnt", "r_hot", "r_inv", "r_done"))
        x_src, x_tr, x_xT, x_up, x_silu, x_h, x_ht, x_hT, x_dn, x_y = (
            sem(n) for n in ("x_src", "x_tr", "x_xT", "x_up", "x_silu", "x_h", "x_ht", "x_hT", "x_dn", "x_y"))
        xg_in, yg_out = sems("xg_in", 2), sems("yg_out", 2)
        y_ld, o_part, o_fin, o_out = sems("y_ld", 2), sem("o_part"), sem("o_fin"), sems("o_out", 2)

        b_qkv = bias3[:, 0:3 * E]
        b_o = bias3[:, 3 * E:4 * E].unsqueeze(1).broadcast_to([3, GT, E])
        b_v2 = bias3[:, 4 * E:5 * E].unsqueeze(1).broadcast_to([3, GT, E])
        b_o2 = bias3[:, 5 * E:6 * E].unsqueeze(1).broadcast_to([3, GT, E])

        def settle(eng):
            eng.sem_inc(settled, 1)

        def grp(n, i=None):
            if i is None:
                return n, n % 2, n // 2
            return 2 * i + n, n % 2, i + n // 2

        FIRST, LAST = -2, NG + 1

        def slots(eng, slot):
            for n in range(FIRST, 4):
                slot(n, None)
            with eng.Fori(2, (NG - 2) // 2) as i:
                slot(0, i)
                slot(1, i)
            for n in range(NG - 2, LAST + 1):
                slot(n, None)

        def stage(n, i, shift):
            if i is None and not 0 <= n + shift < NG:
                return None
            return grp(n + shift, i)

        def pairs(eng, count, body):
            body(0)
            with eng.Fori(1, count) as i:
                body(i)

        def cross_slots(eng, slot):
            for n in range(-1, 4):
                slot(n, None)
            with eng.Fori(2, NG // 2 - 1) as i:
                slot(0, i)
                slot(1, i)
            for n in range(NG - 2, NG + 2):
                slot(n, None)

        def expert_stage(n, i, shift):
            if i is None and not 0 <= n + shift < XT:
                return None
            return grp(n + shift, i)

        def expert_slots(eng, slot):
            for n in range(-4, 4):
                slot(n, None)
            with eng.Fori(2, XT // 2 - 2) as i:
                slot(0, i)
                slot(1, i)
            for n in range(XT - 4, XT + 1):
                slot(n, None)

        xr_rows = xr_d.rearrange("(t p) e -> p t e", p=P)
        y_rows = y_d.rearrange("(t p) e -> p t e", p=P)
        dyn = bass.ds

        block = ctx.enter_context(nc.Block())

        @block.sync
        def _(sp):
            n_w = 0
            sp.dma_start(id_s[:], ident).then_inc(const_in, 16)
            for dst, src in ((wqkv[:], wqkv_p), (wo_s[:], wo), (wq2_s[:], wq2), (wk2_s[:], wk2), (wv2_s[:], wv2),
                             (wo2_s[:], wo2), (bq2_s[:], bq2), (bk2_s[:], bk2), (scale_s[:], scale),
                             (wr_s[:], w_router), (tri_s[:], tri), (stri_s[:], stri),
                             (iota_s[:], iota), (bias_f, bcast_rows(b_all, 3, NBIAS))):
                sp.dma_start(dst, src).then_inc(w_in, 16)
                n_w += 16
            assert n_w == N_W

            def x_load(i):
                for k in range(2):
                    need(sp, x_in[k], i * 16)
                    sp.dma_start(X[:, bass.ds((2 * i + k) * GT, GT), :],
                                 x[:, bass.ds((2 * i + k) * GT, GT), :]).then_inc(x_in[k], 16)

            pairs(sp, NG // 2, x_load)
            for k in range(2):
                sp.dma_start(ct[k][:], ctx_t[:, k * GW:(k + 1) * GW]).then_inc(ct_in[k], 16)

            def gram_store(g, p, r):
                sp.wait_ge(d_gd, g + 1)
                settle(sp)
                need(sp, gram_out[p], 16 * r)
                sp.dma_start(bass.AP(gram_d.tensor, g * (GT * P * 2 * L), [[2 * L, P], [P * 2 * L, GT], [1, 2 * L]]),
                             gd[p][:].rearrange("p t a b -> p t (a b)")).then_inc(gram_out[p], 16)

            def gram_and_context(i):
                for k in range(2):
                    g, p, r = grp(k, i)
                    gram_store(g, p, r)
                    sp.wait_ge(d_k, g + 1)
                    sp.dma_start(ct[p][:], ctx_t[:, bass.ds((g + 2) * GW, GW)]).then_inc(ct_in[p], 16)

            pairs(sp, NG // 2 - 1, gram_and_context)
            for g in (NG - 2, NG - 1):
                gram_store(*grp(g))
            for k in range(2):
                sp.wait_ge(gram_out[k], 16 * NG // 2)
            sp.wait_ge(b_run, 3 * NT)
            sp.dma_start(diag, bass.AP(gram_d.tensor, 0, [[L * 2 * L, P], [2 * L + 1, L], [1, L]])).then_inc(diag_in, 16)

            def ctx_load(g, p, r):
                sp.dma_start(ct[p][:], ctx_r[:, dyn(g * GW, GW)]).then_inc(ct_in[p], 16)

            def circ_load(g, p, r):
                for h in range(2):
                    src = bass.AP(prob_d.tensor, g * (GT * 2 * 2 * L) + (h * 2 * L + 1), [[1, L], [2 * 2 * L, GT], [1, L]])
                    sp.dma_start(circ[p][h * L:(h + 1) * L, :, h * L:(h + 1) * L], src).then_inc(circ_in[p], 16)

            sp.wait_ge(d_k, NG)
            for g in range(2):
                ctx_load(*grp(g))
            sp.wait_ge(w_in, N_W)
            for dst, src in ((wu_s[:], w_up), (wd_s[:], w_down)):
                sp.dma_start(dst, src).then_inc(w_in, 16)
            sp.wait_ge(mean_ch, MEAN_STEPS)
            sp.dma_start(bass.AP(prob_d.tensor, 0, [[2 * L, P], [1, 2 * L]]), prob2[:].rearrange("p a l -> p (a l)")
                         ).then_inc(prob_out, 16)
            sp.wait_ge(prob_out, 16)
            sp.wait_ge(circ_0, 3)
            for g in range(2):
                circ_load(*grp(g))

            def next_loads(i):
                for k in range(2):
                    g, p, r = grp(k, i)
                    sp.wait_ge(e_v, g + 1)
                    ctx_load(*grp(k + 2, i))
                    sp.wait_ge(e_agg, g + 1)
                    circ_load(*grp(k + 2, i))

            pairs(sp, NG // 2 - 1, next_loads)
            for k in range(2):
                sp.wait_ge(yg_out[k], 16 * XT // 2)

            def y_load(i):
                for k in range(2):
                    g, p, r = grp(k, i)
                    need(sp, o_fin, g - 1)
                    for c in range(TOPK):
                        sp.dma_start(y_in[p][:, c], y_rows[:, dyn(GT * g + c * NT, GT), :]).then_inc(y_ld[p], 16)

            pairs(sp, NG // 2, y_load)

        @block.gpsimd
        def _(pool):
            pool.memset(ones3[:], 1.0).then_inc(setup, 1)
            pool.memset(power[:], -0.5).then_inc(setup, 1)
            for k in range(2):
                pool.memset(v9[k][:], 1.0).then_inc(setup, 1)
            pool.memset(ones_f[:], 1.0).then_inc(setup, 1)
            pool.memset(zero_b[:], 0.0).then_inc(circ_0, 1)
            pool.wait_ge(setup, 5)

            def rstd(g, p, stats, seen, ve, ve_sem, rs, rs_sem, normed):
                need(pool, rs_sem, g)
                pool.wait_ge(seen, GT * g + GT)
                settle(pool)
                nc.gpsimd.tensor_scalar(ve[:], stats[p][:, :, 1], 1.0, LN_EPS, ALU.mult, ALU.add).then_inc(ve_sem, 1)
                pool.wait_ge(ve_sem, g + 1)
                need(pool, normed, GT * (g - 1))
                nc.gpsimd.tensor_tensor(rs[p][:], ve[:], power[:], ALU.pow).then_inc(rs_sem, 1)

            def outer_product(g, p, r, k):
                t = GT * g + k
                pool.wait_ge(a_f, t + 1)
                pool.wait_ge(a_pev, 3 * t + 3)
                need(pool, b_run, 3 * (t - GT) + 3)
                kk = qk[p][:, k, E:2 * E].rearrange("p (h d) -> p h d", h=H)
                nc.gpsimd.tensor_tensor(
                    outer[k], v9[k % 2][:].unsqueeze(3).broadcast_to([P, H, D1, D]),
                    kk.unsqueeze(2).broadcast_to([P, H, D1, D]), ALU.mult).then_inc(a_outer, 1)

            def slot(n, i):
                a0, a1, c = stage(n, i, 2), stage(n, i, 1), stage(n, i, -1)
                if a0:
                    rstd(a0[0], a0[1], mv_a, a_mv, ve_a, a_ve, rs_a, a_rs, a_xh)
                if a1:
                    outer_product(*a1, 0)
                    outer_product(*a1, 1)
                if c:
                    rstd(c[0], c[1], mv_c, c_mv, ve_c, c_ve, rs_c, c_rs, d_xh)
                if a1:
                    outer_product(*a1, 2)
                    outer_product(*a1, 3)

            slots(pool, slot)

            for k in range(2):
                nc.gpsimd.memset(circ[k][:], 0.0).then_inc(circ_0, 1)

            def cross_slot(n, i):
                e = stage(n, i, 0)
                if e:
                    g, p, r = e
                    pool.wait_ge(e_mv, GT * g + GT)
                    need(pool, e_ms, g)
                    settle(pool)
                    nc.gpsimd.tensor_scalar(ve_e[:], mv_e[p][:, :, 1], 1.0 + RMS_EPS, LN_EPS * RMS_EPS, ALU.mult, ALU.add
                                            ).then_inc(e_ve, 1)
                    nc.gpsimd.tensor_scalar(vl_e[:], mv_e[p][:, :, 1], 1.0, LN_EPS, ALU.mult, ALU.add).then_inc(e_ve, 1)
                    pool.wait_ge(e_ve, 2 * g + 2)
                    need(pool, f_xr, GT * (g - 1))
                    nc.gpsimd.tensor_tensor(rs_e[p][:], ve_e[:], power[:], ALU.pow).then_inc(e_rs, 1)
                    nc.gpsimd.tensor_tensor(rl_e[:], vl_e[:], power[:], ALU.pow).then_inc(e_rl, 1)
                    pool.wait_ge(e_rs, g + 1)
                    nc.gpsimd.tensor_tensor(vr_e[:], ve_e[:], rs_e[p][:], ALU.mult).then_inc(e_rl, 1)
                    pool.wait_ge(e_rl, 2 * g + 2)
                    need(pool, f_x3, GT * (g - 1))
                    nc.gpsimd.tensor_tensor(ms_e[p][:], vr_e[:], rl_e[:], ALU.mult).then_inc(e_ms, 1)

            cross_slots(pool, cross_slot)

            for k in range(2):
                pool.wait_ge(xr_out[k], 16 * NG // 2)

            def expert_slot(n, i):
                gather, scatter = expert_stage(n, i, 4), expert_stage(n, i, -1)
                if gather:
                    t, p, r = gather
                    pool.wait_ge(x_src, t + 1)
                    need(pool, x_tr, t - 1)
                    settle(pool)
                    nc.gpsimd.indirect_dma_start(xg[p][:], None, xr_d[:, :],
                                                 bass.IndirectOffsetOnAxis(ap=src_x[p][:], axis=0)).then_inc(xg_in[p], 16)
                if scatter:
                    t, p, r = scatter
                    pool.wait_ge(x_y, 2 * t + 2)
                    settle(pool)
                    nc.gpsimd.indirect_dma_start(y_d[:, :], bass.IndirectOffsetOnAxis(ap=dest_x[p][:], axis=0),
                                                 yg[p][:], None).then_inc(yg_out[p], 16)

            expert_slots(pool, expert_slot)
            for k in range(2):
                pool.wait_ge(yg_out[k], 16 * XT // 2)

        @block.scalar
        def _(act):
            def a_evac_xT(g, p, r):
                act.wait_ge(a_tr, g + 1)
                need(act, a_proj, GT * g)
                nc.scalar.activation(xT[:], bank[0][:], ACT.Copy).then_inc(a_xT, 1)

            def a_evac_proj(g, p, r, k):
                t = GT * g + k
                act.wait_ge(a_proj, t + 1)
                need(act, a_f, t - 1)
                nc.scalar.activation(ex[k % 2][:], bank[1][:, 0:2 * E], ACT.Exp).then_inc(a_pev, 1)
                nc.scalar.activation(rl[k % 2][:], bank[1][:, 0:2 * E], ACT.Relu).then_inc(a_pev, 1)
                need(act, a_outer, t - 1)
                nc.scalar.activation(v9[k % 2][:, :, 0:D], bank[1][:, 2 * E:3 * E].rearrange("p (h d) -> p h d", h=H),
                                     ACT.Copy).then_inc(a_pev, 1)

            def slot(n, i):
                a1, c, d = stage(n, i, 1), stage(n, i, -1), stage(n, i, -2)
                if c:
                    act.wait_ge(c_tr, c[0] + 1)
                    need(act, c_y, c[0])
                    nc.scalar.activation(oT[:], bank[5][:], ACT.Copy).then_inc(c_oT, 1)
                if a1:
                    a_evac_xT(*a1)
                    a_evac_proj(*a1, 0)
                    a_evac_proj(*a1, 1)
                if d:
                    act.wait_ge(d_k, d[0] + 1)
                    need(act, d_gram, d[0])
                    nc.scalar.activation(k2T[:], bank[7][:], ACT.Identity, bias=bk2_s[:, 0:1]).then_inc(d_kT, 1)
                    act.wait_ge(d_tr, d[0] + 1)
                    need(act, d_q, d[0])
                    nc.scalar.activation(x2T[:], bank[5][:], ACT.Copy).then_inc(d_xT, 1)
                if a1:
                    a_evac_proj(*a1, 2)
                if d:
                    act.wait_ge(d_q, d[0] + 1)
                    nc.scalar.activation(q2T[:], bank[7][:], ACT.Identity, bias=bq2_s[:, 0:1]).then_inc(d_qT, 1)
                if a1:
                    a_evac_proj(*a1, 3)

            act.wait_ge(w_in, N_W)
            slots(act, slot)

            act.wait_ge(mean_ch, MEAN_EXP)
            nc.scalar.activation(prob[:], scores[:], ACT.Exp, bias=neg_max[:, 0:1]).then_inc(prob_e, 1)

            def cross_slot(n, i):
                v, e, f = stage(n, i, 1), stage(n, i, 0), stage(n, i, -2)
                if v:
                    g = v[0]
                    act.wait_ge(e_v, g + 1)
                    need(act, e_agg, g)
                    nc.scalar.activation(v2[:].rearrange("p t e -> p (t e)"), bank[0][:], ACT.Copy).then_inc(e_v2, 1)
                if e:
                    g = e[0]
                    act.wait_ge(e_agg, g + 1)
                    need(act, e_y, g)
                    nc.scalar.activation(aT[:], bank[1][:], ACT.Copy).then_inc(e_aT, 1)
                if f:
                    g = f[0]
                    act.wait_ge(f_xr, GT * g + GT)
                    act.dma_start(xr_rows[:, dyn(GT * g, GT), :], xr[f[1]][:]).then_inc(xr_out[f[1]], 16)
                    act.wait_ge(f_tr, g + 1)
                    need(act, f_sc, g)
                    nc.scalar.activation(xrT[:], bank[3][:], ACT.Copy).then_inc(f_xT, 1)

            cross_slots(act, cross_slot)

            act.wait_ge(r_gap, 1)
            nc.scalar.activation(gap_e[:], gap[:], ACT.Exp).then_inc(r_exp, 1)

            def expert_slot(n, i):
                xt, up, ht = expert_stage(n, i, 2), expert_stage(n, i, 1), expert_stage(n, i, 0)
                if xt:
                    t, p, r = xt
                    act.wait_ge(x_tr, t + 1)
                    need(act, x_up, t - 1)
                    nc.scalar.activation(xgT[p][:], bank[0][:, 0:P], ACT.Copy).then_inc(x_xT, 1)
                if up:
                    t, p, r = up
                    act.wait_ge(x_up, t + 1)
                    need(act, x_h, t - 1)
                    nc.scalar.activation(silu[p][:], bank[1 + p][:, HID:2 * HID], ACT.Silu).then_inc(x_silu, 1)
                if ht:
                    t, p, r = ht
                    act.wait_ge(x_ht, t + 1)
                    need(act, x_dn, t - 1)
                    nc.scalar.activation(hidT[p][:], bank[3][:, 0:HID], ACT.Copy).then_inc(x_hT, 1)

            expert_slots(act, expert_slot)

            def store(i):
                for k in range(2):
                    g, p, r = grp(k, i)
                    act.wait_ge(o_fin, g + 1)
                    act.dma_start(out[:, dyn(GT * g, GT), :], fin[p][:]).then_inc(o_out[p], 16)

            pairs(act, NG // 2, store)
            for k in range(2):
                act.wait_ge(o_out[k], 16 * NG // 2)

        @block.vector
        def _(dve):
            dve.wait_ge(w_in, N_W)
            dve.wait_ge(const_in, 16)
            n = 0

            def step(ins):
                nonlocal n
                n += 1
                ins.then_inc(bias_ch, 1)
                dve.wait_ge(bias_ch, n)
            step(nc.vector.tensor_copy(bias_p[0][:], bias_f))
            step(nc.vector.tensor_tensor(bias_r, bias_f, bias_p[0][:], ALU.subtract))
            step(nc.vector.tensor_copy(bias_p[1][:], bias_r))
            step(nc.vector.tensor_tensor(bias_a, bias_r, bias_p[1][:], ALU.subtract))
            step(nc.vector.tensor_copy(bias_p[2][:], bias_a))
            step(nc.vector.tensor_scalar(bias_b, bias_p[0][:], id_s[0:3, 0:1], None, ALU.mult))
            step(nc.vector.scalar_tensor_tensor(bias_r, bias_p[1][:], id_s[0:3, 1:2], bias_b, ALU.mult, ALU.add))
            step(nc.vector.scalar_tensor_tensor(bias3[:], bias_p[2][:], id_s[0:3, 2:3], bias_r, ALU.mult, ALU.add))

            def stats(g, p, st, st_sem, mv, mv_sem, normed):
                need(dve, mv_sem, GT * g)
                settle(dve)
                for k in range(GT):
                    nc.vector.bn_stats(st[:, k, :], X[:, bass.ds(GT * g + k, 1), :].rearrange("p a b -> p (a b)")
                                       ).then_inc(st_sem, 1)
                dve.wait_ge(st_sem, GT * g + GT)
                need(dve, normed, GT * (g - 1))
                settle(dve)
                for k in range(GT):
                    nc.vector.bn_aggr(mv[p][:, k, :], st[:, k, :]).then_inc(mv_sem, 1)

            def norm(g, p, mv, rs, dst, dst_sem):
                for k in range(GT):
                    nc.vector.tensor_scalar(dst[:, k, :], X[:, bass.ds(GT * g + k, 1), :].rearrange("p a b -> p (a b)"),
                                            mv[p][:, k, 0:1], rs[p][:, k:k + 1], ALU.subtract, ALU.mult
                                            ).then_inc(dst_sem, 1)

            def times_q(g, p, r, k):
                t = GT * g + k
                need(dve, b_red, t)
                for c, (lo, hi) in enumerate(HEADS):
                    n_h = hi - lo
                    dve.wait_ge(b_run, 3 * t + c + 1)
                    qq = qk[p][:, k, lo * D:hi * D].rearrange("p (h d) -> p h d", h=n_h)
                    nc.vector.tensor_tensor(
                        R[:, lo:hi], bank[2 + c][:, 0:n_h * D1 * D].rearrange("p (h e d) -> p h e d", h=n_h, e=D1),
                        qq.unsqueeze(2).broadcast_to([P, n_h, D1, D]), ALU.mult).then_inc(b_mul, 1)
                dve.wait_ge(b_mul, 3 * t + 3)
                if k == 0:
                    need(dve, c_on, g - 1)
                nc.vector.tensor_reduce(nd[p][:, k], R[:], AX.X, ALU.add).then_inc(b_red, 1)

            def features(g, p, r, k):
                t = GT * g + k
                dve.wait_ge(a_pev, 3 * t + 2)
                need(dve, a_outer, t - 2 * GT + 1)
                need(dve, b_mul, 3 * (t - 2 * GT) + 3)
                nc.vector.scalar_tensor_tensor(qk[p][:, k, :], ex[k % 2][:], 1.0, rl[k % 2][:], ALU.min, ALU.add
                                               ).then_inc(a_f, 1)

            def slot(n, i):
                a0, a1, b, c, d = (stage(n, i, s) for s in (2, 1, 0, -1, -2))
                if a0:
                    g, p, r = a0
                    dve.wait_ge(x_in[p], 16 * r + 16)
                    stats(g, p, st_a, a_st, mv_a, a_mv, a_xh)
                if b:
                    times_q(*b, 0)
                if c:
                    g, p, r = c
                    dve.wait_ge(b_red, GT * g + GT)
                    need(dve, c_on, g)
                    nc.vector.tensor_scalar(den[:], nd[p][:, :, :, D].rearrange("p t h -> p (t h)"), ATT_EPS, None, ALU.add
                                            ).then_inc(c_den, 1)
                    dve.wait_ge(c_den, 2 * g + 1)
                    nc.vector.reciprocal(rden[:], den[:]).then_inc(c_den, 1)
                    dve.wait_ge(c_den, 2 * g + 2)
                    need(dve, c_tr, g)
                    nc.vector.tensor_tensor(
                        on[:].rearrange("p t (h d) -> p (t h) d", h=H), nd[p][:, :, :, 0:D].rearrange("p t h d -> p (t h) d"),
                        rden[:].unsqueeze(2).broadcast_to([P, GT * H, D]), ALU.mult).then_inc(c_on, 1)
                if a1:
                    g, p, r = a1
                    dve.wait_ge(a_rs, g + 1)
                    need(dve, a_tr, g)
                    norm(g, p, mv_a, rs_a, xh, a_xh)
                if b:
                    times_q(*b, 1)
                if d:
                    g, p, r = d
                    dve.wait_ge(c_rs, g + 1)
                    need(dve, d_tr, g)
                    norm(g, p, mv_c, rs_c, xh2, d_xh)
                if a1:
                    features(*a1, 0)
                if c:
                    g, p, r = c
                    dve.wait_ge(c_y, g + 1)
                    dve.wait_ge(a_xh, GT * g + GT)
                    xg = X[:, bass.ds(GT * g, GT), :]
                    nc.vector.tensor_tensor(xg, xg, bank[6][:].rearrange("p (t e) -> p t e", t=GT), ALU.add
                                            ).then_inc(c_x1, 1)
                if a1:
                    features(*a1, 1)
                if b:
                    times_q(*b, 2)
                if c:
                    dve.wait_ge(c_x1, c[0] + 1)
                    stats(c[0], c[1], st_c, c_st, mv_c, c_mv, d_xh)
                if a1:
                    features(*a1, 2)
                if b:
                    times_q(*b, 3)
                if d:
                    g, p, r = d
                    dve.wait_ge(d_gram, g + 1)
                    need(dve, gram_out[p], 16 * r)
                    nc.vector.tensor_copy(gd[p][:], bank[6][:, 0:GT * L].rearrange("p (t l) -> p t l", t=GT)
                                          .unsqueeze(2).broadcast_to([P, GT, 2, L])).then_inc(d_gd, 1)
                if a1:
                    features(*a1, 3)

            slots(dve, slot)

            n = 0

            def mean_step(ins, wait=True):
                nonlocal n
                n += 1
                ins.then_inc(mean_ch, 1)
                if wait:
                    dve.wait_ge(mean_ch, n)

            dve.wait_ge(diag_in, 16)
            mean_step(nc.vector.tensor_reduce(mean_all[:], diag.rearrange("p t l -> p l t"), AX.X, ALU.add))
            mean_step(nc.vector.tensor_scalar(mean[:], mean_all[:], 1.0 / E, None, ALU.mult))
            assert n == MEAN_READY
            dve.wait_ge(mean_mm, 1)
            mean_step(nc.vector.tensor_scalar(mean_all[:], bank[0][:, 0:L], 1.0 / B, None, ALU.mult))
            mean_step(nc.vector.max(top8[:], mean_all[:]))
            mean_step(nc.vector.max_index(top_at[:], top8[:], mean_all[:]))
            mean_step(nc.vector.tensor_copy(top_f[:], top_at[:]))
            mean_step(nc.vector.tensor_scalar(kept[0][:], iota_s[:, 0:L], top_f[:, 0:1], None, ALU.is_equal))
            for k in range(1, LAGS):
                mean_step(nc.vector.scalar_tensor_tensor(kept[k % 2][:], iota_s[:, 0:L], top_f[:, k:k + 1],
                                                         kept[(k - 1) % 2][:], ALU.is_equal, ALU.add))
            keep = kept[(LAGS - 1) % 2]
            mean_step(nc.vector.tensor_scalar(away[:], keep[:], 1.0, 1e30, ALU.subtract, ALU.mult))
            mean_step(nc.vector.tensor_tensor(masked[:], mean[:], keep[:], ALU.mult))
            mean_step(nc.vector.tensor_tensor(scores[:], masked[:], away[:], ALU.add))
            mean_step(nc.vector.tensor_reduce(neg_max[:], scores[:], AX.X, ALU.max, negate=True))
            assert n == MEAN_EXP
            dve.wait_ge(prob_e, 1)
            mean_step(nc.vector.tensor_reduce(prob_sum[:], prob[:], AX.X, ALU.add))
            mean_step(nc.vector.reciprocal(prob_r[:], prob_sum[:]))
            falling = bass.AP(prob[:].tensor, L - 1, [[L, P], [0, 2], [-1, L - 1]])
            mean_step(nc.vector.tensor_scalar(prob2[:, :, 1:L], falling, prob_r[:, 0:1], None, ALU.mult), False)
            mean_step(nc.vector.tensor_scalar(prob2[:, :, 0:1], prob[:, 0:1].unsqueeze(1).broadcast_to([P, 2, 1]),
                                              prob_r[:, 0:1], None, ALU.mult), False)
            assert n == MEAN_STEPS

            def cross_slot(n, i):
                e, f = stage(n, i, 0), stage(n, i, -2)
                if f:
                    g, p, r = f
                    dve.wait_ge(e_rs, g + 1)
                    need(dve, f_tr, g - 1)
                    need(dve, f_x3, GT * (g - 1))
                    need(dve, xr_out[p], 16 * r)
                    norm(g, p, mv_e, rs_e, xr[p], f_xr)
                if e:
                    g, p, r = e
                    dve.wait_ge(e_y, g + 1)
                    xx = X[:, dyn(GT * g, GT), :]
                    nc.vector.tensor_tensor(xx, xx, bank[2][:].rearrange("p (t e) -> p t e", t=GT), ALU.add).then_inc(e_x2, 1)
                    dve.wait_ge(e_x2, g + 1)
                    stats(g, p, st_e, e_st, mv_e, e_mv, f_xr)
                if f:
                    g, p, r = f
                    dve.wait_ge(f_xr, GT * g + GT)
                    dve.wait_ge(e_ms, g + 1)
                    for k in range(GT):
                        xk = X[:, dyn(GT * g + k, 1), :].rearrange("p a e -> p (a e)")
                        nc.vector.scalar_tensor_tensor(xk, xr[p][:, k, :], ms_e[p][:, k:k + 1], xk, ALU.mult, ALU.add
                                                       ).then_inc(f_x3, 1)
                    dve.wait_ge(f_sc, g + 1)
                    need(dve, f_top, 2 * g)
                    settle(dve)
                    for k in range(GT):
                        nc.vector.max(best[:, k, :], bank[4][:, k * NE:(k + 1) * NE]).then_inc(f_max, 1)
                    dve.wait_ge(f_max, GT * g + GT)
                    settle(dve)
                    for k in range(GT):
                        nc.vector.max_index(best_at[:, k, :], best[:, k, :], bank[4][:, k * NE:(k + 1) * NE]).then_inc(f_at, 1)
                    dve.wait_ge(f_at, GT * g + GT)
                    nc.vector.tensor_copy(top_s[:, dyn(GT * g, GT), :], best[:, :, 0:TOPK]).then_inc(f_top, 1)
                    nc.vector.tensor_copy(top_e[:, dyn(GT * g, GT), :], best_at[:, :, 0:TOPK]).then_inc(f_top, 1)

            dve.wait_ge(w_in, N_W + 32)
            nc.vector.tensor_scalar(wu_s[:], wu_s[:], scale_s[:, 0:1], None, ALU.mult).then_inc(setup, 1)
            nc.vector.tensor_scalar(wr_s[:], wr_s[:], scale_s[:, 0:1], None, ALU.mult).then_inc(setup, 1)
            cross_slots(dve, cross_slot)

            n = 0

            def r_step(ins, wait=True):
                nonlocal n
                n += 1
                ins.then_inc(r_ch, 1)
                if wait:
                    dve.wait_ge(r_ch, n)

            dve.wait_ge(f_top, 2 * NG)
            nc.vector.tensor_tensor(gap[:], top_s[:, :, 1], top_s[:, :, 0], ALU.subtract).then_inc(r_gap, 1)
            for c in range(TOPK):
                r_step(nc.vector.tensor_tensor(hot[c][:], iota_s[:, 0:NE].unsqueeze(1).broadcast_to([P, NT, NE]),
                                               top_e[:, :, c:c + 1].broadcast_to([P, NT, NE]), ALU.is_equal))
            nc.vector.tensor_tensor(picked[:], hot[0][:], hot[1][:], ALU.add).then_inc(r_pick, 1)
            r_step(nc.vector.tensor_copy(iota_b[:], iota_s[:]))
            r_step(nc.vector.tensor_scalar(row1[:], iota_s[:, 159:160], 1.0, None, ALU.add))
            dve.wait_ge(r_exp, 1)
            r_step(nc.vector.tensor_scalar(gap_s[:], gap_e[:], 1.0, None, ALU.add))
            r_step(nc.vector.reciprocal(gate[:, 0, :], gap_s[:]))
            r_step(nc.vector.tensor_tensor(gate[:, 1, :], gap_e[:], gate[:, 0, :], ALU.mult))
            dve.wait_ge(r_cnt, 2)
            r_step(nc.vector.tensor_copy(tot[:].rearrange("p t e -> p (t e)"), bank[1][:]))
            for e in range(NE):
                r_step(nc.vector.tensor_tensor_scan(upto[:, :, e], ones_f[:, 0:NT], tot[:, :, e], 0.0, ALU.mult, ALU.add),
                       e == NE - 1)
            r_step(nc.vector.tensor_scalar(cnt_f[:], upto[:, NT - 1, :], float(P - 1), None, ALU.add))
            r_step(nc.vector.tensor_copy(cnt_i[:], cnt_f[:]))
            r_step(nc.vector.tensor_scalar(cnt_s[:], cnt_i[:], 7, None, ALU.arith_shift_right))
            r_step(nc.vector.tensor_copy(cnt_c[:], cnt_s[:]))
            r_step(nc.vector.tensor_tensor_scan(end_t[:], ones_f[:, 0:NE], cnt_c[:], 0.0, ALU.mult, ALU.add))
            r_step(nc.vector.tensor_tensor(base_t[:], end_t[:], cnt_c[:], ALU.subtract))
            r_step(nc.vector.tensor_scalar(base[:], base_t[:], float(P), None, ALU.mult))
            r_step(nc.vector.tensor_tensor(pos[:], upto[:], tot[:], ALU.subtract))
            r_step(nc.vector.tensor_tensor(pos_b[:].rearrange("p t e -> p (t e)"), pos[:].rearrange("p t e -> p (t e)"),
                                           bank[0][:], ALU.add))
            r_step(nc.vector.tensor_tensor(pos_c[:], pos_b[:], base[:].unsqueeze(1).broadcast_to([P, NT, NE]), ALU.add))
            for c in range(TOPK):
                r_step(nc.vector.tensor_tensor(mine[c][:], pos_c[:], hot[c][:], ALU.mult))
                r_step(nc.vector.tensor_reduce(slot_f[:, c, :], mine[c][:], AX.X, ALU.add))
            r_step(nc.vector.tensor_copy(slot_i[:], slot_f[:]))
            r_step(nc.vector.tensor_scalar(hi_i[:], slot_i[:], 7, None, ALU.arith_shift_right))
            r_step(nc.vector.tensor_scalar(lo_i[:], slot_i[:], P - 1, None, ALU.bitwise_and))
            r_step(nc.vector.tensor_copy(hi_f[:], hi_i[:]))
            r_step(nc.vector.tensor_copy(lo_f[:], lo_i[:]))
            r_step(nc.vector.tensor_scalar(of_tile[0][:], iota_s[:, 0:XT], end_t[:, 0:1], None, ALU.is_ge))
            for e in range(1, NE - 1):
                r_step(nc.vector.scalar_tensor_tensor(of_tile[e % 2][:], iota_s[:, 0:XT], end_t[:, e:e + 1],
                                                      of_tile[(e - 1) % 2][:], ALU.is_ge, ALU.add))
            for c, w in enumerate((2 * HID, 2 * E)):
                r_step(nc.vector.tensor_scalar(off_f[:, c, :], of_tile[(NE - 2) % 2][:], float(w), None, ALU.mult))
            r_step(nc.vector.tensor_copy(off_i[:], off_f[:]))

            def hots(i):
                for k in range(2):
                    for c in range(TOPK):
                        m = TOPK * k + c
                        col = 2 * i + k
                        need(dve, r_inv, 4 * i)
                        nc.vector.tensor_scalar(hot_lo[m][:], iota_b[:, 0:P], lo_f[:, c, dyn(col, 1)], None, ALU.is_equal
                                                ).then_inc(r_hot, 1)
                        nc.vector.tensor_scalar(hot_hi[m][:, 0, :], iota_b[:, 0:XT], hi_f[:, c, dyn(col, 1)], row1[:, 0:1],
                                                ALU.is_equal, ALU.mult).then_inc(r_hot, 1)
                        nc.vector.tensor_scalar(hot_hi[m][:, 1, :], iota_b[:, 0:XT], hi_f[:, c, dyn(col, 1)],
                                                iota_s[:, dyn(col + c * NT, 1)], ALU.is_equal, ALU.mult).then_inc(r_hot, 1)
            pairs(dve, NT // 2, hots)
            dve.wait_ge(r_inv, TOPK * NT)
            r_step(nc.vector.tensor_copy(inv_row[:], bank[2][:, 0:XT]))
            r_step(nc.vector.tensor_scalar(inv_pad[:], inv_row[:], 0.0, None, ALU.is_equal))
            r_step(nc.vector.scalar_tensor_tensor(inv[:], bank[2][:, XT:2 * XT], float(P), inv_row[:], ALU.mult, ALU.add))
            r_step(nc.vector.tensor_scalar(spare_a[:], iota_s[:, 0:XT], float(P), row1[:, 0:1], ALU.mult, ALU.add))
            r_step(nc.vector.scalar_tensor_tensor(spare_b[:], spare_a[:], float(SPARE), inv_pad[:], ALU.add, ALU.mult))
            r_step(nc.vector.scalar_tensor_tensor(dest_f[:], inv[:], -1.0, spare_b[:], ALU.add, ALU.add))
            r_step(nc.vector.tensor_copy(dest_i[:], dest_f[:]))
            r_step(nc.vector.tensor_scalar(src_i[:], dest_i[:], T - 1, None, ALU.bitwise_and))
            nc.vector.engine_nop().then_inc(r_done, 1)

            def expert_slot(n, i):
                gather, up, down = expert_stage(n, i, 4), expert_stage(n, i, 1), expert_stage(n, i, -1)
                if gather:
                    t, p, r = gather
                    need(dve, xg_in[p], 16 * r)
                    nc.vector.tensor_copy(src_x[p][:], src_i[:, dyn(t, 1)].bitcast(U32)).then_inc(x_src, 1)
                if up:
                    t, p, r = up
                    dve.wait_ge(x_silu, t + 1)
                    need(dve, x_ht, t - 1)
                    nc.vector.tensor_tensor(hid[p][:], bank[1 + p][:, 0:HID], silu[p][:], ALU.mult).then_inc(x_h, 1)
                if down:
                    t, p, r = down
                    dve.wait_ge(x_dn, t + 1)
                    need(dve, yg_out[p], 16 * r)
                    nc.vector.tensor_copy(yg[p][:], bank[5][:, 0:E]).then_inc(x_y, 1)
                    nc.vector.tensor_copy(dest_x[p][:], dest_i[:, dyn(t, 1)].bitcast(U32)).then_inc(x_y, 1)

            expert_slots(dve, expert_slot)

            def combine(i):
                for k in range(2):
                    g, p, r = grp(k, i)
                    dve.wait_ge(y_ld[p], 32 * r + 32)
                    dve.wait_ge(f_x3, NT)
                    need(dve, o_fin, g)
                    for j in range(GT):
                        tile = 4 * g + j
                        nc.vector.scalar_tensor_tensor(part[:, j, :], y_in[p][:, 0, j, :], gate[:, 0, dyn(tile, 1)],
                                                       X[:, dyn(tile, 1), :].rearrange("p a e -> p (a e)"), ALU.mult, ALU.add
                                                       ).then_inc(o_part, 1)
                    dve.wait_ge(o_part, GT * g + GT)
                    need(dve, o_out[p], 16 * r)
                    for j in range(GT):
                        tile = 4 * g + j
                        last = nc.vector.scalar_tensor_tensor(fin[p][:, j, :], y_in[p][:, 1, j, :], gate[:, 1, dyn(tile, 1)],
                                                              part[:, j, :], ALU.mult, ALU.add)
                    last.then_inc(o_fin, 1)

            pairs(dve, NG // 2, combine)

        @block.tensor
        def _(pe):
            def mm(o, l, r, start=True, stop=True):
                return nc.tensor.matmul(o, l, r, start=start, stop=stop, skip_group_check=True)

            def transposes(o, src):
                for k in range(GT):
                    last = nc.tensor.transpose(o[:, k * P:(k + 1) * P], src[:, k, :], id_s[:])
                return last

            def running_sums(g, p, r, k):
                t = GT * g + k
                pe.wait_ge(a_outer, t + 1)
                for c, (lo, hi) in enumerate(HEADS):
                    need(pe, b_mul, 3 * (t - 1) + c + 1)
                    mm(bank[2 + c][:, 0:(hi - lo) * D1 * D], tri_s[:], outer[k][:, lo:hi].rearrange("p h e d -> p (h e d)")
                       ).then_inc(b_run, 1)

            def project(g, p, r, k):
                t = GT * g + k
                if k == 0:
                    pe.wait_ge(a_xT, g + 1)
                need(pe, a_pev, 3 * t)
                mm(bank[1][:, 0:3 * E], ones3[:], b_qkv, True, False)
                mm(bank[1][:, 0:3 * E], xT[:, k * P:(k + 1) * P], wqkv[:], False, True).then_inc(a_proj, 1)

            def slot(n, i):
                a1, b, c, d = (stage(n, i, s) for s in (1, 0, -1, -2))
                if b:
                    running_sums(*b, 0)
                if c:
                    pe.wait_ge(c_on, c[0] + 1)
                    transposes(bank[5], on).then_inc(c_tr, 1)
                if a1:
                    pe.wait_ge(a_xh, GT * a1[0] + GT)
                    need(pe, a_xT, a1[0])
                    transposes(bank[0], xh).then_inc(a_tr, 1)
                if b:
                    running_sums(*b, 1)
                if a1:
                    project(*a1, 0)
                if c:
                    g = c[0]
                    pe.wait_ge(c_oT, g + 1)
                    need(pe, d_gd, g - 1)
                    mm(bank[6][:], ones3[:], b_o, True, False)
                    for k in range(GT):
                        last = mm(bank[6][:, k * P:(k + 1) * P], oT[:, k * P:(k + 1) * P], wo_s[:], False, k == GT - 1)
                    last.then_inc(c_y, 1)
                if a1:
                    project(*a1, 1)
                if b:
                    running_sums(*b, 2)
                if d:
                    g, p, r = d
                    pe.wait_ge(ct_in[p], 16 * r + 16)
                    need(pe, d_qT, g)
                    mm(bank[7][:], wk2_s[:], ct[p][:]).then_inc(d_k, 1)
                    pe.wait_ge(d_xh, GT * g + GT)
                    transposes(bank[5], xh2).then_inc(d_tr, 1)
                if a1:
                    project(*a1, 2)
                if d:
                    pe.wait_ge(d_xT, d[0] + 1)
                    pe.wait_ge(d_kT, d[0] + 1)
                    mm(bank[7][:], wq2_s[:], x2T[:]).then_inc(d_q, 1)
                if b:
                    running_sums(*b, 3)
                if a1:
                    project(*a1, 3)
                if d:
                    g = d[0]
                    pe.wait_ge(d_qT, g + 1)
                    if i is not None:
                        pe.wait_ge(c_x1, g + 2)
                    else:
                        pe.wait_ge(c_x1, min(g + 2, NG))
                    for k in range(GT):
                        for h in range(2):
                            cols = slice(k * P + h * L, k * P + h * L + L)
                            last = mm(bank[6][h * L:h * L + L, k * L:(k + 1) * L], k2T[:, cols], q2T[:, cols])
                    last.then_inc(d_gram, 1)

            pe.wait_ge(w_in, N_W)
            pe.wait_ge(const_in, 16)
            pe.wait_ge(setup, 5)
            pe.wait_ge(bias_ch, 8)
            slots(pe, slot)

            pe.wait_ge(mean_ch, MEAN_READY)
            mm(bank[0][:, 0:L], ones_f[:], mean[:]).then_inc(mean_mm, 1)
            pe.wait_ge(mean_ch, MEAN_READY + 1)

            def cross_slot(n, i):
                v, e, f = stage(n, i, 1), stage(n, i, 0), stage(n, i, -2)
                if e:
                    g, p, r = e
                    pe.wait_ge(e_v2, g + 1)
                    pe.wait_ge(circ_in[p], 32 * r + 32)
                    need(pe, e_aT, g)
                    for k in range(GT):
                        last = mm(bank[1][:, k * P:(k + 1) * P], v2[:, k, :], circ[p][:, k, :])
                    last.then_inc(e_agg, 1)
                if v:
                    g, p, r = v
                    pe.wait_ge(ct_in[p], 16 * (NG // 2 + 1) + 16 * r)
                    need(pe, e_v2, g)
                    mm(bank[0][:], ones3[:], b_v2, True, False)
                    for k in range(GT):
                        last = mm(bank[0][:, k * P:(k + 1) * P], ct[p][:, k * P:(k + 1) * P], wv2_s[:], False, k == GT - 1)
                    last.then_inc(e_v, 1)
                if f:
                    g, p, r = f
                    pe.wait_ge(f_xr, GT * g + GT)
                    need(pe, f_xT, g)
                    transposes(bank[3], xr[p]).then_inc(f_tr, 1)
                if e:
                    g, p, r = e
                    pe.wait_ge(e_aT, g + 1)
                    need(pe, e_x2, g)
                    mm(bank[2][:], ones3[:], b_o2, True, False)
                    for k in range(GT):
                        last = mm(bank[2][:, k * P:(k + 1) * P], aT[:, k * P:(k + 1) * P], wo2_s[:], False, k == GT - 1)
                    last.then_inc(e_y, 1)
                if f:
                    g, p, r = f
                    pe.wait_ge(f_xT, g + 1)
                    need(pe, f_at, GT * g)
                    for k in range(GT):
                        last = mm(bank[4][:, k * NE:(k + 1) * NE], xrT[:, k * P:(k + 1) * P], wr_s[:])
                    last.then_inc(f_sc, 1)

            pe.wait_ge(setup, 7)
            cross_slots(pe, cross_slot)

            pe.wait_ge(r_pick, 1)
            flat = picked[:].rearrange("p t e -> p (t e)")
            mm(bank[0][:], stri_s[:], flat).then_inc(r_cnt, 1)
            mm(bank[1][:], ones_f[:], flat).then_inc(r_cnt, 1)
            pe.wait_ge(circ_0, 3)
            mm(bank[2][:, 0:2 * XT], zero_b[:, 0:P], zero_b[:], True, False)
            with pe.Fori(0, NT // 2) as i:
                for m in range(4):
                    pe.wait_ge(r_hot, 12 * i + 3 * m + 3)
                    mm(bank[2][:, 0:2 * XT], hot_lo[m][:], hot_hi[m][:].rearrange("p a x -> p (a x)"), False, False
                       ).then_inc(r_inv, 1)

            def expert_slot(n, i):
                tr, up, ht, down = (expert_stage(n, i, s) for s in (2, 1, 0, -1))
                if tr:
                    t, p, r = tr
                    pe.wait_ge(xg_in[p], 16 * r + 16)
                    need(pe, x_xT, t)
                    nc.tensor.transpose(bank[0][:, 0:P], xg[p][:], id_s[:]).then_inc(x_tr, 1)
                if up:
                    t, p, r = up
                    pe.wait_ge(x_xT, t + 1)
                    need(pe, x_h, t - 1)
                    at = nc.tensor.value_load(off_i[0:1, 0, dyn(t, 1)], min_val=0, max_val=(NE - 1) * 2 * HID)
                    mm(bank[1 + p][:], xgT[p][:], wu_s[:, dyn(at, 2 * HID)]).then_inc(x_up, 1)
                if ht:
                    t, p, r = ht
                    pe.wait_ge(x_h, t + 1)
                    need(pe, x_hT, t)
                    for c in range(2):
                        last = nc.tensor.transpose(bank[3][:, c * P:(c + 1) * P], hid[p][:, c * P:(c + 1) * P], id_s[:])
                    last.then_inc(x_ht, 1)
                if down:
                    t, p, r = down
                    pe.wait_ge(x_hT, t + 1)
                    need(pe, x_y, 2 * t)
                    at = nc.tensor.value_load(off_i[0:1, 1, dyn(t, 1)], min_val=0, max_val=(NE - 1) * 2 * E)
                    for c in range(2):
                        last = mm(bank[5][:, 0:E], hidT[p][:, c * P:(c + 1) * P], wd_s[:, dyn(at + c * E, E)], c == 0, c == 1)
                    last.then_inc(x_dn, 1)

            pe.wait_ge(r_done, 1)
            expert_slots(pe, expert_slot)


N_W = 14 * 16
MEAN_READY = 2
MEAN_EXP = MEAN_READY + 4 + LAGS + 4
MEAN_STEPS = MEAN_EXP + 4

_NAMES = ("x", "ctx_t", "ctx_r", "wqkv_p", "b_all", "wo", "wq2", "wk2", "wv2", "wo2", "bq2", "bk2", "scale", "w_router",
          "w_up", "w_down", "tri", "stri", "ident", "iota")


def _arrays(**v):
    import numpy as np
    f = np.ascontiguousarray
    a = {k: np.asarray(w) for k, w in v.items()}
    s, t = np.arange(P)[:, None], np.arange(P)[None, :]
    iota = np.zeros((P, 160), np.float32)
    iota[:, :159] = np.arange(159)
    iota[:, 159] = np.arange(P)
    return {
        "x": f(a["x"].reshape(NT, P, E).transpose(1, 0, 2)),
        "ctx_t": f(a["ctx_1024"].reshape(T, E).T),
        "ctx_r": f(a["ctx_1024"][:, ::-1].reshape(T, E).T),
        "wqkv_p": np.concatenate([a["L0_attn_wq"], a["L0_attn_wk"], a["L0_attn_wv"]], axis=1),
        "b_all": np.concatenate([a["L0_attn_bq"], a["L0_attn_bk"], a["L0_attn_bv"], a["L0_attn_bo"],
                                 a["L0_xattn_bv"], a["L0_xattn_bo"]]),
        "wo": a["L0_attn_wo"], "wq2": a["L0_xattn_Wq"], "wk2": a["L0_xattn_Wk"], "wv2": a["L0_xattn_Wv"],
        "wo2": a["L0_xattn_Wo"], "bq2": a["L0_xattn_bq"].reshape(P, 1), "bk2": a["L0_xattn_bk"].reshape(P, 1),
        "scale": a["L0_ffn_norm_scale"].reshape(P, 1), "w_router": f(a["L0_ffn_w_router"].T),
        "w_up": f(a["L0_ffn_w_up"].transpose(2, 0, 1).reshape(E, NE * 2 * HID)),
        "w_down": f(a["L0_ffn_w_down"].reshape(NE, E, 2, P).transpose(3, 0, 2, 1).reshape(P, NE * 2 * E)),
        "tri": ((s <= t) & (s // L == t // L)).astype(np.float32),
        "stri": (s < t).astype(np.float32),
        "ident": np.eye(P, dtype=np.float32),
        "iota": iota,
    }


def kernel(**inputs):
    import numpy as _np
    import concourse.bacc as _bacc
    from concourse import mybir as _mybir
    from concourse.bass_utils import run_bass_kernel_spmd as _run

    nc = _bacc.Bacc("TRN2", target_bir_lowering=False, num_devices=1)
    arrays = _arrays(**inputs)
    args = [nc.dram_tensor(f"in_{n}", arrays[n].shape, _mybir.dt.from_np(arrays[n].dtype), kind="ExternalInput").ap()
            for n in _NAMES]
    out = nc.dram_tensor("out_x", (P, NT, E), F32, kind="ExternalOutput").ap()
    build(nc, *args, out)
    r = _run(nc, [{f"in_{n}": arrays[n] for n in _NAMES}], core_ids=[0])
    got = r.results[0]["out_x"]
    return _np.ascontiguousarray(got.transpose(1, 0, 2)).reshape(B, L, E)
```

```python
from contextlib import ExitStack

import concourse.bass as bass
from concourse import mybir

F32, BF16 = mybir.dt.float32, mybir.dt.bfloat16
I32, U32 = mybir.dt.int32, mybir.dt.uint32
ALU = mybir.AluOpType
ACT = mybir.ActivationFunctionType
AX = mybir.AxisListType

P = 128
B, L, E, H = 128, 64, 128, 16
D = E // H
D1 = D + 1
T = B * L
NT = T // P
GT = 4
NG = NT // GT
GW = GT * P
NE, HID, TOPK = 8, 256, 2
LAGS = 5
XT = T * TOPK // P + NE
UNROLL = 8
W_E = 2 * HID + 2 * E
ROW = E + 2
PADS = NE * T
SPARE = T * TOPK
LN_EPS, ATT_EPS, RMS_EPS = 1e-5, 1e-6, 1e-6
HEADS = [(0, 6), (6, 11), (11, 16)]


def need(eng, sem, count):
    if not (isinstance(count, int) and count <= 0):
        eng.wait_ge(sem, count)


def bcast_rows(ap, rows, width):
    return bass.AP(ap.tensor, 0, [[0, rows], [1, width]])


def build(nc, x, ctx_t, ctx_r, wqkv_p, b_all, wo, wq2, wk2, wv2, wo2, bq2, bk2, scale, w_router, w_up, w_down,
          tri, stri, ident, iota, where, out):
    with ExitStack() as ctx:
        def sb(name, shape, dt=F32):
            return ctx.enter_context(nc.sbuf_tensor(name, shape, dt))

        def sem(name):
            return ctx.enter_context(nc.semaphore(name))

        def sems(name, n):
            return [sem(f"{name}{i}") for i in range(n)]

        gram_d = nc.dram_tensor("gram_d", (B * L * 2 * L,), F32).ap()
        prob_d = nc.dram_tensor("prob_d", (B * 2 * L,), F32).ap()
        xs_d = nc.dram_tensor("xs_d", (PADS + NE * P, ROW), F32).ap()
        y_d = nc.dram_tensor("y_d", (SPARE + NE * P, E), F32).ap()

        wqkv = sb("wqkv", [P, 3 * E])
        wo_s, wq2_s, wk2_s, wv2_s, wo2_s = (sb(n, [P, E]) for n in ("wo_s", "wq2_s", "wk2_s", "wv2_s", "wo2_s"))
        bq2_s, bk2_s, scale_s = sb("bq2_s", [P, 1]), sb("bk2_s", [P, 1]), sb("scale_s", [P, 1])
        wr_s = sb("wr_s", [P, NE])
        w_s = sb("w_s", [P, NE * W_E])
        w_up_s = w_s[:].rearrange("p (e w) -> p e w", e=NE)[:, :, 0:2 * HID]
        w_down_s = w_s[:].rearrange("p (e w) -> p e w", e=NE)[:, :, 2 * HID:W_E]
        tri_s, stri_s, id_s = sb("tri_s", [P, P]), sb("stri_s", [P, P]), sb("id_s", [P, P])
        iota_s = sb("iota_s", [P, 160])
        where_s = sb("where_s", [P, NT * TOPK + 4 * NE])
        dest_s = where_s[:, 0:NT * TOPK].rearrange("p (t c) -> p t c", c=TOPK)
        pad_dest, pad_row, pad_0, region_0 = (where_s[:, NT * TOPK + j * NE:NT * TOPK + (j + 1) * NE] for j in range(4))
        ones_f = sb("ones_f", [P, P])
        stri_b, ones_b = sb("stri_b", [P, P], BF16), sb("ones_b", [P, P], BF16)
        ones3 = sb("ones3", [3, P], BF16)
        NBIAS = 6 * E
        bias_p = [sb(f"bias_p{i}", [3, NBIAS], BF16) for i in range(3)]
        bias3 = sb("bias3", [3, NBIAS], BF16)
        power = sb("power", [P, 2 * GT])

        X = sb("X", [P, NT, E])

        st_a, mv_a = sb("st_a", [P, GT, 6]), [sb(f"mv_a{i}", [P, GT, 2]) for i in range(2)]
        ve_a, rs_a = sb("ve_a", [P, GT]), [sb(f"rs_a{i}", [P, GT]) for i in range(2)]
        mr_a, nb_a = sb("mr_a", [P, GT]), [sb(f"nb_a{i}", [P, GT]) for i in range(2)]
        xh = sb("xh", [P, GT, E])
        xT = sb("xT", [P, GW])
        ex, rl = [sb(f"ex{i}", [P, 2 * E]) for i in range(2)], [sb(f"rl{i}", [P, 2 * E]) for i in range(2)]
        v9 = [sb(f"v9_{i}", [P, H, D1]) for i in range(2)]
        qk = [sb(f"qk{i}", [P, GT, 2 * E]) for i in range(2)]
        shared = sb("shared", [P, GT * H * D1 * D])
        bias_f, bias_r, bias_a, bias_b = (shared[0:3, i * NBIAS:(i + 1) * NBIAS] for i in range(4))
        outer = [shared[:, i * H * D1 * D:(i + 1) * H * D1 * D].rearrange("p (h e d) -> p h e d", h=H, e=D1)
                 for i in range(GT)]
        diag = shared[:, 0:L * L].rearrange("p (t l) -> p t l", t=L)
        y_in = [shared[:, i * TOPK * GW:(i + 1) * TOPK * GW].rearrange("p (t c e) -> p t c e", c=TOPK, t=GT)
                for i in range(2)]
        R = sb("R", [P, H, D1, D])
        nd = [sb(f"nd{i}", [P, GT, H, D1]) for i in range(2)]
        den, rden = sb("den", [P, GT * H]), sb("rden", [P, GT * H])
        on = sb("on", [P, GT, E])
        oT = sb("oT", [P, GW])
        st_c, mv_c = sb("st_c", [P, GT, 6]), [sb(f"mv_c{i}", [P, GT, 2]) for i in range(2)]
        ve_c, rs_c = sb("ve_c", [P, GT]), [sb(f"rs_c{i}", [P, GT]) for i in range(2)]
        mr_c, nb_c = sb("mr_c", [P, GT]), [sb(f"nb_c{i}", [P, GT]) for i in range(2)]
        xh2 = sb("xh2", [P, GT, E])
        x2T, q2T, k2T = sb("x2T", [P, GW]), sb("q2T", [P, GW]), sb("k2T", [P, GW])
        ct = [sb(f"ct{i}", [P, GW]) for i in range(2)]
        gd = [sb(f"gd{i}", [P, GT, 2, L]) for i in range(2)]

        mean, mean_all = sb("mean", [P, L]), sb("mean_all", [P, L])
        top8, top_at, top_f = sb("top8", [P, 8]), sb("top_at", [P, 8], U32), sb("top_f", [P, 8])
        kept = [sb(f"kept{i}", [P, L]) for i in range(2)]
        away, masked, scores = sb("away", [P, L]), sb("masked", [P, L]), sb("scores", [P, L])
        neg_max, prob, prob_sum, prob_r = sb("neg_max", [P, 1]), sb("prob", [P, L]), sb("prob_sum", [P, 1]), sb("prob_r", [P, 1])
        prob2 = sb("prob2", [P, 2, L])
        circ = [sb(f"circ{i}", [P, GT, P]) for i in range(2)]
        v2, aT = sb("v2", [P, GT, E]), sb("aT", [P, GW])
        st_e, mv_e = sb("st_e", [P, GT, 6]), [sb(f"mv_e{i}", [P, GT, 2]) for i in range(2)]
        vv_e = [sb(f"vv_e{i}", [P, 2 * GT]) for i in range(2)]
        rs_e = [sb(f"rs_e{i}", [P, 2 * GT]) for i in range(2)]
        vr_e = sb("vr_e", [P, GT])
        ms_e = sb("ms_e", [P, GT])
        xr = [sb(f"xr{i}", [P, GT, E]) for i in range(2)]
        xs = [sb(f"xs{i}", [P, GT, TOPK, ROW]) for i in range(2)]
        xrT = sb("xrT", [P, GW])
        best, best_at = sb("best", [P, GT, 8]), sb("best_at", [P, GT, 8], U32)

        top_e = sb("top_e", [P, GT, TOPK])
        hot, mine = sb("hot", [P, GT, TOPK, NE]), sb("mine", [P, GT, TOPK, NE])
        picked = sb("picked", [P, GT + 1, NE], BF16)
        gap, gap_e, gap_s = sb("gap", [P, GT]), sb("gap_e", [P, GT]), sb("gap_s", [P, GT])
        used = [sb(f"used{i}", [P, NE]) for i in range(2)]
        pos, slot_f = sb("pos", [P, GT, NE]), sb("slot_f", [P, GT, TOPK])
        slot_u = [sb(f"slot_u{i}", [P, GT * TOPK], U32) for i in range(2)]
        pads = sb("pads", [P, NE, ROW])
        used_i, in_i = sb("used_i", [P, NE], I32), sb("in_i", [P, NE], I32)
        in_f, fits, open_f, pad_d, pad_m, pad_f = (sb(n, [P, NE]) for n in ("in_f", "fits", "open_f", "pad_d", "pad_m", "pad_f"))
        pad_u = sb("pad_u", [P, NE], U32)
        cnt_f, cnt_c, end_t, skip = (sb(n, [P, NE]) for n in ("cnt_f", "cnt_c", "end_t", "skip"))
        cnt_i, cnt_s = sb("cnt_i", [P, NE], I32), sb("cnt_s", [P, NE], I32)
        of_tile = [sb(f"of_tile{i}", [P, XT]) for i in range(2)]
        jump, row_f = sb("jump", [P, XT]), [sb(f"row_f{i}", [P, XT]) for i in range(2)]
        off_f = sb("off_f", [P, XT])
        off_i = sb("off_i", [P, XT], I32)
        row_i = sb("row_i", [P, XT], I32)

        dest_x = [sb(f"dest_x{i}", [P, 1], U32) for i in range(4)]
        xg, xgT = [sb(f"xg{i}", [P, ROW]) for i in range(4)], [sb(f"xgT{i}", [P, P]) for i in range(2)]
        silu, hid = [sb(f"silu{i}", [P, HID]) for i in range(2)], [sb(f"hid{i}", [P, HID]) for i in range(2)]
        hidT, yg = [sb(f"hidT{i}", [P, HID]) for i in range(2)], [sb(f"yg{i}", [P, E]) for i in range(4)]
        gates = [sb(f"gates{i}", [P, 1]) for i in range(4)]
        part, fin = sb("part", [P, GT, E]), [sb(f"fin{i}", [P, GT, E]) for i in range(2)]

        bank = [ctx.enter_context(nc.psum_tensor(f"bank{i}", [P, 512], F32)) for i in range(8)]

        settled = sem("settled")
        const_in = sem("const_in")
        w_in = sem("w_in")
        bias_ch = sem("bias_ch")
        setup = sem("setup")
        x_in = sems("x_in", 2)
        ct_in = sems("ct_in", 2)
        a_st, a_mv, a_ve, a_rs, a_xh = sem("a_st"), sem("a_mv"), sem("a_ve"), sem("a_rs"), sem("a_xh")
        a_mr, a_nb, c_mr, c_nb = sem("a_mr"), sem("a_nb"), sem("c_mr"), sem("c_nb")
        a_tr, a_xT, a_proj, a_pev, a_f, a_outer = (sem(n) for n in ("a_tr", "a_xT", "a_proj", "a_pev", "a_f", "a_outer"))
        b_run, b_mul, b_red = sem("b_run"), sem("b_mul"), sem("b_red")
        c_den, c_on, c_tr, c_oT, c_y, c_x1, c_st, c_mv, c_ve, c_rs = (
            sem(n) for n in ("c_den", "c_on", "c_tr", "c_oT", "c_y", "c_x1", "c_st", "c_mv", "c_ve", "c_rs"))
        d_xh, d_tr, d_xT, d_k, d_kT, d_q, d_qT, d_gram, d_gd = (
            sem(n) for n in ("d_xh", "d_tr", "d_xT", "d_k", "d_kT", "d_q", "d_qT", "d_gram", "d_gd"))
        gram_out = sems("gram_out", 2)
        diag_in, mean_ch, mean_mm, prob_e = sem("diag_in"), sem("mean_ch"), sem("mean_mm"), sem("prob_e")
        prob_out, circ_0, circ_in = sem("prob_out"), sem("circ_0"), sems("circ_in", 2)
        e_v, e_v2, e_agg, e_aT, e_y, e_x2, e_st, e_mv, e_ve, e_rs = (
            sem(n) for n in ("e_v", "e_v2", "e_agg", "e_aT", "e_y", "e_x2", "e_st", "e_mv", "e_ve", "e_rs"))
        e_vr, e_ms = sem("e_vr"), sem("e_ms")
        f_x3 = sem("f_x3")
        f_xr, f_tr, f_xT, f_sc, f_max, f_at, f_top = (
            sem(n) for n in ("f_xr", "f_tr", "f_xT", "f_sc", "f_max", "f_at", "f_top"))
        f_copy = sem("f_copy")
        s_hot, s_pick, s_gap, s_exp, s_cnt, s_pos, s_used, s_mine, s_slot, s_go = (
            sem(n) for n in ("s_hot", "s_pick", "s_gap", "s_exp", "s_cnt", "s_pos", "s_used", "s_mine", "s_slot", "s_go"))
        s_gate, s_ready = sem("s_gate"), sem("s_ready")
        xs_out = sems("xs_out", 2)
        pads_made, pads_in, pad_at, pads_out, r_ch, r_done = (
            sem(n) for n in ("pads_made", "pads_in", "pad_at", "pads_out", "r_ch", "r_done"))
        x_dest, x_tr, x_xT, x_up, x_silu, x_h, x_ht, x_hT, x_dn, x_y = (
            sem(n) for n in ("x_dest", "x_tr", "x_xT", "x_up", "x_silu", "x_h", "x_ht", "x_hT", "x_dn", "x_y"))
        x_gate = sem("x_gate")
        xg_in, yg_out = sems("xg_in", 4), sems("yg_out", 4)
        y_ld, o_part, o_fin, o_out = sems("y_ld", 2), sem("o_part"), sem("o_fin"), sems("o_out", 2)

        b_qkv = bias3[:, 0:3 * E]
        b_o = bias3[:, 3 * E:4 * E].unsqueeze(1).broadcast_to([3, GT, E])
        b_v2 = bias3[:, 4 * E:5 * E].unsqueeze(1).broadcast_to([3, GT, E])
        b_o2 = bias3[:, 5 * E:6 * E].unsqueeze(1).broadcast_to([3, GT, E])

        def settle(eng):
            eng.sem_inc(settled, 1)

        def grp(n, i=None):
            if i is None:
                return n, n % 2, n // 2
            return 2 * i + n, n % 2, i + n // 2

        FIRST, LAST = -2, NG + 1

        def slots(eng, slot):
            for n in range(FIRST, 4):
                slot(n, None)
            with eng.Fori(2, (NG - 2) // 2) as i:
                slot(0, i)
                slot(1, i)
            for n in range(NG - 2, LAST + 1):
                slot(n, None)

        def stage(n, i, shift):
            if i is None and not 0 <= n + shift < NG:
                return None
            return grp(n + shift, i)

        def pairs(eng, count, body):
            body(0)
            with eng.Fori(1, count) as i:
                body(i)

        def cross_slots(eng, slot):
            for n in range(-1, 6):
                slot(n, None)
            with eng.Fori(3, NG // 2 - 1) as i:
                slot(0, i)
                slot(1, i)
            for n in range(NG - 2, NG + 3):
                slot(n, None)

        def expert_stage(n, i, shift):
            if i is None:
                return (n + shift, (n + shift) % 4, (n + shift) // 4) if 0 <= n + shift < XT else None
            return UNROLL * i + n + shift, (n + shift) % 4, UNROLL // 4 * i + (n + shift) // 4

        def expert_slots(eng, slot):
            for n in range(-4, UNROLL):
                slot(n, None)
            with eng.Fori(1, XT // UNROLL - 1) as i:
                for n in range(UNROLL):
                    slot(n, i)
            for n in range(XT - UNROLL, XT + 1):
                slot(n, None)

        y_rows = y_d[0:SPARE, :].rearrange("(t p c) e -> p t (c e)", p=P, c=TOPK)
        dyn = bass.ds

        block = ctx.enter_context(nc.Block())

        @block.sync
        def _(sp):
            n_w = 0
            sp.dma_start(id_s[:], ident).then_inc(const_in, 16)
            for dst, src in ((wqkv[:], wqkv_p), (wo_s[:], wo), (wq2_s[:], wq2), (wk2_s[:], wk2), (wv2_s[:], wv2),
                             (wo2_s[:], wo2), (bq2_s[:], bq2), (bk2_s[:], bk2), (scale_s[:], scale),
                             (wr_s[:], w_router), (tri_s[:], tri), (stri_s[:], stri),
                             (iota_s[:], iota), (where_s[:], where), (bias_f, bcast_rows(b_all, 3, NBIAS))):
                sp.dma_start(dst, src).then_inc(w_in, 16)
                n_w += 16
            assert n_w == N_W

            def x_load(i):
                for k in range(2):
                    need(sp, x_in[k], i * 16)
                    sp.dma_start(X[:, bass.ds((2 * i + k) * GT, GT), :],
                                 x[:, bass.ds((2 * i + k) * GT, GT), :]).then_inc(x_in[k], 16)

            pairs(sp, NG // 2, x_load)
            for k in range(2):
                sp.dma_start(ct[k][:], ctx_t[:, k * GW:(k + 1) * GW]).then_inc(ct_in[k], 16)

            def gram_store(g, p, r):
                sp.wait_ge(d_gd, g + 1)
                settle(sp)
                need(sp, gram_out[p], 16 * r)
                sp.dma_start(bass.AP(gram_d.tensor, g * (GT * P * 2 * L), [[2 * L, P], [P * 2 * L, GT], [1, 2 * L]]),
                             gd[p][:].rearrange("p t a b -> p t (a b)")).then_inc(gram_out[p], 16)

            def gram_and_context(i):
                for k in range(2):
                    g, p, r = grp(k, i)
                    gram_store(g, p, r)
                    sp.wait_ge(d_k, g + 1)
                    sp.dma_start(ct[p][:], ctx_t[:, bass.ds((g + 2) * GW, GW)]).then_inc(ct_in[p], 16)

            pairs(sp, NG // 2 - 1, gram_and_context)
            for g in (NG - 2, NG - 1):
                gram_store(*grp(g))
            for k in range(2):
                sp.wait_ge(gram_out[k], 16 * NG // 2)
            sp.wait_ge(b_run, 3 * NT)
            sp.dma_start(diag, bass.AP(gram_d.tensor, 0, [[L * 2 * L, P], [2 * L + 1, L], [1, L]])).then_inc(diag_in, 16)

            def ctx_load(g, p, r):
                sp.dma_start(ct[p][:], ctx_r[:, dyn(g * GW, GW)]).then_inc(ct_in[p], 16)

            def circ_load(g, p, r):
                for h in range(2):
                    src = bass.AP(prob_d.tensor, g * (GT * 2 * 2 * L) + (h * 2 * L + 1), [[1, L], [2 * 2 * L, GT], [1, L]])
                    sp.dma_start(circ[p][h * L:(h + 1) * L, :, h * L:(h + 1) * L], src).then_inc(circ_in[p], 16)

            sp.wait_ge(d_k, NG)
            for g in range(2):
                ctx_load(*grp(g))
            sp.wait_ge(w_in, N_W)
            for dst, src in ((w_up_s, w_up), (w_down_s, w_down)):
                sp.dma_start(dst, src).then_inc(w_in, 16)
            sp.wait_ge(pads_made, 3)
            sp.dma_start(xs_d[PADS:PADS + NE * P, :].rearrange("(e p) r -> p e r", p=P), pads[:]).then_inc(pads_in, 16)
            sp.wait_ge(mean_ch, MEAN_STEPS)
            sp.dma_start(bass.AP(prob_d.tensor, 0, [[2 * L, P], [1, 2 * L]]), prob2[:].rearrange("p a l -> p (a l)")
                         ).then_inc(prob_out, 16)
            sp.wait_ge(prob_out, 16)
            sp.wait_ge(circ_0, 2)
            for g in range(2):
                circ_load(*grp(g))

            def next_loads(i):
                for k in range(2):
                    g, p, r = grp(k, i)
                    sp.wait_ge(e_v, g + 1)
                    ctx_load(*grp(k + 2, i))
                    sp.wait_ge(e_agg, g + 1)
                    circ_load(*grp(k + 2, i))

            pairs(sp, NG // 2 - 1, next_loads)

            for k in range(2):
                sp.wait_ge(xs_out[k], 16 * TOPK * GT * NG // 2)
            sp.wait_ge(pads_out, 16 * NE)
            sp.wait_ge(pads_in, 16)
            sp.wait_ge(r_done, 1)

            def expert_slot(n, i):
                load = expert_stage(n, i, 4)
                if load:
                    t, q, r = load
                    at = sp.value_load(row_i[0:1, dyn(t, 1)], min_val=0, max_val=PADS + (NE - 1) * P)
                    need(sp, x_tr, t - 3)
                    need(sp, x_dest, t - 3)
                    need(sp, x_gate, t - 3)
                    sp.dma_start(xg[q][:], xs_d[dyn(at, P), :]).then_inc(xg_in[q], 16)

            expert_slots(sp, expert_slot)

            for q in range(4):
                sp.wait_ge(yg_out[q], 16 * XT // 4)

            def y_load(i):
                for k in range(2):
                    g, p, r = grp(k, i)
                    need(sp, o_fin, g - 1)
                    sp.dma_start(y_in[p].rearrange("p t c e -> p t (c e)"), y_rows[:, dyn(GT * g, GT), :]
                                 ).then_inc(y_ld[p], 16)

            pairs(sp, NG // 2, y_load)

        @block.gpsimd
        def _(pool):
            pool.memset(ones3[:], 1.0).then_inc(setup, 1)
            pool.memset(power[:], -0.5).then_inc(setup, 1)
            for k in range(2):
                pool.memset(v9[k][:], 1.0).then_inc(setup, 1)
            pool.memset(ones_f[:], 1.0).then_inc(setup, 1)
            pool.memset(pads[:], 0.0).then_inc(pads_made, 1)
            pool.memset(picked[:], 0.0).then_inc(pads_made, 1)
            pool.wait_ge(setup, 5)

            def rstd(g, p, stats, seen, ve, ve_sem, rs, rs_sem, mr, mr_sem, nb, nb_sem, normed):
                need(pool, rs_sem, g)
                pool.wait_ge(seen, GT * g + GT)
                settle(pool)
                nc.gpsimd.tensor_scalar(ve[:], stats[p][:, :, 1], 1.0, LN_EPS, ALU.mult, ALU.add).then_inc(ve_sem, 1)
                pool.wait_ge(ve_sem, g + 1)
                need(pool, normed, GT * (g - 1))
                nc.gpsimd.tensor_tensor(rs[p][:], ve[:], power[:, 0:GT], ALU.pow).then_inc(rs_sem, 1)
                need(pool, nb_sem, g)
                pool.wait_ge(rs_sem, g + 1)
                nc.gpsimd.tensor_tensor(mr[:], stats[p][:, :, 0], rs[p][:], ALU.mult).then_inc(mr_sem, 1)
                pool.wait_ge(mr_sem, g + 1)
                settle(pool)
                nc.gpsimd.tensor_scalar(nb[p][:], mr[:], -1.0, None, ALU.mult).then_inc(nb_sem, 1)

            def outer_product(g, p, r, k):
                t = GT * g + k
                pool.wait_ge(a_f, t + 1)
                pool.wait_ge(a_pev, 3 * t + 3)
                need(pool, b_run, 3 * (t - GT) + 3)
                kk = qk[p][:, k, E:2 * E].rearrange("p (h d) -> p h d", h=H)
                nc.gpsimd.tensor_tensor(
                    outer[k], v9[k % 2][:].unsqueeze(3).broadcast_to([P, H, D1, D]),
                    kk.unsqueeze(2).broadcast_to([P, H, D1, D]), ALU.mult).then_inc(a_outer, 1)

            def slot(n, i):
                a0, a1, c = stage(n, i, 2), stage(n, i, 1), stage(n, i, -1)
                if a1:
                    outer_product(*a1, 0)
                if a0:
                    rstd(a0[0], a0[1], mv_a, a_mv, ve_a, a_ve, rs_a, a_rs, mr_a, a_mr, nb_a, a_nb, a_xh)
                if a1:
                    outer_product(*a1, 1)
                    outer_product(*a1, 2)
                if c:
                    rstd(c[0], c[1], mv_c, c_mv, ve_c, c_ve, rs_c, c_rs, mr_c, c_mr, nb_c, c_nb, d_xh)
                if a1:
                    outer_product(*a1, 3)

            slots(pool, slot)

            for k in range(2):
                nc.gpsimd.memset(circ[k][:], 0.0).then_inc(circ_0, 1)

            def scatter_rows(g, p, r, k):
                for c in range(TOPK):
                    m = TOPK * k + c
                    nc.gpsimd.indirect_dma_start(xs_d[:, :], bass.IndirectOffsetOnAxis(ap=slot_u[p][:, m:m + 1], axis=0),
                                                 xs[p][:, k, c, :], None).then_inc(xs_out[p], 16)

            def cross_slot(n, i):
                e, s = stage(n, i, 0), stage(n, i, -3)
                if e:
                    g, p, r = e
                    pool.wait_ge(e_ve, 2 * g + 2)
                    need(pool, f_xr, GT * (g - 1))
                    need(pool, e_ms, g - 1)
                    nc.gpsimd.tensor_tensor(rs_e[p][:], vv_e[p][:], power[:], ALU.pow).then_inc(e_rs, 1)
                if s:
                    pool.wait_ge(s_ready, s[0] + 1)
                    pool.wait_ge(s_gate, 2 * s[0] + 2)
                    pool.wait_ge(f_copy, 3 * s[0] + 3)
                    settle(pool)
                    for k in range(GT):
                        scatter_rows(*s, k)

            cross_slots(pool, cross_slot)

            pool.wait_ge(pad_at, 1)
            pool.wait_ge(pads_made, 3)
            pool.wait_ge(pads_in, 16)
            for e in range(NE):
                nc.gpsimd.indirect_dma_start(xs_d[:, :], bass.IndirectOffsetOnAxis(ap=pad_u[:, e:e + 1], axis=0),
                                             pads[:, e, :], None).then_inc(pads_out, 16)

            def expert_slot(n, i):
                scatter = expert_stage(n, i, -1)
                if scatter:
                    t, q, r = scatter
                    pool.wait_ge(x_y, t + 1)
                    pool.wait_ge(x_dest, t + 1)
                    settle(pool)
                    nc.gpsimd.indirect_dma_start(y_d[:, :], bass.IndirectOffsetOnAxis(ap=dest_x[q][:], axis=0),
                                                 yg[q][:], None).then_inc(yg_out[q], 16)

            expert_slots(pool, expert_slot)
            for q in range(4):
                pool.wait_ge(yg_out[q], 16 * XT // 4)

        @block.scalar
        def _(act):
            def a_evac_xT(g, p, r):
                act.wait_ge(a_tr, g + 1)
                need(act, a_proj, GT * g)
                nc.scalar.activation(xT[:], bank[0][:], ACT.Copy).then_inc(a_xT, 1)

            def a_evac_proj(g, p, r, k):
                t = GT * g + k
                act.wait_ge(a_proj, t + 1)
                need(act, a_f, t - 1)
                nc.scalar.activation(ex[k % 2][:], bank[1][:, 0:2 * E], ACT.Exp).then_inc(a_pev, 1)
                nc.scalar.activation(rl[k % 2][:], bank[1][:, 0:2 * E], ACT.Relu).then_inc(a_pev, 1)
                need(act, a_outer, t - 1)
                nc.scalar.activation(v9[k % 2][:, :, 0:D], bank[1][:, 2 * E:3 * E].rearrange("p (h d) -> p h d", h=H),
                                     ACT.Copy).then_inc(a_pev, 1)

            def norm(g, p, rs, nb, nb_sem, dst, dst_sem):
                act.wait_ge(nb_sem, g + 1)
                for k in range(GT):
                    nc.scalar.activation(dst[:, k, :], X[:, bass.ds(GT * g + k, 1), :].rearrange("p a b -> p (a b)"),
                                         ACT.Identity, bias=nb[p][:, k:k + 1], scale=rs[p][:, k:k + 1]).then_inc(dst_sem, 1)

            def slot(n, i):
                a1, c, d = stage(n, i, 1), stage(n, i, -1), stage(n, i, -2)
                if a1:
                    g, p, r = a1
                    need(act, a_tr, g)
                    norm(g, p, rs_a, nb_a, a_nb, xh, a_xh)
                    a_evac_xT(*a1)
                if d:
                    g, p, r = d
                    need(act, d_tr, g)
                    norm(g, p, rs_c, nb_c, c_nb, xh2, d_xh)
                if a1:
                    a_evac_proj(*a1, 0)
                if c:
                    act.wait_ge(c_tr, c[0] + 1)
                    need(act, c_y, c[0])
                    nc.scalar.activation(oT[:], bank[5][:], ACT.Copy).then_inc(c_oT, 1)
                if a1:
                    a_evac_proj(*a1, 1)
                if d:
                    act.wait_ge(d_k, d[0] + 1)
                    need(act, d_gram, d[0])
                    nc.scalar.activation(k2T[:], bank[7][:], ACT.Identity, bias=bk2_s[:, 0:1]).then_inc(d_kT, 1)
                    act.wait_ge(d_tr, d[0] + 1)
                    need(act, d_q, d[0])
                    nc.scalar.activation(x2T[:], bank[5][:], ACT.Copy).then_inc(d_xT, 1)
                if a1:
                    a_evac_proj(*a1, 2)
                if d:
                    act.wait_ge(d_q, d[0] + 1)
                    nc.scalar.activation(q2T[:], bank[7][:], ACT.Identity, bias=bq2_s[:, 0:1]).then_inc(d_qT, 1)
                if a1:
                    a_evac_proj(*a1, 3)
                if d:
                    g, p, r = d
                    act.wait_ge(d_gram, g + 1)
                    need(act, gram_out[p], 16 * r)
                    nc.scalar.activation(gd[p][:], bank[6][:, 0:GT * L].rearrange("p (t l) -> p t l", t=GT)
                                         .unsqueeze(2).broadcast_to([P, GT, 2, L]), ACT.Copy).then_inc(d_gd, 1)

            act.wait_ge(w_in, N_W)
            slots(act, slot)

            act.wait_ge(mean_ch, MEAN_EXP)
            nc.scalar.activation(prob[:], scores[:], ACT.Exp, bias=neg_max[:, 0:1]).then_inc(prob_e, 1)

            def cross_slot(n, i):
                v, e, f, s = (stage(n, i, k) for k in (1, 0, -2, -3))
                if e:
                    g = e[0]
                    act.wait_ge(e_agg, g + 1)
                    need(act, e_y, g)
                    nc.scalar.activation(aT[:], bank[1][:], ACT.Copy).then_inc(e_aT, 1)
                if v:
                    g = v[0]
                    act.wait_ge(e_v, g + 1)
                    nc.scalar.activation(v2[:].rearrange("p t e -> p (t e)"), bank[0][:], ACT.Copy).then_inc(e_v2, 1)
                if s:
                    act.wait_ge(s_gap, s[0] + 1)
                    need(act, s_gate, 2 * s[0])
                    nc.scalar.activation(gap_e[:], gap[:], ACT.Exp).then_inc(s_exp, 1)
                if f:
                    g, p, r = f
                    act.wait_ge(f_tr, g + 1)
                    need(act, f_sc, g)
                    nc.scalar.activation(xrT[:], bank[3][:], ACT.Copy).then_inc(f_xT, 1)
                    act.wait_ge(f_xr, GT * g + GT)
                    need(act, xs_out[p], 16 * TOPK * GT * r)
                    for c in range(TOPK):
                        nc.scalar.activation(xs[p][:, :, c, 0:E], xr[p][:], ACT.Copy).then_inc(f_copy, 1)
                    nc.scalar.activation(xs[p][:, :, :, E:E + 1], dest_s[:, dyn(GT * g, GT), :].unsqueeze(3), ACT.Copy
                                         ).then_inc(f_copy, 1)

            cross_slots(act, cross_slot)

            def expert_slot(n, i):
                xt, up, ht = expert_stage(n, i, 2), expert_stage(n, i, 1), expert_stage(n, i, 0)
                if xt:
                    t, p = xt[0], xt[1] % 2
                    act.wait_ge(x_tr, t + 1)
                    need(act, x_up, t - 1)
                    nc.scalar.activation(xgT[p][:], bank[0][:, 0:P], ACT.Copy).then_inc(x_xT, 1)
                if up:
                    t, p = up[0], up[1] % 2
                    act.wait_ge(x_up, t + 1)
                    need(act, x_h, t - 1)
                    nc.scalar.activation(silu[p][:], bank[1 + p][:, HID:2 * HID], ACT.Silu).then_inc(x_silu, 1)
                if ht:
                    t, p = ht[0], ht[1] % 2
                    act.wait_ge(x_ht, t + 1)
                    need(act, x_dn, t - 1)
                    nc.scalar.activation(hidT[p][:], bank[3][:, 0:HID], ACT.Copy).then_inc(x_hT, 1)

            expert_slots(act, expert_slot)

            def store(i):
                for k in range(2):
                    g, p, r = grp(k, i)
                    act.wait_ge(o_fin, g + 1)
                    act.dma_start(out[:, dyn(GT * g, GT), :], fin[p][:]).then_inc(o_out[p], 16)

            pairs(act, NG // 2, store)
            for k in range(2):
                act.wait_ge(o_out[k], 16 * NG // 2)

        @block.vector
        def _(dve):
            dve.wait_ge(w_in, N_W)
            dve.wait_ge(const_in, 16)
            n = 0

            def step(ins):
                nonlocal n
                n += 1
                ins.then_inc(bias_ch, 1)
                dve.wait_ge(bias_ch, n)
            step(nc.vector.tensor_copy(bias_p[0][:], bias_f))
            step(nc.vector.tensor_tensor(bias_r, bias_f, bias_p[0][:], ALU.subtract))
            step(nc.vector.tensor_copy(bias_p[1][:], bias_r))
            step(nc.vector.tensor_tensor(bias_a, bias_r, bias_p[1][:], ALU.subtract))
            step(nc.vector.tensor_copy(bias_p[2][:], bias_a))
            step(nc.vector.tensor_scalar(bias_b, bias_p[0][:], id_s[0:3, 0:1], None, ALU.mult))
            step(nc.vector.scalar_tensor_tensor(bias_r, bias_p[1][:], id_s[0:3, 1:2], bias_b, ALU.mult, ALU.add))
            step(nc.vector.scalar_tensor_tensor(bias3[:], bias_p[2][:], id_s[0:3, 2:3], bias_r, ALU.mult, ALU.add))

            def stats(g, p, st, st_sem, mv, mv_sem, seen, per_group):
                need(dve, mv_sem, GT * g)
                settle(dve)
                for k in range(GT):
                    nc.vector.bn_stats(st[:, k, :], X[:, bass.ds(GT * g + k, 1), :].rearrange("p a b -> p (a b)")
                                       ).then_inc(st_sem, 1)
                dve.wait_ge(st_sem, GT * g + GT)
                need(dve, seen, per_group * (g - 1))
                settle(dve)
                for k in range(GT):
                    nc.vector.bn_aggr(mv[p][:, k, :], st[:, k, :]).then_inc(mv_sem, 1)

            def norm(g, p, mv, rs, dst, dst_sem):
                for k in range(GT):
                    nc.vector.tensor_scalar(dst(k), X[:, bass.ds(GT * g + k, 1), :].rearrange("p a b -> p (a b)"),
                                            mv[p][:, k, 0:1], rs[p][:, k:k + 1], ALU.subtract, ALU.mult
                                            ).then_inc(dst_sem, 1)

            def times_q(g, p, r, k):
                t = GT * g + k
                need(dve, b_red, t)
                for c, (lo, hi) in enumerate(HEADS):
                    n_h = hi - lo
                    dve.wait_ge(b_run, 3 * t + c + 1)
                    qq = qk[p][:, k, lo * D:hi * D].rearrange("p (h d) -> p h d", h=n_h)
                    nc.vector.tensor_tensor(
                        R[:, lo:hi], bank[2 + c][:, 0:n_h * D1 * D].rearrange("p (h e d) -> p h e d", h=n_h, e=D1),
                        qq.unsqueeze(2).broadcast_to([P, n_h, D1, D]), ALU.mult).then_inc(b_mul, 1)
                dve.wait_ge(b_mul, 3 * t + 3)
                if k == 0:
                    need(dve, c_on, g - 1)
                nc.vector.tensor_reduce(nd[p][:, k], R[:], AX.X, ALU.add).then_inc(b_red, 1)

            def features(g, p, r, k):
                t = GT * g + k
                dve.wait_ge(a_pev, 3 * t + 2)
                need(dve, a_outer, t - 2 * GT + 1)
                need(dve, b_mul, 3 * (t - 2 * GT) + 3)
                nc.vector.scalar_tensor_tensor(qk[p][:, k, :], ex[k % 2][:], 1.0, rl[k % 2][:], ALU.min, ALU.add
                                               ).then_inc(a_f, 1)

            def slot(n, i):
                a0, a1, b, c = (stage(n, i, s) for s in (2, 1, 0, -1))
                if b:
                    times_q(*b, 0)
                if c:
                    g, p, r = c
                    dve.wait_ge(b_red, GT * g + GT)
                    need(dve, c_on, g)
                    nc.vector.tensor_scalar(den[:], nd[p][:, :, :, D].rearrange("p t h -> p (t h)"), ATT_EPS, None, ALU.add
                                            ).then_inc(c_den, 1)
                    dve.wait_ge(c_den, 2 * g + 1)
                    nc.vector.reciprocal(rden[:], den[:]).then_inc(c_den, 1)
                    dve.wait_ge(c_den, 2 * g + 2)
                    need(dve, c_tr, g)
                    nc.vector.tensor_tensor(
                        on[:].rearrange("p t (h d) -> p (t h) d", h=H), nd[p][:, :, :, 0:D].rearrange("p t h d -> p (t h) d"),
                        rden[:].unsqueeze(2).broadcast_to([P, GT * H, D]), ALU.mult).then_inc(c_on, 1)
                if b:
                    times_q(*b, 1)
                if a1:
                    features(*a1, 0)
                if a0:
                    g, p, r = a0
                    dve.wait_ge(x_in[p], 16 * r + 16)
                    stats(g, p, st_a, a_st, mv_a, a_mv, a_nb, 1)
                if a1:
                    features(*a1, 1)
                if b:
                    times_q(*b, 2)
                if c:
                    g, p, r = c
                    dve.wait_ge(c_y, g + 1)
                    dve.wait_ge(a_xh, GT * g + GT)
                    xg = X[:, bass.ds(GT * g, GT), :]
                    nc.vector.tensor_tensor(xg, xg, bank[6][:].rearrange("p (t e) -> p t e", t=GT), ALU.add
                                            ).then_inc(c_x1, 1)
                    dve.wait_ge(c_x1, c[0] + 1)
                    stats(c[0], c[1], st_c, c_st, mv_c, c_mv, c_nb, 1)
                if a1:
                    features(*a1, 2)
                if b:
                    times_q(*b, 3)
                if a1:
                    features(*a1, 3)

            slots(dve, slot)

            dve.wait_ge(pads_made, 2)
            nc.vector.tensor_copy(pads[:, :, E:E + 1], pad_dest.unsqueeze(2)).then_inc(pads_made, 1)

            n = 0

            def mean_step(ins, wait=True):
                nonlocal n
                n += 1
                ins.then_inc(mean_ch, 1)
                if wait:
                    dve.wait_ge(mean_ch, n)

            dve.wait_ge(diag_in, 16)
            mean_step(nc.vector.tensor_reduce(mean_all[:], diag.rearrange("p t l -> p l t"), AX.X, ALU.add))
            mean_step(nc.vector.tensor_scalar(mean[:], mean_all[:], 1.0 / E, None, ALU.mult))
            assert n == MEAN_READY
            dve.wait_ge(mean_mm, 1)
            mean_step(nc.vector.tensor_scalar(mean_all[:], bank[0][:, 0:L], 1.0 / B, None, ALU.mult))
            mean_step(nc.vector.max(top8[:], mean_all[:]))
            mean_step(nc.vector.max_index(top_at[:], top8[:], mean_all[:]))
            mean_step(nc.vector.tensor_copy(top_f[:], top_at[:]))
            mean_step(nc.vector.tensor_scalar(kept[0][:], iota_s[:, 0:L], top_f[:, 0:1], None, ALU.is_equal))
            for k in range(1, LAGS):
                mean_step(nc.vector.scalar_tensor_tensor(kept[k % 2][:], iota_s[:, 0:L], top_f[:, k:k + 1],
                                                         kept[(k - 1) % 2][:], ALU.is_equal, ALU.add))
            keep = kept[(LAGS - 1) % 2]
            mean_step(nc.vector.tensor_scalar(away[:], keep[:], 1.0, 1e30, ALU.subtract, ALU.mult))
            mean_step(nc.vector.tensor_tensor(masked[:], mean[:], keep[:], ALU.mult))
            mean_step(nc.vector.tensor_tensor(scores[:], masked[:], away[:], ALU.add))
            mean_step(nc.vector.tensor_reduce(neg_max[:], scores[:], AX.X, ALU.max, negate=True))
            assert n == MEAN_EXP
            dve.wait_ge(prob_e, 1)
            mean_step(nc.vector.tensor_reduce(prob_sum[:], prob[:], AX.X, ALU.add))
            mean_step(nc.vector.reciprocal(prob_r[:], prob_sum[:]))
            falling = bass.AP(prob[:].tensor, L - 1, [[L, P], [0, 2], [-1, L - 1]])
            mean_step(nc.vector.tensor_scalar(prob2[:, :, 1:L], falling, prob_r[:, 0:1], None, ALU.mult), False)
            mean_step(nc.vector.tensor_scalar(prob2[:, :, 0:1], prob[:, 0:1].unsqueeze(1).broadcast_to([P, 2, 1]),
                                              prob_r[:, 0:1], None, ALU.mult), False)
            assert n == MEAN_STEPS

            def slots_of_rows(g, p, r):
                dve.wait_ge(s_cnt, g + 1)
                need(dve, s_mine, g)
                nc.vector.tensor_tensor(pos[:], bank[5][:, 0:GT * NE].rearrange("p (t e) -> p t e", t=GT),
                                        used[p][:].unsqueeze(1).broadcast_to([P, GT, NE]), ALU.add).then_inc(s_pos, 1)
                nc.vector.tensor_tensor(used[1 - p][:], used[p][:], bank[5][:, GT * NE:(GT + 1) * NE], ALU.add
                                        ).then_inc(s_used, 1)
                dve.wait_ge(s_exp, g + 1)
                nc.vector.tensor_scalar(gap_s[:], gap_e[:], 1.0, None, ALU.add).then_inc(s_go, 1)
                dve.wait_ge(s_pos, g + 1)
                nc.vector.tensor_tensor(mine[:], hot[:], pos[:].unsqueeze(2).broadcast_to([P, GT, TOPK, NE]), ALU.mult
                                        ).then_inc(s_mine, 1)
                dve.wait_ge(s_go, g + 1)
                need(dve, xs_out[p], 16 * TOPK * GT * r)
                nc.vector.reciprocal(xs[p][:, :, 0, E + 1], gap_s[:]).then_inc(s_gate, 1)
                dve.wait_ge(s_mine, g + 1)
                nc.vector.tensor_reduce(slot_f[:], mine[:], AX.X, ALU.add).then_inc(s_slot, 1)
                dve.wait_ge(s_gate, 2 * g + 1)
                nc.vector.tensor_tensor(xs[p][:, :, 1, E + 1], gap_e[:], xs[p][:, :, 0, E + 1], ALU.mult).then_inc(s_gate, 1)
                dve.wait_ge(s_slot, g + 1)
                nc.vector.tensor_copy(slot_u[p][:], slot_f[:].rearrange("p t c -> p (t c)")).then_inc(s_ready, 1)

            def best_experts(g, p, r):
                dve.wait_ge(f_sc, g + 1)
                need(dve, s_gap, g)
                settle(dve)
                for k in range(GT):
                    nc.vector.max(best[:, k, :], bank[4][:, k * NE:(k + 1) * NE]).then_inc(f_max, 1)
                dve.wait_ge(f_max, GT * g + GT)
                need(dve, f_top, g)
                settle(dve)
                for k in range(GT):
                    nc.vector.max_index(best_at[:, k, :], best[:, k, :], bank[4][:, k * NE:(k + 1) * NE]).then_inc(f_at, 1)
                need(dve, s_exp, g)
                nc.vector.tensor_tensor(gap[:], best[:, :, 1], best[:, :, 0], ALU.subtract).then_inc(s_gap, 1)
                dve.wait_ge(f_at, GT * g + GT)
                need(dve, s_hot, g)
                nc.vector.tensor_copy(top_e[:], best_at[:, :, 0:TOPK]).then_inc(f_top, 1)
                dve.wait_ge(f_top, g + 1)
                need(dve, s_mine, g)
                nc.vector.tensor_tensor(
                    hot[:], iota_s[:, 0:NE].unsqueeze(1).unsqueeze(1).broadcast_to([P, GT, TOPK, NE]),
                    top_e[:].unsqueeze(3).broadcast_to([P, GT, TOPK, NE]), ALU.is_equal).then_inc(s_hot, 1)
                dve.wait_ge(s_hot, g + 1)
                need(dve, s_cnt, g)
                nc.vector.tensor_tensor(picked[:, 0:GT, :], hot[:, :, 0, :], hot[:, :, 1, :], ALU.add).then_inc(s_pick, 1)

            def cross_slot(n, i):
                e, f, s = (stage(n, i, k) for k in (0, -1, -3))
                if s:
                    best_experts(*s)
                if e:
                    g, p, r = e
                    dve.wait_ge(e_y, g + 1)
                    xx = X[:, dyn(GT * g, GT), :]
                    nc.vector.tensor_tensor(xx, xx, bank[2][:].rearrange("p (t e) -> p t e", t=GT), ALU.add).then_inc(e_x2, 1)
                    dve.wait_ge(e_x2, g + 1)
                    stats(g, p, st_e, e_st, mv_e, e_mv, f_xr, GT)
                    dve.wait_ge(e_mv, GT * g + GT)
                    need(dve, e_rs, g - 1)
                    need(dve, e_vr, g - 1)
                    nc.vector.tensor_scalar(vv_e[p][:, 0:GT], mv_e[p][:, :, 1], 1.0 + RMS_EPS, LN_EPS * RMS_EPS, ALU.mult, ALU.add
                                            ).then_inc(e_ve, 1)
                    nc.vector.tensor_scalar(vv_e[p][:, GT:2 * GT], mv_e[p][:, :, 1], 1.0, LN_EPS, ALU.mult, ALU.add
                                            ).then_inc(e_ve, 1)
                if s:
                    slots_of_rows(*s)
                if f:
                    g, p, r = f
                    dve.wait_ge(e_rs, g + 1)
                    need(dve, f_tr, g - 1)
                    need(dve, f_x3, GT * (g - 1))
                    need(dve, f_copy, 3 * (g - 1))
                    norm(g, p, mv_e, rs_e, lambda k: xr[p][:, k, :], f_xr)
                    nc.vector.tensor_tensor(vr_e[:], vv_e[p][:, 0:GT], rs_e[p][:, 0:GT], ALU.mult).then_inc(e_vr, 1)
                    dve.wait_ge(e_vr, g + 1)
                    need(dve, f_x3, GT * g)
                    nc.vector.tensor_tensor(ms_e[:], vr_e[:], rs_e[p][:, GT:2 * GT], ALU.mult).then_inc(e_ms, 1)
                    dve.wait_ge(f_xr, GT * g + GT)
                    dve.wait_ge(e_ms, g + 1)
                    for k in range(GT):
                        xk = X[:, dyn(GT * g + k, 1), :].rearrange("p a e -> p (a e)")
                        nc.vector.scalar_tensor_tensor(xk, xr[p][:, k, :], ms_e[:, k:k + 1], xk, ALU.mult, ALU.add
                                                       ).then_inc(f_x3, 1)

            dve.wait_ge(w_in, N_W + 32)
            nc.vector.tensor_scalar(w_up_s, w_up_s, scale_s[:, 0:1], None, ALU.mult).then_inc(setup, 1)
            nc.vector.tensor_scalar(wr_s[:], wr_s[:], scale_s[:, 0:1], None, ALU.mult).then_inc(setup, 1)
            nc.vector.tensor_copy(stri_b[:], stri_s[:]).then_inc(setup, 1)
            nc.vector.tensor_copy(ones_b[:], ones_f[:]).then_inc(setup, 1)
            nc.vector.tensor_copy(used[0][:], region_0).then_inc(s_used, 1)
            dve.wait_ge(s_used, 1)
            cross_slots(dve, cross_slot)

            n = 0

            def r_step(ins, wait=True):
                nonlocal n
                n += 1
                ins.then_inc(r_ch, 1)
                if wait:
                    dve.wait_ge(r_ch, n)

            dve.wait_ge(s_used, NG + 1)
            end = used[NG % 2]
            r_step(nc.vector.tensor_copy(used_i[:], end[:]), False)
            r_step(nc.vector.tensor_tensor(pad_d[:], end[:], pad_0, ALU.subtract), False)
            r_step(nc.vector.tensor_tensor(cnt_f[:], end[:], region_0, ALU.subtract))
            r_step(nc.vector.tensor_scalar(in_i[:], used_i[:], P - 1, None, ALU.bitwise_and))
            r_step(nc.vector.tensor_copy(in_f[:], in_i[:]))
            r_step(nc.vector.tensor_scalar(fits[:], in_f[:], iota_s[:, 159:160], float(P), ALU.add, ALU.is_lt))
            r_step(nc.vector.scalar_tensor_tensor(open_f[:], in_f[:], 0.0, fits[:], ALU.is_gt, ALU.mult))
            r_step(nc.vector.tensor_tensor(pad_m[:], pad_d[:], open_f[:], ALU.mult))
            r_step(nc.vector.tensor_tensor(pad_f[:], pad_m[:], pad_row, ALU.add))
            nc.vector.tensor_copy(pad_u[:], pad_f[:]).then_inc(pad_at, 1)
            r_step(nc.vector.tensor_scalar(cnt_f[:], cnt_f[:], float(P - 1), None, ALU.add))
            r_step(nc.vector.tensor_copy(cnt_i[:], cnt_f[:]))
            r_step(nc.vector.tensor_scalar(cnt_s[:], cnt_i[:], 7, None, ALU.arith_shift_right))
            r_step(nc.vector.tensor_copy(cnt_c[:], cnt_s[:]))
            r_step(nc.vector.tensor_scalar(skip[:], cnt_c[:], -float(P), float(T), ALU.mult, ALU.add), False)
            r_step(nc.vector.tensor_tensor_scan(end_t[:], ones_f[:, 0:NE], cnt_c[:], 0.0, ALU.mult, ALU.add))
            r_step(nc.vector.tensor_scalar(of_tile[0][:], iota_s[:, 0:XT], end_t[:, 0:1], None, ALU.is_ge), False)
            r_step(nc.vector.tensor_scalar(row_f[1][:], iota_s[:, 0:XT], float(P), None, ALU.mult))
            for e in range(NE):
                if 0 < e < NE - 1:
                    r_step(nc.vector.scalar_tensor_tensor(of_tile[e % 2][:], iota_s[:, 0:XT], end_t[:, e:e + 1],
                                                          of_tile[(e - 1) % 2][:], ALU.is_ge, ALU.add), False)
                r_step(nc.vector.tensor_scalar(jump[:], iota_s[:, 0:XT], end_t[:, e:e + 1], skip[:, e:e + 1],
                                               ALU.is_ge, ALU.mult))
                r_step(nc.vector.tensor_tensor(row_f[e % 2][:], row_f[(e + 1) % 2][:], jump[:], ALU.add))
            r_step(nc.vector.tensor_scalar(off_f[:], of_tile[(NE - 2) % 2][:], float(W_E), None, ALU.mult))
            r_step(nc.vector.tensor_copy(off_i[:], off_f[:]), False)
            r_step(nc.vector.tensor_copy(row_i[:], row_f[(NE - 1) % 2][:]))
            nc.vector.engine_nop().then_inc(r_done, 1)

            def expert_slot(n, i):
                xt, up, down = (expert_stage(n, i, s) for s in (1, 1, -1))
                if up:
                    t, p = up[0], up[1] % 2
                    dve.wait_ge(x_silu, t + 1)
                    need(dve, x_ht, t - 1)
                    nc.vector.tensor_tensor(hid[p][:], bank[1 + p][:, 0:HID], silu[p][:], ALU.mult).then_inc(x_h, 1)
                if xt:
                    t, q, r = xt
                    dve.wait_ge(xg_in[q], 16 * r + 16)
                    need(dve, yg_out[q], 16 * r)
                    need(dve, x_y, t - 3)
                    nc.vector.tensor_copy(gates[q][:], xg[q][:, E + 1:E + 2]).then_inc(x_gate, 1)
                    nc.vector.tensor_copy(dest_x[q][:], xg[q][:, E:E + 1]).then_inc(x_dest, 1)
                if down:
                    t, q, r = down
                    dve.wait_ge(x_dn, t + 1)
                    need(dve, yg_out[q], 16 * r)
                    dve.wait_ge(x_gate, t + 1)
                    nc.vector.tensor_scalar(yg[q][:], bank[5][:, 0:E], gates[q][:, 0:1], None, ALU.mult).then_inc(x_y, 1)

            expert_slots(dve, expert_slot)

            def combine(i):
                for k in range(2):
                    g, p, r = grp(k, i)
                    dve.wait_ge(y_ld[p], 16 * r + 16)
                    dve.wait_ge(f_x3, NT)
                    need(dve, o_fin, g)
                    nc.vector.tensor_tensor(part[:], X[:, dyn(GT * g, GT), :], y_in[p][:, :, 0, :], ALU.add
                                            ).then_inc(o_part, 1)
                    dve.wait_ge(o_part, g + 1)
                    need(dve, o_out[p], 16 * r)
                    nc.vector.tensor_tensor(fin[p][:], part[:], y_in[p][:, :, 1, :], ALU.add).then_inc(o_fin, 1)

            pairs(dve, NG // 2, combine)

        @block.tensor
        def _(pe):
            def mm(o, l, r, start=True, stop=True):
                return nc.tensor.matmul(o, l, r, start=start, stop=stop, skip_group_check=True)

            def transposes(o, src):
                for k in range(GT):
                    last = nc.tensor.transpose(o[:, k * P:(k + 1) * P], src[:, k, :], id_s[:])
                return last

            def running_sums(g, p, r, k):
                t = GT * g + k
                pe.wait_ge(a_outer, t + 1)
                for c, (lo, hi) in enumerate(HEADS):
                    need(pe, b_mul, 3 * (t - 1) + c + 1)
                    mm(bank[2 + c][:, 0:(hi - lo) * D1 * D], tri_s[:], outer[k][:, lo:hi].rearrange("p h e d -> p (h e d)")
                       ).then_inc(b_run, 1)

            def project(g, p, r, k):
                t = GT * g + k
                if k == 0:
                    pe.wait_ge(a_xT, g + 1)
                need(pe, a_pev, 3 * t)
                mm(bank[1][:, 0:3 * E], ones3[:], b_qkv, True, False)
                mm(bank[1][:, 0:3 * E], xT[:, k * P:(k + 1) * P], wqkv[:], False, True).then_inc(a_proj, 1)

            def slot(n, i):
                a1, b, c, d = (stage(n, i, s) for s in (1, 0, -1, -2))
                if b:
                    running_sums(*b, 0)
                if a1:
                    pe.wait_ge(a_xh, GT * a1[0] + GT)
                    need(pe, a_xT, a1[0])
                    transposes(bank[0], xh).then_inc(a_tr, 1)
                if d:
                    g, p, r = d
                    pe.wait_ge(ct_in[p], 16 * r + 16)
                    need(pe, d_qT, g)
                    mm(bank[7][:], wk2_s[:], ct[p][:]).then_inc(d_k, 1)
                if b:
                    running_sums(*b, 1)
                if a1:
                    project(*a1, 0)
                    project(*a1, 1)
                if c:
                    pe.wait_ge(c_on, c[0] + 1)
                    transposes(bank[5], on).then_inc(c_tr, 1)
                if b:
                    running_sums(*b, 2)
                if c:
                    g = c[0]
                    pe.wait_ge(c_oT, g + 1)
                    need(pe, d_gd, g - 1)
                    mm(bank[6][:], ones3[:], b_o, True, False)
                    for k in range(GT):
                        last = mm(bank[6][:, k * P:(k + 1) * P], oT[:, k * P:(k + 1) * P], wo_s[:], False, k == GT - 1)
                    last.then_inc(c_y, 1)
                if a1:
                    project(*a1, 2)
                if d:
                    g, p, r = d
                    pe.wait_ge(d_xh, GT * g + GT)
                    transposes(bank[5], xh2).then_inc(d_tr, 1)
                if b:
                    running_sums(*b, 3)
                if d:
                    pe.wait_ge(d_xT, d[0] + 1)
                    pe.wait_ge(d_kT, d[0] + 1)
                    mm(bank[7][:], wq2_s[:], x2T[:]).then_inc(d_q, 1)
                if a1:
                    project(*a1, 3)
                if d:
                    g = d[0]
                    pe.wait_ge(d_qT, g + 1)
                    if i is not None:
                        pe.wait_ge(c_x1, g + 2)
                    else:
                        pe.wait_ge(c_x1, min(g + 2, NG))
                    for k in range(GT):
                        for h in range(2):
                            cols = slice(k * P + h * L, k * P + h * L + L)
                            last = mm(bank[6][h * L:h * L + L, k * L:(k + 1) * L], k2T[:, cols], q2T[:, cols])
                    last.then_inc(d_gram, 1)

            pe.wait_ge(w_in, N_W)
            pe.wait_ge(const_in, 16)
            pe.wait_ge(setup, 5)
            pe.wait_ge(bias_ch, 8)
            slots(pe, slot)

            pe.wait_ge(mean_ch, MEAN_READY)
            mm(bank[0][:, 0:L], ones_f[:], mean[:]).then_inc(mean_mm, 1)
            pe.wait_ge(mean_ch, MEAN_READY + 1)

            def cross_slot(n, i):
                v, e, f, s = (stage(n, i, k) for k in (1, 0, -2, -3))
                if e:
                    g, p, r = e
                    pe.wait_ge(e_v2, g + 1)
                    pe.wait_ge(circ_in[p], 32 * r + 32)
                    need(pe, e_aT, g)
                    for k in range(GT):
                        last = mm(bank[1][:, k * P:(k + 1) * P], v2[:, k, :], circ[p][:, k, :])
                    last.then_inc(e_agg, 1)
                if v:
                    g, p, r = v
                    pe.wait_ge(ct_in[p], 16 * (NG // 2 + 1) + 16 * r)
                    need(pe, e_v2, g)
                    mm(bank[0][:], ones3[:], b_v2, True, False)
                    for k in range(GT):
                        last = mm(bank[0][:, k * P:(k + 1) * P], ct[p][:, k * P:(k + 1) * P], wv2_s[:], False, k == GT - 1)
                    last.then_inc(e_v, 1)
                if f:
                    g, p, r = f
                    pe.wait_ge(f_xr, GT * g + GT)
                    need(pe, f_xT, g)
                    transposes(bank[3], xr[p]).then_inc(f_tr, 1)
                if s:
                    g, p, r = s
                    pe.wait_ge(s_pick, g + 1)
                    need(pe, s_used, g + 1)
                    mm(bank[5][:, 0:(GT + 1) * NE], stri_b[:], picked[:].rearrange("p t e -> p (t e)"), True, False)
                    for k in range(GT):
                        last = mm(bank[5][:, (k + 1) * NE:(GT + 1) * NE], ones_b[:],
                                  picked[:, k:k + 1, :].broadcast_to([P, GT - k, NE]), False, k == GT - 1)
                    last.then_inc(s_cnt, 1)
                if e:
                    g, p, r = e
                    pe.wait_ge(e_aT, g + 1)
                    need(pe, e_x2, g)
                    mm(bank[2][:], ones3[:], b_o2, True, False)
                    for k in range(GT):
                        last = mm(bank[2][:, k * P:(k + 1) * P], aT[:, k * P:(k + 1) * P], wo2_s[:], False, k == GT - 1)
                    last.then_inc(e_y, 1)
                if f:
                    g, p, r = f
                    pe.wait_ge(f_xT, g + 1)
                    need(pe, f_at, GT * g)
                    for k in range(GT):
                        last = mm(bank[4][:, k * NE:(k + 1) * NE], xrT[:, k * P:(k + 1) * P], wr_s[:])
                    last.then_inc(f_sc, 1)

            pe.wait_ge(setup, 9)
            cross_slots(pe, cross_slot)

            found = {}

            def find_weights(n, i, shift):
                tile = expert_stage(n, i, shift)
                if tile and n + shift not in found:
                    found[n + shift] = nc.tensor.value_load(off_i[0:1, dyn(tile[0], 1)], min_val=0, max_val=(NE - 1) * W_E)

            def expert_slot(n, i):
                tr, up, ht, down = (expert_stage(n, i, s) for s in (2, 1, 0, -1))
                if n % UNROLL == 0:
                    found.clear()
                if tr:
                    t, q, r = tr
                    pe.wait_ge(xg_in[q], 16 * r + 16)
                    need(pe, x_xT, t)
                    nc.tensor.transpose(bank[0][:, 0:P], xg[q][:, 0:E], id_s[:]).then_inc(x_tr, 1)
                if up:
                    t, p = up[0], up[1] % 2
                    find_weights(n, i, 1)
                    pe.wait_ge(x_xT, t + 1)
                    need(pe, x_h, t - 1)
                    mm(bank[1 + p][:], xgT[p][:], w_s[:, dyn(found[n + 1], 2 * HID)]).then_inc(x_up, 1)
                find_weights(n, i, -1)
                if n % UNROLL != UNROLL - 1:
                    find_weights(n, i, 2)
                if ht:
                    t, p = ht[0], ht[1] % 2
                    pe.wait_ge(x_h, t + 1)
                    need(pe, x_hT, t)
                    for c in range(2):
                        last = nc.tensor.transpose(bank[3][:, c * P:(c + 1) * P], hid[p][:, c * P:(c + 1) * P], id_s[:])
                    last.then_inc(x_ht, 1)
                if down:
                    t, p = down[0], down[1] % 2
                    pe.wait_ge(x_hT, t + 1)
                    need(pe, x_y, t)
                    for c in range(2):
                        last = mm(bank[5][:, 0:E], hidT[p][:, c * P:(c + 1) * P],
                                  w_s[:, 2 * HID + c * E:][:, dyn(found[n - 1], E)], c == 0, c == 1)
                    last.then_inc(x_dn, 1)

            pe.wait_ge(r_done, 1)
            expert_slots(pe, expert_slot)


N_W = 15 * 16
MEAN_READY = 2
MEAN_EXP = MEAN_READY + 4 + LAGS + 4
MEAN_STEPS = MEAN_EXP + 4

_NAMES = ("x", "ctx_t", "ctx_r", "wqkv_p", "b_all", "wo", "wq2", "wk2", "wv2", "wo2", "bq2", "bk2", "scale", "w_router",
          "w_up", "w_down", "tri", "stri", "ident", "iota", "where")


def _arrays(**v):
    import numpy as np
    f = np.ascontiguousarray
    a = {k: np.asarray(w) for k, w in v.items()}
    s, t = np.arange(P)[:, None], np.arange(P)[None, :]
    iota = np.zeros((P, 160), np.float32)
    iota[:, :159] = np.arange(159)
    iota[:, 159] = np.arange(P)
    p, e = np.arange(P)[:, None], np.arange(NE)[None, :]
    row = np.arange(NT)[None, :] * P + p
    where = np.concatenate([
        (row[:, :, None] * TOPK + np.arange(TOPK)).reshape(P, NT * TOPK),
        SPARE + e * P + p,
        PADS + e * P + p,
        PADS + e * P + 0 * p,
        e * T + 0 * p], axis=1).astype(np.float32)
    return {
        "where": where,
        "x": f(a["x"].reshape(NT, P, E).transpose(1, 0, 2)),
        "ctx_t": f(a["ctx_1024"].reshape(T, E).T),
        "ctx_r": f(a["ctx_1024"][:, ::-1].reshape(T, E).T),
        "wqkv_p": np.concatenate([a["L0_attn_wq"], a["L0_attn_wk"], a["L0_attn_wv"]], axis=1),
        "b_all": np.concatenate([a["L0_attn_bq"], a["L0_attn_bk"], a["L0_attn_bv"], a["L0_attn_bo"],
                                 a["L0_xattn_bv"], a["L0_xattn_bo"]]),
        "wo": a["L0_attn_wo"], "wq2": a["L0_xattn_Wq"], "wk2": a["L0_xattn_Wk"], "wv2": a["L0_xattn_Wv"],
        "wo2": a["L0_xattn_Wo"], "bq2": a["L0_xattn_bq"].reshape(P, 1), "bk2": a["L0_xattn_bk"].reshape(P, 1),
        "scale": a["L0_ffn_norm_scale"].reshape(P, 1), "w_router": f(a["L0_ffn_w_router"].T),
        "w_up": f(a["L0_ffn_w_up"].transpose(2, 0, 1).reshape(E, NE, 2 * HID)),
        "w_down": f(a["L0_ffn_w_down"].reshape(NE, E, 2, P).transpose(3, 0, 2, 1).reshape(P, NE, 2 * E)),
        "tri": ((s <= t) & (s // L == t // L)).astype(np.float32),
        "stri": (s < t).astype(np.float32),
        "ident": np.eye(P, dtype=np.float32),
        "iota": iota,
    }


def kernel(**inputs):
    import numpy as _np
    import concourse.bacc as _bacc
    from concourse import mybir as _mybir
    from concourse.bass_utils import run_bass_kernel_spmd as _run

    nc = _bacc.Bacc("TRN2", target_bir_lowering=False, num_devices=1)
    arrays = _arrays(**inputs)
    args = [nc.dram_tensor(f"in_{n}", arrays[n].shape, _mybir.dt.from_np(arrays[n].dtype), kind="ExternalInput").ap()
            for n in _NAMES]
    out = nc.dram_tensor("out_x", (P, NT, E), F32, kind="ExternalOutput").ap()
    build(nc, *args, out)
    r = _run(nc, [{f"in_{n}": arrays[n] for n in _NAMES}], core_ids=[0])
    got = r.results[0]["out_x"]
    return _np.ascontiguousarray(got.transpose(1, 0, 2)).reshape(B, L, E)
```

```python
from contextlib import ExitStack

import concourse.bass as bass
from concourse import mybir

F32, BF16 = mybir.dt.float32, mybir.dt.bfloat16
I32, U32 = mybir.dt.int32, mybir.dt.uint32
ALU = mybir.AluOpType
ACT = mybir.ActivationFunctionType
AX = mybir.AxisListType

P = 128
B, L, E, H = 128, 64, 128, 16
D = E // H
D1 = D + 1
T = B * L
NT = T // P
GT = 4
NG = NT // GT
GW = GT * P
NE, HID, TOPK = 8, 256, 2
LAGS = 5
XT = T * TOPK // P + NE
UNROLL = 8
PACK = 5
W_E = 2 * HID + 2 * E
ROW = E + 2
REGION = T + P
PADS = NE * REGION
SPARE = T * TOPK
LN_EPS, ATT_EPS, RMS_EPS = 1e-5, 1e-6, 1e-6
DIAG_PARTS = [(0, 8), (8, 14), (14, 16)]
HEADS = [(0, 6), (6, 11), (11, 16)]


def need(eng, sem, count):
    if not (isinstance(count, int) and count <= 0):
        eng.wait_ge(sem, count)


def bcast_rows(ap, rows, width):
    return bass.AP(ap.tensor, 0, [[0, rows], [1, width]])


def build(nc, x, ctx_t, ctx_r, wqkv_p, b_all, wo, wq2, wk2, wv2, wo2, bq2, bk2, scale, w_router, w_up, w_down,
          tri, stri, ident, iota, where, out):
    with ExitStack() as ctx:
        def sb(name, shape, dt=F32):
            return ctx.enter_context(nc.sbuf_tensor(name, shape, dt))

        def sem(name):
            return ctx.enter_context(nc.semaphore(name))

        def sems(name, n):
            return [sem(f"{name}{i}") for i in range(n)]

        gram_d = nc.dram_tensor("gram_d", (B * L * 2 * L,), F32).ap()
        prob_d = nc.dram_tensor("prob_d", (B * 2 * L,), F32).ap()
        xs_d = nc.dram_tensor("xs_d", (PADS + NE * P, ROW), F32).ap()
        y_d = nc.dram_tensor("y_d", (SPARE + NE * P, E), F32).ap()

        wqkv = sb("wqkv", [P, 3 * E])
        wo_s, wq2_s, wk2_s, wv2_s, wo2_s = (sb(n, [P, E]) for n in ("wo_s", "wq2_s", "wk2_s", "wv2_s", "wo2_s"))
        bq2_s, bk2_s, scale_s = sb("bq2_s", [P, 1]), sb("bk2_s", [P, 1]), sb("scale_s", [P, 1])
        wr_s = sb("wr_s", [P, NE])
        w_s = sb("w_s", [P, NE * W_E])
        diag = w_s[:, 0:L * L].rearrange("p (t l) -> p t l", t=L)
        w_up_s = w_s[:].rearrange("p (e w) -> p e w", e=NE)[:, :, 0:2 * HID]
        w_down_s = w_s[:].rearrange("p (e w) -> p e w", e=NE)[:, :, 2 * HID:W_E]
        tri_s, stri_s, id_s = sb("tri_s", [P, P]), sb("stri_s", [P, P]), sb("id_s", [P, P])
        iota_s = sb("iota_s", [P, 160])
        where_s = sb("where_s", [P, NT * TOPK + 2 * NE])
        dest_s = where_s[:, 0:NT * TOPK].rearrange("p (t c) -> p t c", c=TOPK)
        pad_dest, region_0 = (where_s[:, NT * TOPK + j * NE:NT * TOPK + (j + 1) * NE] for j in range(2))
        ones_f = sb("ones_f", [P, P])
        stri_b, ones_b = sb("stri_b", [P, P], BF16), sb("ones_b", [P, P], BF16)
        ones3 = sb("ones3", [3, P], BF16)
        NBIAS = 6 * E
        bias_p = [sb(f"bias_p{i}", [3, NBIAS], BF16) for i in range(3)]
        bias3 = sb("bias3", [3, NBIAS], BF16)
        power = sb("power", [P, GT])

        X = sb("X", [P, NT, E])

        st_a, mv_a = sb("st_a", [P, GT, 6]), [sb(f"mv_a{i}", [P, GT, 2]) for i in range(2)]
        ve_a, rs_a = sb("ve_a", [P, GT]), [sb(f"rs_a{i}", [P, GT]) for i in range(2)]
        mr_a, nb_a = sb("mr_a", [P, GT]), [sb(f"nb_a{i}", [P, GT]) for i in range(2)]
        xh = sb("xh", [P, GT, E])
        xT = sb("xT", [P, GW])
        ex, rl = [sb(f"ex{i}", [P, 2 * E]) for i in range(2)], [sb(f"rl{i}", [P, 2 * E]) for i in range(2)]
        v9 = [sb(f"v9_{i}", [P, H, D1]) for i in range(2)]
        qk = [sb(f"qk{i}", [P, GT, 2 * E]) for i in range(2)]
        shared = sb("shared", [P, GT * H * D1 * D])
        bias_f, bias_r, bias_a, bias_b = (shared[0:3, i * NBIAS:(i + 1) * NBIAS] for i in range(4))
        outer = [shared[:, i * H * D1 * D:(i + 1) * H * D1 * D].rearrange("p (h e d) -> p h e d", h=H, e=D1)
                 for i in range(GT)]
        y_in = [shared[:, i * TOPK * GW:(i + 1) * TOPK * GW].rearrange("p (t c e) -> p t c e", c=TOPK, t=GT)
                for i in range(4)]
        R = sb("R", [P, H, D1, D])
        nd = [sb(f"nd{i}", [P, GT, H, D1]) for i in range(2)]
        den, rden = sb("den", [P, GT * H]), sb("rden", [P, GT * H])
        on = sb("on", [P, GT, E])
        oT = sb("oT", [P, GW])
        st_c, mv_c = sb("st_c", [P, GT, 6]), [sb(f"mv_c{i}", [P, GT, 2]) for i in range(2)]
        ve_c, rs_c = sb("ve_c", [P, GT]), [sb(f"rs_c{i}", [P, GT]) for i in range(2)]
        mr_c, nb_c = sb("mr_c", [P, GT]), [sb(f"nb_c{i}", [P, GT]) for i in range(2)]
        xh2 = sb("xh2", [P, GT, E])
        x2T, q2T, k2T = sb("x2T", [P, GW]), sb("q2T", [P, GW]), sb("k2T", [P, GW])
        ct = [sb(f"ct{i}", [P, GW]) for i in range(2)]
        gd = [sb(f"gd{i}", [P, GT, 2, L]) for i in range(2)]

        mean, mean_all = sb("mean", [P, L]), sb("mean_all", [P, L])
        top8, top_at, top_f = sb("top8", [P, 8]), sb("top_at", [P, 8], U32), sb("top_f", [P, 8])
        kept = [sb(f"kept{i}", [P, L]) for i in range(2)]
        away, masked, scores = sb("away", [P, L]), sb("masked", [P, L]), sb("scores", [P, L])
        neg_max, prob, prob_sum, prob_r = sb("neg_max", [P, 1]), sb("prob", [P, L]), sb("prob_sum", [P, 1]), sb("prob_r", [P, 1])
        prob2 = sb("prob2", [P, 2, L])
        circ = [sb(f"circ{i}", [P, GT, P]) for i in range(2)]
        v2, aT = sb("v2", [P, GT, E]), sb("aT", [P, GW])
        st_e, mv_e = sb("st_e", [P, GT, 6]), [sb(f"mv_e{i}", [P, GT, 2]) for i in range(2)]
        vv_e = [sb(f"vv_e{i}", [P, 2 * GT]) for i in range(2)]
        rs_e = [sb(f"rs_e{i}", [P, 2 * GT]) for i in range(2)]
        vr_e = sb("vr_e", [P, GT])
        root_i = [sb(f"root_i{i}", [P, 2 * GT], I32) for i in range(2)]
        root = [sb(f"root{i}", [P, 2 * GT]) for i in range(2)]
        root_a, root_b = sb("root_a", [P, 2 * GT]), sb("root_b", [P, 2 * GT])
        nb_e = [sb(f"nb_e{i}", [P, GT]) for i in range(2)]
        ms_e = [sb(f"ms_e{i}", [P, GT]) for i in range(2)]
        xr = [sb(f"xr{i}", [P, GT, E]) for i in range(2)]
        xs = [sb(f"xs{i}", [P, GT, TOPK, ROW]) for i in range(2)]
        xrT = sb("xrT", [P, GW])
        best, best_at = sb("best", [P, GT, 8]), sb("best_at", [P, GT, 8], U32)

        top_e = sb("top_e", [P, GT, TOPK])
        hot, mine = sb("hot", [P, GT, TOPK, NE]), sb("mine", [P, GT, TOPK, NE])
        picked = sb("picked", [P, GT + 1, NE], BF16)
        gap, gap_e, gap_s = sb("gap", [P, GT]), sb("gap_e", [P, GT]), sb("gap_s", [P, GT])
        used = [sb(f"used{i}", [P, NE]) for i in range(2)]
        pos, slot_f = sb("pos", [P, GT, NE]), sb("slot_f", [P, GT, TOPK])
        slot_u = [sb(f"slot_u{i}", [P, GT * TOPK], U32) for i in range(2)]
        pads = sb("pads", [P, NE, ROW])
        used_i = sb("used_i", [P, NE], I32)
        cnt_f, cnt_c, end_t, skip = (sb(n, [P, NE]) for n in ("cnt_f", "cnt_c", "end_t", "skip"))
        cnt_i, cnt_s = sb("cnt_i", [P, NE], I32), sb("cnt_s", [P, NE], I32)
        of_tile = [sb(f"of_tile{i}", [P, XT]) for i in range(2)]
        jump, row_f = sb("jump", [P, XT]), [sb(f"row_f{i}", [P, XT]) for i in range(2)]
        e_pad = sb("e_pad", [P, XT + PACK + 1])
        pack = [sb(f"pack{i}", [P, XT + 1]) for i in range(2)]
        pack_i = sb("pack_i", [P, XT + 1], I32)
        row_i = sb("row_i", [P, XT], I32)

        dest_x = [sb(f"dest_x{i}", [P, 1], U32) for i in range(4)]
        xg, xgT = [sb(f"xg{i}", [P, ROW]) for i in range(4)], [sb(f"xgT{i}", [P, P]) for i in range(2)]
        silu, hid = [sb(f"silu{i}", [P, HID]) for i in range(2)], [sb(f"hid{i}", [P, HID]) for i in range(2)]
        hidT, yg = [sb(f"hidT{i}", [P, HID]) for i in range(2)], [sb(f"yg{i}", [P, E]) for i in range(4)]
        gates = [sb(f"gates{i}", [P, 1]) for i in range(4)]
        bank = [ctx.enter_context(nc.psum_tensor(f"bank{i}", [P, 512], F32)) for i in range(8)]

        settled = sem("settled")
        const_in = sem("const_in")
        w_in = sem("w_in")
        bias_ch = sem("bias_ch")
        setup = sem("setup")
        x_in = sems("x_in", 2)
        ct_in = sems("ct_in", 2)
        a_st, a_mv, a_ve, a_rs, a_xh = sem("a_st"), sem("a_mv"), sem("a_ve"), sem("a_rs"), sem("a_xh")
        a_ex = sem("a_ex")
        a_mr, a_nb, c_mr, c_nb = sem("a_mr"), sem("a_nb"), sem("c_mr"), sem("c_nb")
        a_tr, a_xT, a_proj, a_pev, a_f, a_outer = (sem(n) for n in ("a_tr", "a_xT", "a_proj", "a_pev", "a_f", "a_outer"))
        b_run, b_mul, b_red = sem("b_run"), sem("b_mul"), sem("b_red")
        c_den, c_on, c_tr, c_oT, c_y, c_x1, c_st, c_mv, c_ve, c_rs = (
            sem(n) for n in ("c_den", "c_on", "c_tr", "c_oT", "c_y", "c_x1", "c_st", "c_mv", "c_ve", "c_rs"))
        d_xh, d_tr, d_xT, d_k, d_kT, d_q, d_qT, d_gram, d_gd = (
            sem(n) for n in ("d_xh", "d_tr", "d_xT", "d_k", "d_kT", "d_q", "d_qT", "d_gram", "d_gd"))
        gram_out = sems("gram_out", 2)
        diag_in, mean_ch, mean_mm, prob_e = sem("diag_in"), sem("mean_ch"), sem("mean_mm"), sem("prob_e")
        prob_out, circ_0, circ_in = sem("prob_out"), sem("circ_0"), sems("circ_in", 2)
        e_v, e_v2, e_agg, e_aT, e_y, e_x2, e_st, e_mv, e_ve, e_rs = (
            sem(n) for n in ("e_v", "e_v2", "e_agg", "e_aT", "e_y", "e_x2", "e_st", "e_mv", "e_ve", "e_rs"))
        e_root, e_nb, e_vr, e_ms = sem("e_root"), sem("e_nb"), sem("e_vr"), sem("e_ms")
        f_x3 = sem("f_x3")
        f_xr, f_tr, f_xT, f_sc, f_max, f_at, f_top = (
            sem(n) for n in ("f_xr", "f_tr", "f_xT", "f_sc", "f_max", "f_at", "f_top"))
        f_copy = sem("f_copy")
        s_hot, s_pick, s_gap, s_exp, s_cnt, s_pos, s_used, s_mine, s_slot, s_go = (
            sem(n) for n in ("s_hot", "s_pick", "s_gap", "s_exp", "s_cnt", "s_pos", "s_used", "s_mine", "s_slot", "s_go"))
        s_gate, s_ready = sem("s_gate"), sem("s_ready")
        xs_out = sems("xs_out", 2)
        pads_made, pads_in, pad_at, pads_out, r_ch, r_done = (
            sem(n) for n in ("pads_made", "pads_in", "pad_at", "pads_out", "r_ch", "r_done"))
        x_dest, x_tr, x_xT, x_up, x_silu, x_h, x_ht, x_hT, x_dn, x_y = (
            sem(n) for n in ("x_dest", "x_tr", "x_xT", "x_up", "x_silu", "x_h", "x_ht", "x_hT", "x_dn", "x_y"))
        x_gate = sem("x_gate")
        xg_in, yg_out = sems("xg_in", 4), sems("yg_out", 4)
        y_ld, o_part, o_fin, o_out = sems("y_ld", 4), sem("o_part"), sem("o_fin"), sem("o_out")

        b_qkv = bias3[:, 0:3 * E]
        b_o = bias3[:, 3 * E:4 * E].unsqueeze(1).broadcast_to([3, GT, E])
        b_v2 = bias3[:, 4 * E:5 * E].unsqueeze(1).broadcast_to([3, GT, E])
        b_o2 = bias3[:, 5 * E:6 * E].unsqueeze(1).broadcast_to([3, GT, E])

        def settle(eng):
            eng.sem_inc(settled, 1)

        def grp(n, i=None):
            if i is None:
                return n, n % 2, n // 2
            return 2 * i + n, n % 2, i + n // 2

        FIRST, LAST = -2, NG + 1

        def slots(eng, slot):
            for n in range(FIRST, 4):
                slot(n, None)
            with eng.Fori(2, (NG - 2) // 2) as i:
                slot(0, i)
                slot(1, i)
            for n in range(NG - 2, LAST + 1):
                slot(n, None)

        def stage(n, i, shift):
            if i is None and not 0 <= n + shift < NG:
                return None
            return grp(n + shift, i)

        def pairs(eng, count, body):
            body(0)
            with eng.Fori(1, count) as i:
                body(i)

        def cross_slots(eng, slot):
            for n in range(-1, 6):
                slot(n, None)
            with eng.Fori(3, NG // 2 - 1) as i:
                slot(0, i)
                slot(1, i)
            for n in range(NG - 2, NG + 3):
                slot(n, None)

        def expert_stage(n, i, shift):
            if i is None:
                return (n + shift, (n + shift) % 4, (n + shift) // 4) if 0 <= n + shift < XT else None
            return UNROLL * i + n + shift, (n + shift) % 4, UNROLL // 4 * i + (n + shift) // 4

        def expert_slots(eng, slot):
            for n in range(-4, UNROLL):
                slot(n, None)
            with eng.Fori(1, XT // UNROLL - 1) as i:
                for n in range(UNROLL):
                    slot(n, i)
            for n in range(XT - UNROLL, XT + 1):
                slot(n, None)

        y_rows = y_d[0:SPARE, :].rearrange("(t p c) e -> p t (c e)", p=P, c=TOPK)
        dyn = bass.ds

        block = ctx.enter_context(nc.Block())

        @block.sync
        def _(sp):
            def x_load(i):
                for k in range(2):
                    need(sp, x_in[k], i * 16)
                    sp.dma_start(X[:, bass.ds((2 * i + k) * GT, GT), :],
                                 x[:, bass.ds((2 * i + k) * GT, GT), :]).then_inc(x_in[k], 16)

            x_load(0)
            n_w = 0
            for dst, src in ((id_s[:], ident), (bias_f, bcast_rows(b_all, 3, NBIAS)), (wqkv[:], wqkv_p)):
                sp.dma_start(dst, src).then_inc(const_in, 16)
            for dst, src in ((wo_s[:], wo), (wq2_s[:], wq2), (wk2_s[:], wk2), (wv2_s[:], wv2),
                             (wo2_s[:], wo2), (bq2_s[:], bq2), (bk2_s[:], bk2), (scale_s[:], scale),
                             (wr_s[:], w_router), (tri_s[:], tri), (stri_s[:], stri),
                             (iota_s[:], iota), (where_s[:], where)):
                sp.dma_start(dst, src).then_inc(w_in, 16)
                n_w += 16
            assert n_w == N_W
            with sp.Fori(1, NG // 2) as i:
                x_load(i)
            for k in range(2):
                sp.dma_start(ct[k][:], ctx_t[:, k * GW:(k + 1) * GW]).then_inc(ct_in[k], 16)

            def gram_store(g, p, r):
                sp.wait_ge(d_gd, g + 1)
                settle(sp)
                need(sp, gram_out[p], 16 * r)
                sp.dma_start(bass.AP(gram_d.tensor, g * (GT * P * 2 * L), [[2 * L, P], [P * 2 * L, GT], [1, 2 * L]]),
                             gd[p][:].rearrange("p t a b -> p t (a b)")).then_inc(gram_out[p], 16)

            def gram_and_context(i):
                for k in range(2):
                    g, p, r = grp(k, i)
                    gram_store(g, p, r)
                    sp.wait_ge(d_k, g + 1)
                    sp.dma_start(ct[p][:], ctx_t[:, bass.ds((g + 2) * GW, GW)]).then_inc(ct_in[p], 16)

            def diagonals(first, last):
                for k in range(2):
                    sp.wait_ge(gram_out[k], 16 * last // 2)
                a, n = first * 2 * GT, (last - first) * 2 * GT
                sp.dma_start(diag[a:a + n], bass.AP(gram_d.tensor, a * L * 2 * L, [[L * 2 * L, n], [2 * L + 1, L], [1, L]])
                             ).then_inc(diag_in, 16)

            for first, last in DIAG_PARTS[:-1]:
                if first == 0:
                    gram_and_context(0)
                with sp.Fori(max(first // 2, 1), last // 2) as i:
                    gram_and_context(i)
                diagonals(first, last)
            for g in (NG - 2, NG - 1):
                gram_store(*grp(g))
            diagonals(*DIAG_PARTS[-1])

            def ctx_load(g, p, r):
                sp.dma_start(ct[p][:], ctx_r[:, dyn(g * GW, GW)]).then_inc(ct_in[p], 16)

            def circ_load(g, p, r):
                for h in range(2):
                    src = bass.AP(prob_d.tensor, g * (GT * 2 * 2 * L) + (h * 2 * L + 1), [[1, L], [2 * 2 * L, GT], [1, L]])
                    sp.dma_start(circ[p][h * L:(h + 1) * L, :, h * L:(h + 1) * L], src).then_inc(circ_in[p], 16)

            sp.wait_ge(d_k, NG)
            for g in range(2):
                ctx_load(*grp(g))
            sp.wait_ge(pads_made, 4)
            sp.dma_start(xs_d[PADS:PADS + NE * P, :].rearrange("(e p) r -> p e r", p=P), pads[:]).then_inc(pads_in, 16)
            sp.wait_ge(mean_ch, MEAN_STEPS)
            sp.dma_start(bass.AP(prob_d.tensor, 0, [[2 * L, P], [1, 2 * L]]), prob2[:].rearrange("p a l -> p (a l)")
                         ).then_inc(prob_out, 16)
            sp.wait_ge(prob_out, 16)
            sp.wait_ge(circ_0, 2)
            for g in range(2):
                circ_load(*grp(g))

            def next_loads(i):
                for k in range(2):
                    g, p, r = grp(k, i)
                    sp.wait_ge(e_v, g + 1)
                    ctx_load(*grp(k + 2, i))
                    sp.wait_ge(e_agg, g + 1)
                    circ_load(*grp(k + 2, i))

            pairs(sp, NG // 2 - 1, next_loads)
            for dst, src in ((w_up_s, w_up), (w_down_s, w_down)):
                sp.dma_start(dst, src).then_inc(w_in, 16)

            sp.wait_ge(pad_at, 1)
            for e in range(NE):
                at = sp.value_load(used_i[0:1, e:e + 1], min_val=0, max_val=PADS - P)
                sp.dma_start(xs_d[dyn(at, P), :], pads[:, e, :]).then_inc(pads_out, 16)

            for k in range(2):
                sp.wait_ge(xs_out[k], 16 * TOPK * GT * NG // 2)
            sp.wait_ge(pads_out, 16 * NE)
            sp.wait_ge(pads_in, 16)
            sp.wait_ge(r_done, 1)

            def expert_slot(n, i):
                load = expert_stage(n, i, 4)
                if load:
                    t, q, r = load
                    at = sp.value_load(row_i[0:1, dyn(t, 1)], min_val=0, max_val=PADS + (NE - 1) * P)
                    need(sp, x_tr, t - 3)
                    need(sp, x_dest, t - 3)
                    need(sp, x_gate, t - 3)
                    sp.dma_start(xg[q][:], xs_d[dyn(at, P), :]).then_inc(xg_in[q], 16)

            expert_slots(sp, expert_slot)

            for q in range(4):
                sp.wait_ge(yg_out[q], 16 * XT // 4)

            def y_load(i):
                for q in range(4):
                    g = 4 * i + q
                    need(sp, o_fin, g - 3)
                    sp.dma_start(y_in[q].rearrange("p t c e -> p t (c e)"), y_rows[:, dyn(GT * g, GT), :]
                                 ).then_inc(y_ld[q], 16)

            pairs(sp, NG // 4, y_load)

        @block.gpsimd
        def _(pool):
            pool.memset(ones3[:], 1.0).then_inc(setup, 1)
            pool.memset(power[:], -0.5).then_inc(setup, 1)
            for k in range(2):
                pool.memset(v9[k][:], 1.0).then_inc(setup, 1)
            pool.memset(ones_f[:], 1.0).then_inc(setup, 1)
            pool.memset(pads[:], 0.0).then_inc(pads_made, 1)
            pool.memset(picked[:], 0.0).then_inc(pads_made, 1)
            pool.memset(e_pad[:], 0.0).then_inc(pads_made, 1)
            pool.wait_ge(setup, 5)

            def rstd(g, p, stats, seen, ve, ve_sem, rs, rs_sem, mr, mr_sem, nb, nb_sem, normed):
                need(pool, rs_sem, g)
                pool.wait_ge(seen, GT * g + GT)
                settle(pool)
                nc.gpsimd.tensor_scalar(ve[:], stats[p][:, :, 1], 1.0, LN_EPS, ALU.mult, ALU.add).then_inc(ve_sem, 1)
                pool.wait_ge(ve_sem, g + 1)
                need(pool, normed, GT * (g - 1))
                nc.gpsimd.tensor_tensor(rs[p][:], ve[:], power[:], ALU.pow).then_inc(rs_sem, 1)
                need(pool, nb_sem, g)
                pool.wait_ge(rs_sem, g + 1)
                nc.gpsimd.tensor_tensor(mr[:], stats[p][:, :, 0], rs[p][:], ALU.mult).then_inc(mr_sem, 1)
                pool.wait_ge(mr_sem, g + 1)
                settle(pool)
                nc.gpsimd.tensor_scalar(nb[p][:], mr[:], -1.0, None, ALU.mult).then_inc(nb_sem, 1)

            def outer_product(g, p, r, k):
                t = GT * g + k
                pool.wait_ge(a_ex, t + 1)
                need(pool, b_mul, 3 * (t - 2 * GT) + 3)
                need(pool, a_outer, t - 2 * GT + 1)
                nc.gpsimd.tensor_tensor(qk[p][:, k, :], ex[k % 2][:], rl[k % 2][:], ALU.add).then_inc(a_f, 1)
                pool.wait_ge(a_f, t + 1)
                pool.wait_ge(a_pev, 3 * t + 3)
                need(pool, b_run, 3 * (t - GT) + 3)
                kk = qk[p][:, k, E:2 * E].rearrange("p (h d) -> p h d", h=H)
                nc.gpsimd.tensor_tensor(
                    outer[k], v9[k % 2][:].unsqueeze(3).broadcast_to([P, H, D1, D]),
                    kk.unsqueeze(2).broadcast_to([P, H, D1, D]), ALU.mult).then_inc(a_outer, 1)

            def slot(n, i):
                a0, a1, c = stage(n, i, 2), stage(n, i, 1), stage(n, i, -1)
                if a1:
                    outer_product(*a1, 0)
                if a0:
                    rstd(a0[0], a0[1], mv_a, a_mv, ve_a, a_ve, rs_a, a_rs, mr_a, a_mr, nb_a, a_nb, a_xh)
                if a1:
                    outer_product(*a1, 1)
                    outer_product(*a1, 2)
                if c:
                    rstd(c[0], c[1], mv_c, c_mv, ve_c, c_ve, rs_c, c_rs, mr_c, c_mr, nb_c, c_nb, d_xh)
                if a1:
                    outer_product(*a1, 3)

            slots(pool, slot)

            for k in range(2):
                nc.gpsimd.memset(circ[k][:], 0.0).then_inc(circ_0, 1)

            def scatter_rows(g, p, r, k):
                for c in range(TOPK):
                    m = TOPK * k + c
                    nc.gpsimd.indirect_dma_start(xs_d[:, :], bass.IndirectOffsetOnAxis(ap=slot_u[p][:, m:m + 1], axis=0),
                                                 xs[p][:, k, c, :], None).then_inc(xs_out[p], 16)

            def cross_slot(n, i):
                s = stage(n, i, -3)
                if s:
                    pool.wait_ge(s_ready, s[0] + 1)
                    pool.wait_ge(s_gate, 2 * s[0] + 2)
                    pool.wait_ge(f_copy, 3 * s[0] + 3)
                    settle(pool)
                    for k in range(GT):
                        scatter_rows(*s, k)

            cross_slots(pool, cross_slot)

            def expert_slot(n, i):
                scatter = expert_stage(n, i, -1)
                if scatter:
                    t, q, r = scatter
                    pool.wait_ge(x_y, t + 1)
                    pool.wait_ge(x_dest, t + 1)
                    settle(pool)
                    nc.gpsimd.indirect_dma_start(y_d[:, :], bass.IndirectOffsetOnAxis(ap=dest_x[q][:], axis=0),
                                                 yg[q][:], None).then_inc(yg_out[q], 16)

            expert_slots(pool, expert_slot)
            for q in range(4):
                pool.wait_ge(yg_out[q], 16 * XT // 4)

        @block.scalar
        def _(act):
            def a_evac_xT(g, p, r):
                act.wait_ge(a_tr, g + 1)
                need(act, a_proj, GT * g)
                nc.scalar.activation(xT[:], bank[0][:], ACT.Copy).then_inc(a_xT, 1)

            def a_evac_proj(g, p, r, k):
                t = GT * g + k
                act.wait_ge(a_proj, t + 1)
                need(act, a_f, t - 1)
                nc.scalar.activation(ex[k % 2][:], bank[1][:, 0:2 * E], ACT.Relu, scale=-1.0).then_inc(a_pev, 1)
                nc.scalar.activation(rl[k % 2][:], bank[1][:, 0:2 * E], ACT.Relu).then_inc(a_pev, 1)
                need(act, a_outer, t - 1)
                nc.scalar.activation(v9[k % 2][:, :, 0:D], bank[1][:, 2 * E:3 * E].rearrange("p (h d) -> p h d", h=H),
                                     ACT.Copy).then_inc(a_pev, 1)
                act.wait_ge(a_pev, 3 * t + 1)
                nc.scalar.activation(ex[k % 2][:], ex[k % 2][:], ACT.Exp, scale=-1.0).then_inc(a_ex, 1)

            def norm(g, p, rs, nb, nb_sem, dst, dst_sem):
                act.wait_ge(nb_sem, g + 1)
                for k in range(GT):
                    nc.scalar.activation(dst[:, k, :], X[:, bass.ds(GT * g + k, 1), :].rearrange("p a b -> p (a b)"),
                                         ACT.Identity, bias=nb[p][:, k:k + 1], scale=rs[p][:, k:k + 1]).then_inc(dst_sem, 1)

            def slot(n, i):
                a0, a1, c, d = (stage(n, i, s) for s in (2, 1, -1, -2))
                if a1:
                    a_evac_xT(*a1)
                if d:
                    g, p, r = d
                    need(act, d_tr, g)
                    norm(g, p, rs_c, nb_c, c_nb, xh2, d_xh)
                if a1:
                    a_evac_proj(*a1, 0)
                if c:
                    act.wait_ge(c_tr, c[0] + 1)
                    need(act, c_y, c[0])
                    nc.scalar.activation(oT[:], bank[5][:], ACT.Copy).then_inc(c_oT, 1)
                if a1:
                    a_evac_proj(*a1, 1)
                if d:
                    act.wait_ge(d_k, d[0] + 1)
                    need(act, d_gram, d[0])
                    nc.scalar.activation(k2T[:], bank[7][:], ACT.Identity, bias=bk2_s[:, 0:1]).then_inc(d_kT, 1)
                    act.wait_ge(d_tr, d[0] + 1)
                    need(act, d_q, d[0])
                    nc.scalar.activation(x2T[:], bank[5][:], ACT.Copy).then_inc(d_xT, 1)
                if a1:
                    a_evac_proj(*a1, 2)
                if a0:
                    g, p, r = a0
                    need(act, a_tr, g)
                    norm(g, p, rs_a, nb_a, a_nb, xh, a_xh)
                if d:
                    act.wait_ge(d_q, d[0] + 1)
                    nc.scalar.activation(q2T[:], bank[7][:], ACT.Identity, bias=bq2_s[:, 0:1]).then_inc(d_qT, 1)
                if a1:
                    a_evac_proj(*a1, 3)
                if d:
                    g, p, r = d
                    act.wait_ge(d_gram, g + 1)
                    need(act, gram_out[p], 16 * r)
                    nc.scalar.activation(gd[p][:], bank[6][:, 0:GT * L].rearrange("p (t l) -> p t l", t=GT)
                                         .unsqueeze(2).broadcast_to([P, GT, 2, L]), ACT.Copy).then_inc(d_gd, 1)

            slots(act, slot)

            act.wait_ge(mean_ch, MEAN_EXP)
            nc.scalar.activation(prob[:], scores[:], ACT.Exp, bias=neg_max[:, 0:1]).then_inc(prob_e, 1)

            def cross_slot(n, i):
                v, e, m, f, s = (stage(n, i, k) for k in (1, 0, -1, -2, -3))
                if s:
                    g, p, r = s
                    act.wait_ge(f_xr, GT * g + GT)
                    need(act, xs_out[p], 16 * TOPK * GT * r)
                    for c in range(TOPK):
                        nc.scalar.activation(xs[p][:, :, c, 0:E], xr[p][:], ACT.Copy).then_inc(f_copy, 1)
                    nc.scalar.activation(xs[p][:, :, :, E:E + 1], dest_s[:, dyn(GT * g, GT), :].unsqueeze(3), ACT.Copy
                                         ).then_inc(f_copy, 1)
                if e:
                    g = e[0]
                    act.wait_ge(e_agg, g + 1)
                    need(act, e_y, g)
                    nc.scalar.activation(aT[:], bank[1][:], ACT.Copy).then_inc(e_aT, 1)
                if v:
                    g = v[0]
                    act.wait_ge(e_v, g + 1)
                    nc.scalar.activation(v2[:].rearrange("p t e -> p (t e)"), bank[0][:], ACT.Copy).then_inc(e_v2, 1)
                if m:
                    g, p, r = m
                    need(act, f_tr, g - 1)
                    need(act, f_x3, GT * (g - 1))
                    need(act, f_copy, 3 * (g - 1))
                    norm(g, p, rs_e, nb_e, e_nb, xr[p], f_xr)
                if s:
                    act.wait_ge(s_gap, s[0] + 1)
                    need(act, s_gate, 2 * s[0])
                    nc.scalar.activation(gap_e[:], gap[:], ACT.Exp).then_inc(s_exp, 1)
                if f:
                    g = f[0]
                    act.wait_ge(f_tr, g + 1)
                    need(act, f_sc, g)
                    nc.scalar.activation(xrT[:], bank[3][:], ACT.Copy).then_inc(f_xT, 1)

            cross_slots(act, cross_slot)

            def expert_slot(n, i):
                xt, up, ht = expert_stage(n, i, 2), expert_stage(n, i, 1), expert_stage(n, i, 0)
                if xt:
                    t, p = xt[0], xt[1] % 2
                    act.wait_ge(x_tr, t + 1)
                    need(act, x_up, t - 1)
                    nc.scalar.activation(xgT[p][:], bank[0][:, 0:P], ACT.Copy).then_inc(x_xT, 1)
                if up:
                    t, p = up[0], up[1] % 2
                    act.wait_ge(x_up, t + 1)
                    need(act, x_h, t - 1)
                    nc.scalar.activation(silu[p][:], bank[1 + p][:, HID:2 * HID], ACT.Silu).then_inc(x_silu, 1)
                if ht:
                    t, p = ht[0], ht[1] % 2
                    act.wait_ge(x_ht, t + 1)
                    need(act, x_dn, t - 1)
                    nc.scalar.activation(hidT[p][:], bank[3][:, 0:HID], ACT.Copy).then_inc(x_hT, 1)

            expert_slots(act, expert_slot)

            def store(i):
                for q in range(4):
                    g = 4 * i + q
                    act.wait_ge(o_fin, g + 1)
                    act.dma_start(out[:, dyn(GT * g, GT), :], X[:, dyn(GT * g, GT), :]).then_inc(o_out, 16)

            pairs(act, NG // 4, store)
            act.wait_ge(o_out, 16 * NG)

        @block.vector
        def _(dve):
            def split_biases():
                dve.wait_ge(const_in, 48)
                n = 0

                def step(ins):
                    nonlocal n
                    n += 1
                    ins.then_inc(bias_ch, 1)
                    dve.wait_ge(bias_ch, n)
                step(nc.vector.tensor_copy(bias_p[0][:], bias_f))
                step(nc.vector.tensor_tensor(bias_r, bias_f, bias_p[0][:], ALU.subtract))
                step(nc.vector.tensor_copy(bias_p[1][:], bias_r))
                step(nc.vector.tensor_tensor(bias_a, bias_r, bias_p[1][:], ALU.subtract))
                step(nc.vector.tensor_copy(bias_p[2][:], bias_a))
                step(nc.vector.tensor_scalar(bias_b, bias_p[0][:], id_s[0:3, 0:1], None, ALU.mult))
                step(nc.vector.scalar_tensor_tensor(bias_r, bias_p[1][:], id_s[0:3, 1:2], bias_b, ALU.mult, ALU.add))
                step(nc.vector.scalar_tensor_tensor(bias3[:], bias_p[2][:], id_s[0:3, 2:3], bias_r, ALU.mult, ALU.add))

            def stats(g, p, st, st_sem, mv, mv_sem, seen, per_group):
                need(dve, mv_sem, GT * g)
                settle(dve)
                for k in range(GT):
                    nc.vector.bn_stats(st[:, k, :], X[:, bass.ds(GT * g + k, 1), :].rearrange("p a b -> p (a b)")
                                       ).then_inc(st_sem, 1)
                dve.wait_ge(st_sem, GT * g + GT)
                need(dve, seen, per_group * (g - 1))
                settle(dve)
                for k in range(GT):
                    nc.vector.bn_aggr(mv[p][:, k, :], st[:, k, :]).then_inc(mv_sem, 1)

            def times_q(g, p, r, k):
                t = GT * g + k
                need(dve, b_red, t)
                for c, (lo, hi) in enumerate(HEADS):
                    n_h = hi - lo
                    dve.wait_ge(b_run, 3 * t + c + 1)
                    qq = qk[p][:, k, lo * D:hi * D].rearrange("p (h d) -> p h d", h=n_h)
                    nc.vector.tensor_tensor(
                        R[:, lo:hi], bank[2 + c][:, 0:n_h * D1 * D].rearrange("p (h e d) -> p h e d", h=n_h, e=D1),
                        qq.unsqueeze(2).broadcast_to([P, n_h, D1, D]), ALU.mult).then_inc(b_mul, 1)
                dve.wait_ge(b_mul, 3 * t + 3)
                if k == 0:
                    need(dve, c_on, g - 1)
                nc.vector.tensor_reduce(nd[p][:, k], R[:], AX.X, ALU.add).then_inc(b_red, 1)

            def slot(n, i):
                a0, a1, b, c = (stage(n, i, s) for s in (2, 1, 0, -1))
                if b:
                    times_q(*b, 0)
                if c:
                    g, p, r = c
                    dve.wait_ge(b_red, GT * g + GT)
                    need(dve, c_on, g)
                    nc.vector.tensor_scalar(den[:], nd[p][:, :, :, D].rearrange("p t h -> p (t h)"), ATT_EPS, None, ALU.add
                                            ).then_inc(c_den, 1)
                    dve.wait_ge(c_den, 2 * g + 1)
                    nc.vector.reciprocal(rden[:], den[:]).then_inc(c_den, 1)
                    dve.wait_ge(c_den, 2 * g + 2)
                    need(dve, c_tr, g)
                    nc.vector.tensor_tensor(
                        on[:].rearrange("p t (h d) -> p (t h) d", h=H), nd[p][:, :, :, 0:D].rearrange("p t h d -> p (t h) d"),
                        rden[:].unsqueeze(2).broadcast_to([P, GT * H, D]), ALU.mult).then_inc(c_on, 1)
                if b:
                    times_q(*b, 1)
                if a0:
                    g, p, r = a0
                    dve.wait_ge(x_in[p], 16 * r + 16)
                    stats(g, p, st_a, a_st, mv_a, a_mv, a_nb, 1)
                if i is None and n == FIRST:
                    split_biases()
                if b:
                    times_q(*b, 2)
                if c:
                    g, p, r = c
                    dve.wait_ge(c_y, g + 1)
                    dve.wait_ge(a_xh, GT * g + GT)
                    xg = X[:, bass.ds(GT * g, GT), :]
                    nc.vector.tensor_tensor(xg, xg, bank[6][:].rearrange("p (t e) -> p t e", t=GT), ALU.add
                                            ).then_inc(c_x1, 1)
                    dve.wait_ge(c_x1, c[0] + 1)
                    stats(c[0], c[1], st_c, c_st, mv_c, c_mv, c_nb, 1)
                if b:
                    times_q(*b, 3)

            slots(dve, slot)

            dve.wait_ge(w_in, N_W)
            dve.wait_ge(pads_made, 3)
            nc.vector.tensor_copy(pads[:, :, E:E + 1], pad_dest.unsqueeze(2)).then_inc(pads_made, 1)

            nc.vector.tensor_scalar(wr_s[:], wr_s[:], scale_s[:, 0:1], None, ALU.mult).then_inc(setup, 1)
            nc.vector.tensor_copy(stri_b[:], stri_s[:]).then_inc(setup, 1)
            nc.vector.tensor_copy(ones_b[:], ones_f[:]).then_inc(setup, 1)
            nc.vector.tensor_copy(used[0][:], region_0).then_inc(s_used, 1)
            dve.wait_ge(s_used, 1)

            n = 0

            def mean_step(ins, wait=True):
                nonlocal n
                n += 1
                ins.then_inc(mean_ch, 1)
                if wait:
                    dve.wait_ge(mean_ch, n)

            dve.wait_ge(diag_in, 16 * len(DIAG_PARTS))
            mean_step(nc.vector.tensor_reduce(mean_all[:], diag.rearrange("p t l -> p l t"), AX.X, ALU.add))
            mean_step(nc.vector.tensor_scalar(mean[:], mean_all[:], 1.0 / E, None, ALU.mult))
            assert n == MEAN_READY
            dve.wait_ge(mean_mm, 1)
            mean_step(nc.vector.tensor_scalar(mean_all[:], bank[0][:, 0:L], 1.0 / B, None, ALU.mult))
            mean_step(nc.vector.max(top8[:], mean_all[:]))
            mean_step(nc.vector.max_index(top_at[:], top8[:], mean_all[:]))
            mean_step(nc.vector.tensor_copy(top_f[:], top_at[:]))
            mean_step(nc.vector.tensor_scalar(kept[0][:], iota_s[:, 0:L], top_f[:, 0:1], None, ALU.is_equal))
            for k in range(1, LAGS):
                mean_step(nc.vector.scalar_tensor_tensor(kept[k % 2][:], iota_s[:, 0:L], top_f[:, k:k + 1],
                                                         kept[(k - 1) % 2][:], ALU.is_equal, ALU.add))
            keep = kept[(LAGS - 1) % 2]
            mean_step(nc.vector.tensor_scalar(away[:], keep[:], 1.0, 1e30, ALU.subtract, ALU.mult))
            mean_step(nc.vector.tensor_tensor(masked[:], mean[:], keep[:], ALU.mult))
            mean_step(nc.vector.tensor_tensor(scores[:], masked[:], away[:], ALU.add))
            mean_step(nc.vector.tensor_reduce(neg_max[:], scores[:], AX.X, ALU.max, negate=True))
            assert n == MEAN_EXP
            dve.wait_ge(prob_e, 1)
            mean_step(nc.vector.tensor_reduce(prob_sum[:], prob[:], AX.X, ALU.add))
            mean_step(nc.vector.reciprocal(prob_r[:], prob_sum[:]))
            falling = bass.AP(prob[:].tensor, L - 1, [[L, P], [0, 2], [-1, L - 1]])
            mean_step(nc.vector.tensor_scalar(prob2[:, :, 1:L], falling, prob_r[:, 0:1], None, ALU.mult), False)
            mean_step(nc.vector.tensor_scalar(prob2[:, :, 0:1], prob[:, 0:1].unsqueeze(1).broadcast_to([P, 2, 1]),
                                              prob_r[:, 0:1], None, ALU.mult), False)
            assert n == MEAN_STEPS

            def slots_of_rows(g, p, r):
                dve.wait_ge(s_cnt, g + 1)
                need(dve, s_mine, g)
                nc.vector.tensor_tensor(pos[:], bank[5][:, 0:GT * NE].rearrange("p (t e) -> p t e", t=GT),
                                        used[p][:].unsqueeze(1).broadcast_to([P, GT, NE]), ALU.add).then_inc(s_pos, 1)
                nc.vector.tensor_tensor(used[1 - p][:], used[p][:], bank[5][:, GT * NE:(GT + 1) * NE], ALU.add
                                        ).then_inc(s_used, 1)
                dve.wait_ge(s_exp, g + 1)
                nc.vector.tensor_scalar(gap_s[:], gap_e[:], 1.0, None, ALU.add).then_inc(s_go, 1)
                dve.wait_ge(s_pos, g + 1)
                nc.vector.tensor_tensor(mine[:], hot[:], pos[:].unsqueeze(2).broadcast_to([P, GT, TOPK, NE]), ALU.mult
                                        ).then_inc(s_mine, 1)
                dve.wait_ge(s_go, g + 1)
                need(dve, xs_out[p], 16 * TOPK * GT * r)
                nc.vector.reciprocal(xs[p][:, :, 0, E + 1], gap_s[:]).then_inc(s_gate, 1)
                dve.wait_ge(s_mine, g + 1)
                nc.vector.tensor_reduce(slot_f[:], mine[:], AX.X, ALU.add).then_inc(s_slot, 1)
                dve.wait_ge(s_gate, 2 * g + 1)
                nc.vector.tensor_tensor(xs[p][:, :, 1, E + 1], gap_e[:], xs[p][:, :, 0, E + 1], ALU.mult).then_inc(s_gate, 1)
                dve.wait_ge(s_slot, g + 1)
                nc.vector.tensor_copy(slot_u[p][:], slot_f[:].rearrange("p t c -> p (t c)")).then_inc(s_ready, 1)

            def add_norm(g, p, r, k):
                dve.wait_ge(f_xr, GT * g + k + 1)
                dve.wait_ge(e_ms, g + 1)
                xk = X[:, dyn(GT * g + k, 1), :].rearrange("p a e -> p (a e)")
                nc.vector.scalar_tensor_tensor(xk, xr[p][:, k, :], ms_e[p][:, k:k + 1], xk, ALU.mult, ALU.add
                                               ).then_inc(f_x3, 1)

            def inverse_roots(g, p, r, f):
                x, steps = vv_e[p][:], 0

                def step(ins, k=None):
                    nonlocal steps
                    steps += 1
                    ins.then_inc(e_root, 1)
                    if f and k is not None:
                        add_norm(*f, k)
                    dve.wait_ge(e_root, ROOT_STEPS * g + steps)

                dve.wait_ge(e_ve, 2 * g + 2)
                step(nc.vector.tensor_scalar(root_i[0][:], x.bitcast(I32), 1, None, ALU.arith_shift_right), 0)
                step(nc.vector.tensor_scalar(root_i[1][:], root_i[0][:], -1.0, float(0x5f3759df), ALU.mult, ALU.add))
                y = root_i[1][:].bitcast(F32)
                for k in range(3):
                    step(nc.vector.tensor_tensor(root_a[:], y, y, ALU.mult), k + 1)
                    step(nc.vector.scalar_tensor_tensor(root_b[:], root_a[:], -0.5, x, ALU.mult, ALU.mult))
                    if k < 2:
                        step(nc.vector.scalar_tensor_tensor(root[k][:], root_b[:], 1.5, y, ALU.add, ALU.mult))
                        y = root[k][:]
                assert steps == ROOT_STEPS
                need(dve, f_xr, GT * (g - 1))
                nc.vector.scalar_tensor_tensor(rs_e[p][:], root_b[:], 1.5, y, ALU.add, ALU.mult).then_inc(e_rs, 1)
                dve.wait_ge(e_rs, g + 1)
                nc.vector.scalar_tensor_tensor(nb_e[p][:], mv_e[p][:, :, 0], -1.0, rs_e[p][:, 0:GT], ALU.mult, ALU.mult
                                               ).then_inc(e_nb, 1)
                nc.vector.tensor_tensor(vr_e[:], vv_e[p][:, 0:GT], rs_e[p][:, 0:GT], ALU.mult).then_inc(e_vr, 1)
                dve.wait_ge(e_vr, g + 1)
                need(dve, f_x3, GT * (g - 1))
                nc.vector.tensor_tensor(ms_e[p][:], vr_e[:], rs_e[p][:, GT:2 * GT], ALU.mult).then_inc(e_ms, 1)

            def best_experts(g, p, r):
                dve.wait_ge(f_sc, g + 1)
                need(dve, s_gap, g)
                settle(dve)
                for k in range(GT):
                    nc.vector.max(best[:, k, :], bank[4][:, k * NE:(k + 1) * NE]).then_inc(f_max, 1)
                dve.wait_ge(f_max, GT * g + GT)
                need(dve, f_top, g)
                settle(dve)
                for k in range(GT):
                    nc.vector.max_index(best_at[:, k, :], best[:, k, :], bank[4][:, k * NE:(k + 1) * NE]).then_inc(f_at, 1)
                need(dve, s_exp, g)
                nc.vector.tensor_tensor(gap[:], best[:, :, 1], best[:, :, 0], ALU.subtract).then_inc(s_gap, 1)
                dve.wait_ge(f_at, GT * g + GT)
                need(dve, s_hot, g)
                nc.vector.tensor_copy(top_e[:], best_at[:, :, 0:TOPK]).then_inc(f_top, 1)
                dve.wait_ge(f_top, g + 1)
                need(dve, s_mine, g)
                nc.vector.tensor_tensor(
                    hot[:], iota_s[:, 0:NE].unsqueeze(1).unsqueeze(1).broadcast_to([P, GT, TOPK, NE]),
                    top_e[:].unsqueeze(3).broadcast_to([P, GT, TOPK, NE]), ALU.is_equal).then_inc(s_hot, 1)
                dve.wait_ge(s_hot, g + 1)
                need(dve, s_cnt, g)
                nc.vector.tensor_tensor(picked[:, 0:GT, :], hot[:, :, 0, :], hot[:, :, 1, :], ALU.add).then_inc(s_pick, 1)

            def cross_slot(n, i):
                e, f, s = (stage(n, i, k) for k in (0, -1, -3))
                if s:
                    best_experts(*s)
                if e:
                    g, p, r = e
                    dve.wait_ge(e_y, g + 1)
                    xx = X[:, dyn(GT * g, GT), :]
                    nc.vector.tensor_tensor(xx, xx, bank[2][:].rearrange("p (t e) -> p t e", t=GT), ALU.add).then_inc(e_x2, 1)
                    if s:
                        slots_of_rows(*s)
                    dve.wait_ge(e_x2, g + 1)
                    stats(g, p, st_e, e_st, mv_e, e_mv, e_nb, 1)
                    dve.wait_ge(e_mv, GT * g + GT)
                    need(dve, e_vr, g - 1)
                    nc.vector.tensor_scalar(vv_e[p][:, 0:GT], mv_e[p][:, :, 1], 1.0 + RMS_EPS, LN_EPS * RMS_EPS, ALU.mult, ALU.add
                                            ).then_inc(e_ve, 1)
                    nc.vector.tensor_scalar(vv_e[p][:, GT:2 * GT], mv_e[p][:, :, 1], 1.0, LN_EPS, ALU.mult, ALU.add
                                            ).then_inc(e_ve, 1)
                elif s:
                    slots_of_rows(*s)
                if e:
                    inverse_roots(*e, f)
                elif f:
                    for k in range(GT):
                        add_norm(*f, k)

            cross_slots(dve, cross_slot)

            n = 0

            def r_step(ins, wait=True):
                nonlocal n
                n += 1
                ins.then_inc(r_ch, 1)
                if wait:
                    dve.wait_ge(r_ch, n)

            dve.wait_ge(s_used, NG + 1)
            end = used[NG % 2]
            nc.vector.tensor_copy(used_i[:], end[:]).then_inc(pad_at, 1)
            r_step(nc.vector.tensor_tensor(cnt_f[:], end[:], region_0, ALU.subtract))
            r_step(nc.vector.tensor_scalar(cnt_f[:], cnt_f[:], float(P - 1), None, ALU.add))
            r_step(nc.vector.tensor_copy(cnt_i[:], cnt_f[:]))
            r_step(nc.vector.tensor_scalar(cnt_s[:], cnt_i[:], 7, None, ALU.arith_shift_right))
            r_step(nc.vector.tensor_copy(cnt_c[:], cnt_s[:]))
            r_step(nc.vector.tensor_scalar(skip[:], cnt_c[:], -float(P), float(REGION), ALU.mult, ALU.add), False)
            r_step(nc.vector.tensor_tensor_scan(end_t[:], ones_f[:, 0:NE], cnt_c[:], 0.0, ALU.mult, ALU.add))
            r_step(nc.vector.tensor_scalar(of_tile[0][:], iota_s[:, 0:XT], end_t[:, 0:1], None, ALU.is_ge), False)
            r_step(nc.vector.tensor_scalar(row_f[1][:], iota_s[:, 0:XT], float(P), None, ALU.mult))
            for e in range(NE):
                if 0 < e < NE - 1:
                    r_step(nc.vector.scalar_tensor_tensor(of_tile[e % 2][:], iota_s[:, 0:XT], end_t[:, e:e + 1],
                                                          of_tile[(e - 1) % 2][:], ALU.is_ge, ALU.add), False)
                r_step(nc.vector.tensor_scalar(jump[:], iota_s[:, 0:XT], end_t[:, e:e + 1], skip[:, e:e + 1],
                                               ALU.is_ge, ALU.mult))
                r_step(nc.vector.tensor_tensor(row_f[e % 2][:], row_f[(e + 1) % 2][:], jump[:], ALU.add))
            dve.wait_ge(pads_made, 4)
            r_step(nc.vector.tensor_copy(e_pad[:, 1:XT + 1], of_tile[(NE - 2) % 2][:]))
            packed = e_pad[:, PACK - 1:PACK + XT]
            for j in range(PACK - 2, -1, -1):
                r_step(nc.vector.scalar_tensor_tensor(pack[j % 2][:], packed, float(NE), e_pad[:, j:j + XT + 1], ALU.mult, ALU.add))
                packed = pack[j % 2][:]
            r_step(nc.vector.tensor_copy(pack_i[:], packed), False)
            r_step(nc.vector.tensor_copy(row_i[:], row_f[(NE - 1) % 2][:]))
            nc.vector.engine_nop().then_inc(r_done, 1)

            dve.wait_ge(w_in, N_W + 32)
            nc.vector.tensor_scalar(w_up_s, w_up_s, scale_s[:, 0:1], None, ALU.mult).then_inc(setup, 1)

            def expert_slot(n, i):
                xt, up, down = (expert_stage(n, i, s) for s in (1, 1, -1))
                if up:
                    t, p = up[0], up[1] % 2
                    dve.wait_ge(x_silu, t + 1)
                    need(dve, x_ht, t - 1)
                    nc.vector.tensor_tensor(hid[p][:], bank[1 + p][:, 0:HID], silu[p][:], ALU.mult).then_inc(x_h, 1)
                if xt:
                    t, q, r = xt
                    dve.wait_ge(xg_in[q], 16 * r + 16)
                    need(dve, yg_out[q], 16 * r)
                    need(dve, x_y, t - 3)
                    nc.vector.tensor_copy(gates[q][:], xg[q][:, E + 1:E + 2]).then_inc(x_gate, 1)
                    nc.vector.tensor_copy(dest_x[q][:], xg[q][:, E:E + 1]).then_inc(x_dest, 1)
                if down:
                    t, q, r = down
                    dve.wait_ge(x_dn, t + 1)
                    need(dve, yg_out[q], 16 * r)
                    dve.wait_ge(x_gate, t + 1)
                    nc.vector.tensor_scalar(yg[q][:], bank[5][:, 0:E], gates[q][:, 0:1], None, ALU.mult).then_inc(x_y, 1)

            expert_slots(dve, expert_slot)

            def combine(i):
                for q in range(4):
                    g = 4 * i + q
                    dve.wait_ge(y_ld[q], 16 * i + 16)
                    xg = X[:, dyn(GT * g, GT), :]
                    nc.vector.tensor_tensor(xg, xg, y_in[q][:, :, 0, :], ALU.add).then_inc(o_part, 1)
                    dve.wait_ge(o_part, g + 1)
                    nc.vector.tensor_tensor(xg, xg, y_in[q][:, :, 1, :], ALU.add).then_inc(o_fin, 1)

            dve.wait_ge(f_x3, NT)
            pairs(dve, NG // 4, combine)

        @block.tensor
        def _(pe):
            def mm(o, l, r, start=True, stop=True):
                return nc.tensor.matmul(o, l, r, start=start, stop=stop, skip_group_check=True)

            def transposes(o, src):
                for k in range(GT):
                    last = nc.tensor.transpose(o[:, k * P:(k + 1) * P], src[:, k, :], id_s[:])
                return last

            def running_sums(g, p, r, k):
                t = GT * g + k
                pe.wait_ge(a_outer, t + 1)
                for c, (lo, hi) in enumerate(HEADS):
                    need(pe, b_mul, 3 * (t - 1) + c + 1)
                    mm(bank[2 + c][:, 0:(hi - lo) * D1 * D], tri_s[:], outer[k][:, lo:hi].rearrange("p h e d -> p (h e d)")
                       ).then_inc(b_run, 1)

            def project(g, p, r, k):
                t = GT * g + k
                if k == 0:
                    pe.wait_ge(a_xT, g + 1)
                need(pe, a_pev, 3 * t)
                mm(bank[1][:, 0:3 * E], ones3[:], b_qkv, True, False)
                mm(bank[1][:, 0:3 * E], xT[:, k * P:(k + 1) * P], wqkv[:], False, True).then_inc(a_proj, 1)

            def slot(n, i):
                a1, b, c, d = (stage(n, i, s) for s in (1, 0, -1, -2))
                if a1:
                    pe.wait_ge(a_xh, GT * a1[0] + GT)
                    need(pe, a_xT, a1[0])
                    transposes(bank[0], xh).then_inc(a_tr, 1)
                if b:
                    running_sums(*b, 1)
                if d:
                    g, p, r = d
                    pe.wait_ge(ct_in[p], 16 * r + 16)
                    need(pe, d_qT, g)
                    mm(bank[7][:], wk2_s[:], ct[p][:]).then_inc(d_k, 1)
                if a1:
                    if i is None and a1[0] == 0:
                        pe.wait_ge(setup, 5)
                        pe.wait_ge(bias_ch, 8)
                    project(*a1, 0)
                    project(*a1, 1)
                if c:
                    pe.wait_ge(c_on, c[0] + 1)
                    transposes(bank[5], on).then_inc(c_tr, 1)
                if b:
                    running_sums(*b, 2)
                if c:
                    g = c[0]
                    pe.wait_ge(c_oT, g + 1)
                    need(pe, d_gd, g - 1)
                    mm(bank[6][:], ones3[:], b_o, True, False)
                    for k in range(GT):
                        last = mm(bank[6][:, k * P:(k + 1) * P], oT[:, k * P:(k + 1) * P], wo_s[:], False, k == GT - 1)
                    last.then_inc(c_y, 1)
                if a1:
                    project(*a1, 2)
                if d:
                    g, p, r = d
                    pe.wait_ge(d_xh, GT * g + GT)
                    transposes(bank[5], xh2).then_inc(d_tr, 1)
                if b:
                    running_sums(*b, 3)
                if d:
                    pe.wait_ge(d_xT, d[0] + 1)
                    pe.wait_ge(d_kT, d[0] + 1)
                    mm(bank[7][:], wq2_s[:], x2T[:]).then_inc(d_q, 1)
                if a1:
                    project(*a1, 3)
                if i is None and n == -1:
                    pe.wait_ge(w_in, N_W)
                if a1:
                    running_sums(*a1, 0)
                if d:
                    g = d[0]
                    pe.wait_ge(d_qT, g + 1)
                    if i is not None:
                        pe.wait_ge(c_x1, g + 2)
                    else:
                        pe.wait_ge(c_x1, min(g + 2, NG))
                    for k in range(GT):
                        for h in range(2):
                            cols = slice(k * P + h * L, k * P + h * L + L)
                            last = mm(bank[6][h * L:h * L + L, k * L:(k + 1) * L], k2T[:, cols], q2T[:, cols])
                    last.then_inc(d_gram, 1)

            pe.wait_ge(const_in, 48)
            slots(pe, slot)

            pe.wait_ge(mean_ch, MEAN_READY)
            mm(bank[0][:, 0:L], ones_f[:], mean[:]).then_inc(mean_mm, 1)
            pe.wait_ge(mean_ch, MEAN_READY + 1)

            def cross_slot(n, i):
                v, e, f, s = (stage(n, i, k) for k in (1, 0, -2, -3))
                if e:
                    g, p, r = e
                    pe.wait_ge(e_v2, g + 1)
                    pe.wait_ge(circ_in[p], 32 * r + 32)
                    need(pe, e_aT, g)
                    for k in range(GT):
                        last = mm(bank[1][:, k * P:(k + 1) * P], v2[:, k, :], circ[p][:, k, :])
                    last.then_inc(e_agg, 1)
                if v:
                    g, p, r = v
                    pe.wait_ge(ct_in[p], 16 * (NG // 2 + 1) + 16 * r)
                    need(pe, e_v2, g)
                    mm(bank[0][:], ones3[:], b_v2, True, False)
                    for k in range(GT):
                        last = mm(bank[0][:, k * P:(k + 1) * P], ct[p][:, k * P:(k + 1) * P], wv2_s[:], False, k == GT - 1)
                    last.then_inc(e_v, 1)
                if f:
                    g, p, r = f
                    pe.wait_ge(f_xr, GT * g + GT)
                    need(pe, f_xT, g)
                    transposes(bank[3], xr[p]).then_inc(f_tr, 1)
                if e:
                    g, p, r = e
                    pe.wait_ge(e_aT, g + 1)
                    need(pe, e_x2, g)
                    mm(bank[2][:], ones3[:], b_o2, True, False)
                    for k in range(GT):
                        last = mm(bank[2][:, k * P:(k + 1) * P], aT[:, k * P:(k + 1) * P], wo2_s[:], False, k == GT - 1)
                    last.then_inc(e_y, 1)
                if s:
                    g, p, r = s
                    pe.wait_ge(s_pick, g + 1)
                    need(pe, s_used, g + 1)
                    mm(bank[5][:, 0:(GT + 1) * NE], stri_b[:], picked[:].rearrange("p t e -> p (t e)"), True, False)
                    for k in range(GT):
                        last = mm(bank[5][:, (k + 1) * NE:(GT + 1) * NE], ones_b[:],
                                  picked[:, k:k + 1, :].broadcast_to([P, GT - k, NE]), False, k == GT - 1)
                    last.then_inc(s_cnt, 1)
                if f:
                    g, p, r = f
                    pe.wait_ge(f_xT, g + 1)
                    need(pe, f_at, GT * g)
                    for k in range(GT):
                        last = mm(bank[4][:, k * NE:(k + 1) * NE], xrT[:, k * P:(k + 1) * P], wr_s[:])
                    last.then_inc(f_sc, 1)

            pe.wait_ge(setup, 8)
            cross_slots(pe, cross_slot)

            packs = [None, None]

            def load_experts(which, n, i):
                at = n + which * PACK
                if i is not None or at <= XT:
                    at = at if i is None else UNROLL * i + at
                    packs[which] = nc.tensor.value_load(pack_i[0:1, dyn(at, 1)], min_val=0, max_val=NE ** PACK - 1)

            def weights(n, shift, first, width):
                which, k = divmod(n % UNROLL + shift + 1, PACK) if n >= 0 else divmod(n + shift + 1, PACK)
                expert = (packs[which] >> (3 * k)) & (NE - 1)
                return w_s[:, first:][:, dyn(expert * W_E, width)]

            def expert_slot(n, i):
                tr, up, ht, down = (expert_stage(n, i, s) for s in (2, 1, 0, -1))
                if tr:
                    t, q, r = tr
                    pe.wait_ge(xg_in[q], 16 * r + 16)
                    need(pe, x_xT, t)
                    nc.tensor.transpose(bank[0][:, 0:P], xg[q][:, 0:E], id_s[:]).then_inc(x_tr, 1)
                if i is None and n == -1:
                    load_experts(0, 0, i)
                elif n % UNROLL == 0 and not (i is None and n == 0):
                    load_experts(0, n, i)
                if up:
                    t, p = up[0], up[1] % 2
                    pe.wait_ge(x_xT, t + 1)
                    need(pe, x_h, t - 1)
                    mm(bank[1 + p][:], xgT[p][:], weights(n, 1, 0, 2 * HID)).then_inc(x_up, 1)
                    if n % UNROLL == 1:
                        load_experts(1, n - 1, i)
                if ht:
                    t, p = ht[0], ht[1] % 2
                    pe.wait_ge(x_h, t + 1)
                    need(pe, x_hT, t)
                    for c in range(2):
                        last = nc.tensor.transpose(bank[3][:, c * P:(c + 1) * P], hid[p][:, c * P:(c + 1) * P], id_s[:])
                    last.then_inc(x_ht, 1)
                if down:
                    t, p = down[0], down[1] % 2
                    pe.wait_ge(x_hT, t + 1)
                    need(pe, x_y, t)
                    for c in range(2):
                        last = mm(bank[5][:, 0:E], hidT[p][:, c * P:(c + 1) * P],
                                  weights(n, -1, 2 * HID + c * E, E), c == 0, c == 1)
                    last.then_inc(x_dn, 1)

            pe.wait_ge(r_done, 1)
            pe.wait_ge(setup, 9)
            expert_slots(pe, expert_slot)


ROOT_STEPS = 2 + 3 * 3 - 1
N_W = 13 * 16
MEAN_READY = 2
MEAN_EXP = MEAN_READY + 4 + LAGS + 4
MEAN_STEPS = MEAN_EXP + 4

_NAMES = ("x", "ctx_t", "ctx_r", "wqkv_p", "b_all", "wo", "wq2", "wk2", "wv2", "wo2", "bq2", "bk2", "scale", "w_router",
          "w_up", "w_down", "tri", "stri", "ident", "iota", "where")


def _arrays(**v):
    import numpy as np
    f = np.ascontiguousarray
    a = {k: np.asarray(w) for k, w in v.items()}
    s, t = np.arange(P)[:, None], np.arange(P)[None, :]
    iota = np.zeros((P, 160), np.float32)
    iota[:, :159] = np.arange(159)
    iota[:, 159] = np.arange(P)
    p, e = np.arange(P)[:, None], np.arange(NE)[None, :]
    row = np.arange(NT)[None, :] * P + p
    where = np.concatenate([
        (row[:, :, None] * TOPK + np.arange(TOPK)).reshape(P, NT * TOPK),
        SPARE + e * P + p,
        e * REGION + 0 * p], axis=1).astype(np.float32)
    return {
        "where": where,
        "x": f(a["x"].reshape(NT, P, E).transpose(1, 0, 2)),
        "ctx_t": f(a["ctx_1024"].reshape(T, E).T),
        "ctx_r": f(a["ctx_1024"][:, ::-1].reshape(T, E).T),
        "wqkv_p": np.concatenate([a["L0_attn_wq"], a["L0_attn_wk"], a["L0_attn_wv"]], axis=1),
        "b_all": np.concatenate([a["L0_attn_bq"], a["L0_attn_bk"], a["L0_attn_bv"], a["L0_attn_bo"],
                                 a["L0_xattn_bv"], a["L0_xattn_bo"]]),
        "wo": a["L0_attn_wo"], "wq2": a["L0_xattn_Wq"], "wk2": a["L0_xattn_Wk"], "wv2": a["L0_xattn_Wv"],
        "wo2": a["L0_xattn_Wo"], "bq2": a["L0_xattn_bq"].reshape(P, 1), "bk2": a["L0_xattn_bk"].reshape(P, 1),
        "scale": a["L0_ffn_norm_scale"].reshape(P, 1), "w_router": f(a["L0_ffn_w_router"].T),
        "w_up": f(a["L0_ffn_w_up"].transpose(2, 0, 1).reshape(E, NE, 2 * HID)),
        "w_down": f(a["L0_ffn_w_down"].reshape(NE, E, 2, P).transpose(3, 0, 2, 1).reshape(P, NE, 2 * E)),
        "tri": ((s <= t) & (s // L == t // L)).astype(np.float32),
        "stri": (s < t).astype(np.float32),
        "ident": np.eye(P, dtype=np.float32),
        "iota": iota,
    }


def kernel(**inputs):
    import numpy as _np
    import concourse.bacc as _bacc
    from concourse import mybir as _mybir
    from concourse.bass_utils import run_bass_kernel_spmd as _run

    nc = _bacc.Bacc("TRN2", target_bir_lowering=False, num_devices=1)
    arrays = _arrays(**inputs)
    args = [nc.dram_tensor(f"in_{n}", arrays[n].shape, _mybir.dt.from_np(arrays[n].dtype), kind="ExternalInput").ap()
            for n in _NAMES]
    out = nc.dram_tensor("out_x", (P, NT, E), F32, kind="ExternalOutput").ap()
    build(nc, *args, out)
    r = _run(nc, [{f"in_{n}": arrays[n] for n in _NAMES}], core_ids=[0])
    got = r.results[0]["out_x"]
    return _np.ascontiguousarray(got.transpose(1, 0, 2)).reshape(B, L, E)
```
